# Optimizing a Trainium2 kernel written in Bass

```python
import numpy as np
import jax
import jax.numpy as jnp

def _softmax(x, axis=-1):
    return jax.nn.softmax(x, axis=axis)

def _gelu(x):
    return jax.nn.gelu(x, approximate=True)

def _silu(x):
    return jax.nn.silu(x)

def _sigmoid(x):
    return jax.nn.sigmoid(x)

def _layernorm(x, axis=-1, eps=1e-05):
    m = jnp.mean(x, axis=axis, keepdims=True)
    v = jnp.var(x, axis=axis, keepdims=True)
    return (x - m) / jnp.sqrt(v + eps)

def _scatter_add(tgt, idx, src, axis=0):
    return tgt.at[idx].add(src)

def _segment_sum(src, seg, n):
    return jax.ops.segment_sum(src, seg, n)
kernel_name = 'mk_sandwich_d1_jaxref_r4_b9a437'

def setup_inputs(seed: int=0):
    np.random.seed(seed)
    _w = jnp.asarray

    def _L0_attn_setup():
        import jax, jax.numpy as jnp
        from jax import lax
        import numpy as np
        D = 256
        H = 16
        DK = 64
        DV = 128
        KDIM = H * DK
        VDIM = H * DV
        CONV_K = 4
        B, T = (2, 1024)
        EPS = 1e-05

        def _causal_conv_silu(x, w):
            C = x.shape[-1]
            Kw = w.shape[-1]
            xp = jnp.pad(x, ((0, 0), (Kw - 1, 0), (0, 0))).transpose(0, 2, 1)
            y = lax.conv_general_dilated(xp, w[:, None, :], window_strides=(1,), padding='VALID', feature_group_count=C, dimension_numbers=('NCH', 'OIH', 'NCH'))
            return jax.nn.silu(y.transpose(0, 2, 1))

        def _l2norm(x, eps=1e-06):
            return x * lax.rsqrt(jnp.sum(x * x, axis=-1, keepdims=True) + eps)

        def _gated_delta_rule(q, k, v, g, beta):
            scale = q.shape[-1] ** (-0.5)
            qs = jnp.moveaxis(q, 1, 0)
            ks_ = jnp.moveaxis(k, 1, 0)
            vs = jnp.moveaxis(v, 1, 0)
            gs = jnp.moveaxis(g, 1, 0)
            bs = jnp.moveaxis(beta, 1, 0)

            def step(S, inp):
                q_t, k_t, v_t, g_t, b_t = inp
                S = S * jnp.exp(g_t)[..., None, None]
                mem = jnp.einsum('bhk,bhkv->bhv', k_t, S)
                delta = (v_t - mem) * b_t[..., None]
                S = S + jnp.einsum('bhk,bhv->bhkv', k_t, delta)
                o_t = jnp.einsum('bhk,bhkv->bhv', q_t * scale, S)
                return (S, o_t)
            S0 = jnp.zeros((q.shape[0], q.shape[2], q.shape[3], v.shape[3]), q.dtype)
            _, o = lax.scan(step, S0, (qs, ks_, vs, gs, bs))
            return jnp.moveaxis(o, 0, 1)
        key = jax.random.key(seed)
        ks = jax.random.split(key, 14)

        def w(k, shape, s=0.02):
            return jax.random.normal(k, shape, jnp.float32) * s
        return {'x': jax.random.normal(ks[0], (B, T, D), jnp.float32), 'w_q': w(ks[1], (D, KDIM)), 'w_k': w(ks[2], (D, KDIM)), 'w_v': w(ks[3], (D, VDIM)), 'w_a': w(ks[4], (D, H)), 'w_b': w(ks[5], (D, H)), 'w_g': w(ks[6], (D, VDIM)), 'w_out': w(ks[7], (VDIM, D)), 'A_log': jnp.log(jax.random.uniform(ks[8], (H,), jnp.float32, 1.0, 16.0)), 'dt_bias': jax.random.uniform(ks[9], (H,), jnp.float32, -4.0, -1.0), 'conv_q': w(ks[10], (KDIM, CONV_K), 0.1), 'conv_k': w(ks[11], (KDIM, CONV_K), 0.1), 'conv_v': w(ks[12], (VDIM, CONV_K), 0.1), 'norm_w': jnp.ones((DV,), jnp.float32)}
    _L0_attn_in = _L0_attn_setup()

    def _L0_ffn_setup():
        import jax, jax.numpy as jnp
        import numpy as np
        B, S, H, DV = (4, 1024, 256, 256)
        E, INNER, P, K = (8, 32, 8, 2)

        def _ln(v, g, b, eps=1e-05):
            m = jnp.mean(v, axis=-1, keepdims=True)
            var = jnp.var(v, axis=-1, keepdims=True)
            return (v - m) * jax.lax.rsqrt(var + eps) * g + b
        key = jax.random.key(seed)
        ks = jax.random.split(key, 8)
        sc = lambda d: 1.0 / np.sqrt(d)
        return {'x': jax.random.normal(ks[0], (B, S, H), jnp.float32), 'Wv': jax.random.normal(ks[1], (DV, H), jnp.float32) * sc(H), 'bv': jnp.zeros((DV,), jnp.float32), 'Wg': jax.random.normal(ks[2], (E, DV), jnp.float32) * sc(DV), 'bg': jnp.zeros((E,), jnp.float32), 'Wp': jax.random.normal(ks[3], (E, P, DV), jnp.float32) * sc(DV), 'alpha': jnp.zeros((), jnp.float32), 'g_r': jnp.ones((E,), jnp.float32), 'b_r': jnp.zeros((E,), jnp.float32), 'g_c': jnp.ones((E,), jnp.float32), 'b_c': jnp.zeros((E,), jnp.float32), 'W1': jax.random.normal(ks[4], (E, INNER, DV), jnp.float32) * sc(DV), 'b1': jnp.zeros((E, INNER), jnp.float32), 'W2': jax.random.normal(ks[5], (E, DV, INNER), jnp.float32) * sc(INNER), 'b2': jnp.zeros((E, DV), jnp.float32)}
    _L0_ffn_in = _L0_ffn_setup()
    _d = {'L0_attn_x': _L0_attn_in['x'], 'L0_attn_w_q': _L0_attn_in['w_q'], 'L0_attn_w_k': _L0_attn_in['w_k'], 'L0_attn_w_v': _L0_attn_in['w_v'], 'L0_attn_w_a': _L0_attn_in['w_a'], 'L0_attn_w_b': _L0_attn_in['w_b'], 'L0_attn_w_g': _L0_attn_in['w_g'], 'L0_attn_w_out': _L0_attn_in['w_out'], 'L0_attn_A_log': _L0_attn_in['A_log'], 'L0_attn_dt_bias': _L0_attn_in['dt_bias'], 'L0_attn_conv_q': _L0_attn_in['conv_q'], 'L0_attn_conv_k': _L0_attn_in['conv_k'], 'L0_attn_conv_v': _L0_attn_in['conv_v'], 'L0_attn_norm_w': _L0_attn_in['norm_w'], 'L0_ffn_Wv': _L0_ffn_in['Wv'], 'L0_ffn_bv': _L0_ffn_in['bv'], 'L0_ffn_Wg': _L0_ffn_in['Wg'], 'L0_ffn_bg': _L0_ffn_in['bg'], 'L0_ffn_Wp': _L0_ffn_in['Wp'], 'L0_ffn_alpha': _L0_ffn_in['alpha'], 'L0_ffn_g_r': _L0_ffn_in['g_r'], 'L0_ffn_b_r': _L0_ffn_in['b_r'], 'L0_ffn_g_c': _L0_ffn_in['g_c'], 'L0_ffn_b_c': _L0_ffn_in['b_c'], 'L0_ffn_W1': _L0_ffn_in['W1'], 'L0_ffn_b1': _L0_ffn_in['b1'], 'L0_ffn_W2': _L0_ffn_in['W2'], 'L0_ffn_b2': _L0_ffn_in['b2']}
    _x0 = _d['L0_attn_x']
    _d['L0_attn_x'] = jax.random.normal(jax.random.fold_in(jax.random.key(seed), 1), (16, 512, 256), dtype=_x0.dtype)
    del _x0
    return _d

def reference(L0_attn_x, L0_attn_w_q, L0_attn_w_k, L0_attn_w_v, L0_attn_w_a, L0_attn_w_b, L0_attn_w_g, L0_attn_w_out, L0_attn_A_log, L0_attn_dt_bias, L0_attn_conv_q, L0_attn_conv_k, L0_attn_conv_v, L0_attn_norm_w, L0_ffn_Wv, L0_ffn_bv, L0_ffn_Wg, L0_ffn_bg, L0_ffn_Wp, L0_ffn_alpha, L0_ffn_g_r, L0_ffn_b_r, L0_ffn_g_c, L0_ffn_b_c, L0_ffn_W1, L0_ffn_b1, L0_ffn_W2, L0_ffn_b2):

    def _L0_attn_ref(x, w_q, w_k, w_v, w_a, w_b, w_g, w_out, A_log, dt_bias, conv_q, conv_k, conv_v, norm_w):
        import jax, jax.numpy as jnp
        from jax import lax
        import numpy as np
        D = 256
        H = 16
        DK = 64
        DV = 128
        KDIM = H * DK
        VDIM = H * DV
        CONV_K = 4
        B, T = (2, 1024)
        EPS = 1e-05

        def _causal_conv_silu(x, w):
            C = x.shape[-1]
            Kw = w.shape[-1]
            xp = jnp.pad(x, ((0, 0), (Kw - 1, 0), (0, 0))).transpose(0, 2, 1)
            y = lax.conv_general_dilated(xp, w[:, None, :], window_strides=(1,), padding='VALID', feature_group_count=C, dimension_numbers=('NCH', 'OIH', 'NCH'))
            return jax.nn.silu(y.transpose(0, 2, 1))

        def _l2norm(x, eps=1e-06):
            return x * lax.rsqrt(jnp.sum(x * x, axis=-1, keepdims=True) + eps)

        def _gated_delta_rule(q, k, v, g, beta):
            scale = q.shape[-1] ** (-0.5)
            qs = jnp.moveaxis(q, 1, 0)
            ks_ = jnp.moveaxis(k, 1, 0)
            vs = jnp.moveaxis(v, 1, 0)
            gs = jnp.moveaxis(g, 1, 0)
            bs = jnp.moveaxis(beta, 1, 0)

            def step(S, inp):
                q_t, k_t, v_t, g_t, b_t = inp
                S = S * jnp.exp(g_t)[..., None, None]
                mem = jnp.einsum('bhk,bhkv->bhv', k_t, S)
                delta = (v_t - mem) * b_t[..., None]
                S = S + jnp.einsum('bhk,bhv->bhkv', k_t, delta)
                o_t = jnp.einsum('bhk,bhkv->bhv', q_t * scale, S)
                return (S, o_t)
            S0 = jnp.zeros((q.shape[0], q.shape[2], q.shape[3], v.shape[3]), q.dtype)
            _, o = lax.scan(step, S0, (qs, ks_, vs, gs, bs))
            return jnp.moveaxis(o, 0, 1)
        Bx, Tx, _ = x.shape
        q = x @ w_q
        k = x @ w_k
        v = x @ w_v
        beta = jax.nn.sigmoid(x @ w_b) * 2.0
        g = -jnp.exp(A_log) * jax.nn.softplus(x @ w_a + dt_bias)
        q = _causal_conv_silu(q, conv_q)
        k = _causal_conv_silu(k, conv_k)
        v = _causal_conv_silu(v, conv_v)
        q = q.reshape(Bx, Tx, H, DK)
        k = k.reshape(Bx, Tx, H, DK)
        v = v.reshape(Bx, Tx, H, DV)
        q = _l2norm(q)
        k = _l2norm(k)
        o = _gated_delta_rule(q, k, v, g, beta)
        g_gate = (x @ w_g).reshape(Bx, Tx, H, DV)
        rms = o * lax.rsqrt(jnp.mean(o * o, axis=-1, keepdims=True) + EPS)
        y = rms * norm_w * jax.nn.silu(g_gate)
        return y.reshape(Bx, Tx, VDIM) @ w_out

    def _L0_ffn_ref(x, Wv, bv, Wg, bg, Wp, alpha, g_r, b_r, g_c, b_c, W1, b1, W2, b2):
        import jax, jax.numpy as jnp
        import numpy as np
        B, S, H, DV = (4, 1024, 256, 256)
        E, INNER, P, K = (8, 32, 8, 2)

        def _ln(v, g, b, eps=1e-05):
            m = jnp.mean(v, axis=-1, keepdims=True)
            var = jnp.var(v, axis=-1, keepdims=True)
            return (v - m) * jax.lax.rsqrt(var + eps) * g + b
        V = jnp.einsum('bsh,dh->bsd', x, Wv) + bv
        Vf = V.reshape(-1, DV)
        r = Vf @ Wg.T + bg
        pv = jnp.einsum('epd,nd->nep', Wp, Vf)
        c = jnp.sqrt(jnp.sum(pv * pv, axis=-1)) / np.sqrt(P)
        s = _ln(r, g_r, b_r) + jax.nn.sigmoid(alpha) * _ln(c, g_c, b_c)
        topv, sel = jax.lax.top_k(s, K)
        w = jax.nn.softmax(topv, axis=-1)
        delta = jnp.zeros_like(Vf)
        for e in range(E):
            h = jax.nn.silu(Vf @ W1[e].T + b1[e])
            out = h @ W2[e].T + b2[e]
            we = jnp.sum(jnp.where(sel == e, w, 0.0), axis=-1)
            delta = delta + out * we[:, None]
        return (Vf + delta).reshape(V.shape)
    x = L0_attn_x
    x = x + _layernorm(_L0_attn_ref(_layernorm(x, axis=-1), L0_attn_w_q, L0_attn_w_k, L0_attn_w_v, L0_attn_w_a, L0_attn_w_b, L0_attn_w_g, L0_attn_w_out, L0_attn_A_log, L0_attn_dt_bias, L0_attn_conv_q, L0_attn_conv_k, L0_attn_conv_v, L0_attn_norm_w), axis=-1)
    x = x + _layernorm(_L0_ffn_ref(_layernorm(x, axis=-1), L0_ffn_Wv, L0_ffn_bv, L0_ffn_Wg, L0_ffn_bg, L0_ffn_Wp, L0_ffn_alpha, L0_ffn_g_r, L0_ffn_b_r, L0_ffn_g_c, L0_ffn_b_c, L0_ffn_W1, L0_ffn_b1, L0_ffn_W2, L0_ffn_b2), axis=-1)
    return x

_drawn_inputs = setup_inputs


def setup_inputs(seed=0):
    import zlib

    import numpy as np

    out = dict(_drawn_inputs(seed))
    spreads = {'L0_attn_norm_w': (1.0, 0.2),
     'L0_ffn_bv': (0.0, 0.1),
     'L0_ffn_bg': (0.0, 0.1),
     'L0_ffn_g_r': (1.0, 0.2),
     'L0_ffn_b_r': (0.0, 0.1),
     'L0_ffn_g_c': (1.0, 0.2),
     'L0_ffn_b_c': (0.0, 0.1),
     'L0_ffn_b1': (0.0, 0.322),
     'L0_ffn_b2': (0.0, 0.1)}
    factors = {}
    for name, (base, spread) in spreads.items():
        noise = np.random.default_rng([zlib.crc32(name.encode()), seed]).standard_normal(out[name].shape)
        drawn = base * np.exp(spread * noise) if base else spread * noise
        out[name] = jnp.asarray(drawn.astype(out[name].dtype))
    for name, factor in factors.items():
        out[name] = (out[name] * factor).astype(out[name].dtype)
    return out
```

```python
from contextlib import ExitStack

import concourse.bass as bass
from concourse import mybir

ALU = mybir.AluOpType
ACT = mybir.ActivationFunctionType
AX = mybir.AxisListType
F32 = mybir.dt.float32
F16 = mybir.dt.float16
U32 = mybir.dt.uint32

P = 128
D = 256
KT = D // P
NB, T = 16, 512
H, DK, DV = 16, 64, 128
NP = H // 2
NIT = NP * NB
CH = T // P
NU = 2 * CH
TAPS = 4
PAD = TAPS - 1
NLEV = 6
NTILE = NB * CH
E, INNER, PP = 8, 32, 8
COMPUTE = (mybir.EngineType.PE, mybir.EngineType.Activation, mybir.EngineType.DVE, mybir.EngineType.Pool)
EVERY = COMPUTE + (mybir.EngineType.SP,)
NEG = -1.0e4
LN_EPS = 1e-5
N_QKV = 2 * P + 2 * P


class Phase(ExitStack):

    def __init__(self, nc):
        super().__init__()
        self.nc, self.sems = nc, []

    def semaphore(self, name):
        self.sems.append(self.nc.alloc_semaphore(name=name))
        return self.sems[-1]

    def finish(self):
        self.nc.all_engine_barrier()
        self.nc.clear_and_free_semaphores(self.sems)
        self.nc.all_engine_barrier()


class Steps:

    def __init__(self, nc, ctx):
        self.nc, self.ctx, self.at, self.last = nc, ctx, {}, {}

    def series(self, name, steps):
        sem = self.ctx.semaphore(name)
        self.last[name] = len(steps) - 1
        for k, step in enumerate(steps):
            self.at[step] = (sem, name, k, len(steps))

    def find(self, name):
        if name not in self.at:
            self.series(name, [name])
        return self.at[name]

    def sem(self, name):
        return self.find(name)[0]

    def done(self, instruction, name):
        sem, series, k, n = self.find(name)
        assert k == (self.last[series] + 1) % n, (name, self.last[series])
        self.last[series] = k
        instruction.then_inc(sem, 1)

    def loaded(self, dma, name):
        dma.then_inc(self.sem(name), 16)

    def need(self, eng, i, *names):
        if isinstance(i, int) and i < 0:
            return
        latest = {}
        for name in names:
            sem, series, k, n = self.find(name)
            if series not in latest or latest[series][1] < k:
                latest[series] = (sem, k, n)
        for sem, k, n in latest.values():
            eng.wait_ge(sem, i * n + (k + 1))

    def need_dma(self, eng, i, name):
        if isinstance(i, int) and i < 0:
            return
        eng.wait_ge(self.sem(name), (i + 1) * 16)

    def need_dma_of(self, eng, i, name, par):
        if isinstance(i, int) and i < 0:
            return
        eng.wait_ge(self.sem(f"{name}{par}"), (i // 2 + 1) * 16)


class Chain:

    def __init__(self, nc, ctx, name, per):
        self.sem, self.per, self.k = ctx.semaphore(name), per, 0

    def start(self, i):
        self.i, self.k = i, 0

    def inc(self, instruction):
        instruction.then_inc(self.sem, 1)
        self.k += 1
        return self.i * self.per + self.k

    def end(self):
        assert self.k == self.per, (self.k, self.per)

    def last_of(self, i):
        return (i + 1) * self.per


def in_slots(nc, n, lag, first, engines, body):
    for t in range(first):
        body(t, t % 2)
    end = first + (n - first) // 2 * 2
    with nc.Fori(first, end, 2, engines=engines) as t:
        body(t, first % 2)
        body(t + 1, (first + 1) % 2)
    for t in range(end, n + lag):
        body(t, t % 2)


def active(i, n):
    return not isinstance(i, int) or 0 <= i < n


def merged(*stages):
    keyed = []
    for order, steps in enumerate(stages):
        for k, step in enumerate(steps):
            keyed.append(((k + 0.5) / len(steps), order, k, step))
    return [step for _, _, _, step in sorted(keyed, key=lambda x: x[:3])]


def settle(eng, scratch):
    eng.tensor_tensor(scratch[0:1, 0:1], scratch[0:1, 1:2], scratch[0:1, 1:2], ALU.add)


def make_constants(nc, ctx, sb):
    pool = nc.gpsimd
    s_const = ctx.enter_context(nc.semaphore("const_built"))
    n = [0]

    def step(ins):
        ins.then_inc(s_const, 1)
        n[0] += 1
        pool.wait_ge(s_const, n[0])

    c = {}
    c["ident"] = sb("ident", [P, P], F32)
    step(pool.memset(c["ident"][:], 1.0))
    step(pool.affine_select(out=c["ident"][:], in_=c["ident"][:], pattern=[[-1, P]], compare_op=ALU.is_equal,
                            fill=0.0, base=0, channel_multiplier=1))
    c["ident16"] = sb("ident16", [P, P], F16)
    step(pool.tensor_copy(c["ident16"][:], c["ident"][:]))
    c["upper"] = sb("upper", [P, P], F32)
    step(pool.memset(c["upper"][:], 1.0))
    step(pool.affine_select(out=c["upper"][:], in_=c["upper"][:], pattern=[[1, P]], compare_op=ALU.is_ge,
                            fill=0.0, base=0, channel_multiplier=-1))
    c["ones_col"] = sb("ones_col", [P, 1], F32)
    step(pool.memset(c["ones_col"][:], 1.0))
    c["head_sel"] = sb("head_sel", [P, 2], F32)
    step(pool.memset(c["head_sel"][:], 0.0))
    step(pool.memset(c["head_sel"][0:DK, 0:1], 1.0))
    step(pool.memset(c["head_sel"][DK:P, 1:2], 1.0))
    for name in ("settle_dve", "settle_pool"):
        c[name] = sb(name, [P, 2], F32)
        step(pool.memset(c[name][:], 0.0))
    for name, value in (("half", 0.5), ("minus_half", -0.5)):
        c[name] = sb(name, [P, 16], F32)
        step(pool.memset(c[name][:], value))

    def block_mask(view_of, size, value):
        nblk = P // (2 * size)
        v = view_of.rearrange("p (b t r) -> p b t r", t=2, r=size)[:, :, 1, :]
        step(pool.memset(v, value))
        step(pool.affine_select(out=v, in_=v, pattern=[[-2 * size, nblk], [0, size]], compare_op=ALU.is_ge,
                                fill=0.0, base=0, channel_multiplier=1))
        step(pool.affine_select(out=v, in_=v, pattern=[[2 * size, nblk], [0, size]], compare_op=ALU.is_ge,
                                fill=0.0, base=size - 1, channel_multiplier=-1))

    c["mask"] = sb("mask", [P, NLEV, P], F16)
    step(pool.memset(c["mask"][:], 0.0))
    for lev in range(NLEV):
        block_mask(c["mask"][:, lev, :], 2 << lev, 1.0)
    c["first"] = sb("first", [P, P], F16)
    step(pool.memset(c["first"][:], 0.0))
    block_mask(c["first"][:], 1, -1.0)
    step(pool.tensor_tensor(c["first"][:], c["first"][:], c["ident16"][:], ALU.add))
    return c, s_const, n[0]


def phase_norm(nc, c, x, w_ab, xT_dram, gate_tok):
    with Phase(nc) as ctx:
        sb = lambda name, shape, dt=F32: ctx.enter_context(nc.sbuf_tensor(name, shape, dt))
        x_in = [sb(f"n_x{p}", [P, CH, D]) for p in range(2)]
        xn = [sb(f"n_xn{p}", [P, CH, D]) for p in range(2)]
        xT = [sb(f"n_xT{p}", [P, KT, T]) for p in range(2)]
        stats = sb("n_stats", [P, CH, 6])
        mv = sb("n_mv", [P, CH, 2])
        rstd = sb("n_rstd", [P, CH])
        wab = sb("n_wab", [P, KT, 2 * H])
        turn_ps = [ctx.enter_context(nc.psum_tensor(f"n_turn{k}", [P, T], F32)) for k in range(KT)]
        ab_ps = ctx.enter_context(nc.psum_tensor("n_ab", [P, CH, P], F32))
        s = Steps(nc, ctx)
        dve = Chain(nc, ctx, "n_dve", 3 * CH)

        nc.sync.dma_start(wab[:], w_ab).then_inc(s.sem("n_wab_in"), 16)

        def body(t, par):
            i, j = t, t - 1
            if active(i, NB):
                s.need(nc.sync, i - 2, "n_xn")
                s.loaded(nc.sync.dma_start(x_in[par][:], x[bass.ds(i, 1)].rearrange("a p c d -> p (a c) d")), f"n_x_in{par}")
                s.need_dma_of(nc.vector, i, "n_x_in", par)
                dve.start(i)
                for k in range(CH):
                    v = dve.inc(nc.vector.bn_stats(stats[:, k, :], x_in[par][:, k, :]))
                nc.vector.wait_ge(dve.sem, v)
                settle(nc.vector, c["settle_dve"])
                for k in range(CH):
                    v = dve.inc(nc.vector.bn_aggr(mv[:, k, :], stats[:, k, :]))
                nc.vector.wait_ge(dve.sem, v)
                s.need(nc.vector, i - 1, "n_rstd")
                v = dve.inc(nc.vector.tensor_scalar(rstd[:], mv[:, :, 1], LN_EPS, None, ALU.add))
                nc.gpsimd.wait_ge(dve.sem, v)
                s.done(nc.gpsimd.tensor_tensor(rstd[:], rstd[:], c["minus_half"][:, 0:CH], ALU.pow), "n_rstd")
                s.need(nc.vector, i, "n_rstd")
                s.need(nc.vector, i - 2, "n_turn")
                for k in range(CH):
                    ins = nc.vector.tensor_scalar(xn[par][:, k, :], x_in[par][:, k, :], mv[:, k, 0:1],
                                                  rstd[:, k:k + 1], ALU.subtract, ALU.mult)
                    if k < CH - 1:
                        dve.inc(ins)
                s.done(ins, "n_xn")
            if active(j, NB):
                q = 1 - par
                s.need(nc.tensor, j, "n_xn")
                s.need(nc.tensor, j - 1, "n_xT")
                for k in range(KT):
                    for m in range(CH):
                        ins = nc.tensor.transpose(turn_ps[k][:, m * P:(m + 1) * P], xn[q][:, m, k * P:(k + 1) * P],
                                                  c["ident"][:])
                s.done(ins, "n_turn")
                s.need_dma_of(nc.scalar, j - 2, "n_xT_out", q)
                s.need(nc.scalar, j - 2, "n_ab")
                s.need(nc.scalar, j, "n_turn")
                for k in range(KT):
                    ins = nc.scalar.copy(xT[q][:, k, :], turn_ps[k][:])
                s.done(ins, "n_xT")
                s.need(nc.sync, j, "n_xT")
                s.loaded(nc.sync.dma_start(xT_dram[bass.ds(j, 1)].rearrange("a p k t -> p (a k) t"), xT[q][:]),
                         f"n_xT_out{q}")
                s.need(nc.tensor, j, "n_xT")
                if isinstance(j, int) and j == 0:
                    nc.tensor.wait_ge(s.sem("n_wab_in"), 16)
                s.need(nc.tensor, j - 1, "n_ab_out")
                for m in range(CH):
                    for k in range(KT):
                        ins = nc.tensor.matmul(ab_ps[:, m, 0:2 * H], xT[q][:, k, m * P:(m + 1) * P], wab[:, k, :],
                                               start=k == 0, stop=k == KT - 1)
                s.done(ins, "n_ab")
                s.need(nc.vector, j, "n_ab")
                dve2_in = ab_ps[:, :, 0:2 * H].rearrange("p c (n q h) -> p n c q h", n=2, h=2)
                for n in range(2):
                    for m in range(CH):
                        dst = gate_tok[n][:].rearrange("p (q x) -> p q x", q=NP)[:, :, bass.ds(j * NU + 2 * m, 2)]
                        ins = nc.vector.tensor_copy(dst, dve2_in[:, n, m])
                s.done(ins, "n_ab_out")

        in_slots(nc, NB, 1, 3, EVERY, body)
        for p in range(2):
            nc.sync.wait_ge(s.sem(f"n_xT_out{p}"), 16 * NB // 2)
        ctx.finish()


def phase_gates(nc, c, a_log, dt_bias, gate_tok, g_dram):
    with Phase(nc) as ctx:
        sb = lambda name, shape, dt=F32: ctx.enter_context(nc.sbuf_tensor(name, shape, dt))
        W = NIT * NU
        alog = sb("g_alog", [P, H])
        nega = sb("g_nega", [P, H])
        dtb = sb("g_dtb", [P, H])
        z, az, rows = sb("g_z", [P, W]), sb("g_az", [P, W]), sb("g_rows", [P, W // P, P])
        ps = [ctx.enter_context(nc.psum_tensor(f"g_ps{k}", [P, 512], F32)) for k in range(2)]
        s_in = ctx.semaphore("g_in")
        s_v = ctx.semaphore("g_dve")
        s_a = ctx.semaphore("g_act")
        s_p = ctx.semaphore("g_pe")
        s_out = ctx.semaphore("g_out")
        by_head = lambda t: t[:].rearrange("p (q x h) -> p q x h", q=NP, h=2)
        spread = lambda t: t[:].rearrange("p (q x h) -> p q x h", x=1, h=2).broadcast_to([P, NP, W // H, 2])

        nc.sync.dma_start(alog[:], a_log.partition_broadcast(P)).then_inc(s_in, 16)
        nc.sync.dma_start(dtb[:], dt_bias.partition_broadcast(P)).then_inc(s_in, 16)
        nc.vector.wait_ge(s_in, 32)
        nc.scalar.wait_ge(s_in, 32)
        nc.vector.tensor_tensor(by_head(z), by_head(gate_tok[0]), spread(dtb), ALU.add).then_inc(s_v, 1)
        nc.scalar.wait_ge(s_v, 1)
        nc.scalar.activation(az[:], z[:], ACT.Abs).then_inc(s_a, 1)
        nc.scalar.wait_ge(s_a, 1)
        nc.scalar.activation(az[:], az[:], ACT.Exp, scale=-1.0).then_inc(s_a, 1)
        nc.scalar.activation(nega[:], alog[:], ACT.Exp).then_inc(s_a, 1)
        nc.scalar.wait_ge(s_a, 2)
        nc.scalar.activation(az[:], az[:], ACT.Ln, bias=1.0).then_inc(s_a, 1)
        nc.vector.wait_ge(s_v, 1)
        nc.vector.wait_ge(s_a, 4)
        nc.vector.scalar_tensor_tensor(z[:], z[:], 0.0, az[:], ALU.max, ALU.add).then_inc(s_v, 1)
        nc.vector.tensor_scalar(nega[:], nega[:], -1.0, None, ALU.mult).then_inc(s_v, 1)
        nc.vector.wait_ge(s_v, 3)
        nc.vector.tensor_tensor(by_head(z), by_head(z), spread(nega), ALU.mult).then_inc(s_v, 1)
        nc.scalar.activation(gate_tok[1][:], gate_tok[1][:], ACT.Tanh, scale=0.5).then_inc(s_a, 1)
        nc.vector.wait_ge(s_a, 5)
        nc.vector.tensor_scalar(gate_tok[1][:], gate_tok[1][:], 1.0, None, ALU.add).then_inc(s_v, 1)
        nc.tensor.wait_ge(s_v, 4)
        for k in range(2):
            nc.tensor.matmul(ps[k][:], c["upper"][:], z[:, k * 512:(k + 1) * 512], start=True,
                             stop=True).then_inc(s_p, 1)
        for k in range(2):
            nc.vector.wait_ge(s_p, k + 1)
            nc.vector.tensor_copy(gate_tok[0][:, k * 512:(k + 1) * 512], ps[k][:]).then_inc(s_v, 1)
        for k in range(2):
            nc.tensor.wait_ge(s_v, 6 + k)
            for m in range(4):
                col = k * 512 + m * P
                ins = nc.tensor.transpose(ps[k][:, m * P:(m + 1) * P], gate_tok[0][:, col:col + P], c["ident"][:])
            ins.then_inc(s_p, 1)
        for k in range(2):
            nc.scalar.wait_ge(s_p, 3 + k)
            nc.scalar.copy(rows[:, 4 * k:4 * k + 4, :], ps[k][:].rearrange("p (a b) -> p a b", a=4)).then_inc(s_a, 1)
        nc.sync.wait_ge(s_a, 7)
        nc.sync.dma_start(g_dram[0:NIT * NU].rearrange("(a r) t -> r a t", r=P), rows[:]).then_inc(s_out, 16)
        nc.sync.wait_ge(s_out, 16)
        ctx.finish()


def phase_delta(nc, c, w_qkv, w_gate, w_out, taps, norm_w, xT_dram, g_dram, gate_tok, acc):
    with Phase(nc) as ctx:
        sb = lambda name, shape, dt=F32: ctx.enter_context(nc.sbuf_tensor(name, shape, dt))
        two = lambda name, shape, dt=F32: [sb(f"{name}{p}", shape, dt) for p in range(2)]
        bank = lambda name: ctx.enter_context(nc.psum_tensor(name, [P, 512], F32))
        pe, act, dve, pool, sp = nc.tensor, nc.scalar, nc.vector, nc.gpsimd, nc.sync
        s = Steps(nc, ctx)

        wq = sb("wqkv", [P, KT * N_QKV + 4 * TAPS])
        wqkv = wq[:, 0:KT * N_QKV].rearrange("p (k n) -> p k n", k=KT)
        tap = wq[:, KT * N_QKV:].rearrange("p (j r) -> p j r", r=TAPS)
        wg = sb("wgate", [P, KT, 2 * P])
        wo = sb("wout", [P, 2, D])
        normw = sb("normw", [P, 1])
        xin = two("xin", [P, KT, T])
        kq = two("kq", [P, 2, T])
        vch = two("vch", [P, 2, T])
        pad = two("pad", [P, PAD + T])
        cv = two("cv", [P, T])
        th = sb("th", [P, T])
        grow = sb("grow", [P, NU, P])
        g_it = sb("g_it", [P, NU])
        dec = sb("dec", [P, NU, P])
        dend = sb("dend", [P, NU])
        gam = sb("gam", [P, T])
        sq = sb("sq", [P, 2, T])
        ss, rc, root = sb("ss", [P, 16]), sb("rc", [P, 16]), sb("root", [P, 16])
        bt = sb("bt", [P, NU, P])
        bm = sb("bm", [P, NLEV, NU, P], F16)
        tt = sb("tt", [P, NU, 2, P], F16)
        m1 = sb("m1", [P, NU, P], F16)
        t32 = sb("t32", [P, 4, P])
        r16 = sb("r16", [P, 4, P], F16)
        kqs = two("kqs", [P, 2, T])
        ktok = two("ktok", [P, NU, DK])
        vtok = two("vtok", [P, NU, DV])
        w1 = two("w1", [P, NU])
        s2 = two("s2", [P, NU])
        s2sq = two("s2sq", [P, NU])
        gend = two("gend", [P, CH])
        sg = two("sg", [P, 2, T])
        at = two("at", [P, NU, P])
        tinv = two("tinv", [P, NU, P])
        state = sb("state", [P, 2, DV])
        rr = sb("rr", [P, 2, DV])
        uu = sb("uu", [P, 2, DV])
        yy = sb("yy", [P, 2, P])
        sqo = sb("sqo", [P, 2, P])
        msq, rms = sb("msq", [P, 2]), sb("rms", [P, 2])

        ps_a, ps_b = bank("ps_a"), bank("ps_b")
        b0, b1, b2 = bank("b0"), bank("b1"), bank("b2")
        ck, cz, co = bank("ck"), bank("cz"), bank("co")
        halves = (b1, b2)

        def free(eng, users, name, i):
            k = users.index(name)
            if k:
                s.need(eng, i, users[k - 1])
            else:
                s.need(eng, i - 1, users[-1])

        A_USERS = [f"a_evac{j}" for j in range(4)]
        PB_USERS = ["b_ss", "b_sg0", "b_sg1", "b_ktok", "b_vtok0", "b_vtok1"]
        B0_USERS = [f"b_T2e{g}" for g in range(2)]
        for l in range(NLEV):
            B0_USERS += [f"b_Me{l}{g}" for g in range(2)]
        B0_USERS += [f"b_R{g}" for g in range(2)]
        BH_USERS = [[f"b_ev{g}{k}" for g in range(2)] + [f"b_Ue{l}{g}{k}" for l in range(NLEV) for g in range(2)]
                    + [f"b_T{k}"] for k in range(2)]
        CK_USERS = [n for k in range(CH) for n in ([f"c_R{k}"] if k else []) + ([f"c_S{k}"] if k < CH - 1 else [])
                    + [f"c_m{k}"]]
        CZ_USERS = [n for k in range(CH) for n in (f"c_u{k}", f"c_acc{k}")]
        CO_USERS = [f"c_y{k}" for k in range(CH)]
        levels = [(l, g) for l in range(NLEV) for g in range(2)]
        for name in ("a_proj", "a_pad", "a_evac", "a_tanh", "a_silu"):
            s.series(name, [f"{name}{j}" for j in range(4)])
        s.series("a_tap", [f"a_tap{j}{r}" for j in range(4) for r in range(PAD)])
        s.series("b_M", [f"b_M{l}{g}" for l, g in levels])
        s.series("b_Me", [f"b_Me{l}{g}" for l, g in levels])
        s.series("b_bm", [f"b_bm0{g}" for g in range(2)] + [f"b_bm{l}{g}" for l, g in levels if l])
        s.series("b_U", [f"b_U{l}{g}{k}" for l, g in levels for k in range(2)])
        s.series("b_Ue", [f"b_Ue{l}{g}{k}" for l, g in levels for k in range(2)])
        for name in ("b_vT", "b_vtok", "b_g", "b_tg", "b_sg", "b_diag", "b_t2", "b_T2p", "b_T2e", "b_t32", "b_P",
                     "b_R", "b_F", "b_T"):
            s.series(name, [f"{name}{g}" for g in range(2)])
        for name in ("b_kk", "b_ev"):
            s.series(name, [f"{name}{g}{k}" for g in range(2) for k in range(2)])
        for name in ("c_KS", "c_R"):
            s.series(name, [f"{name}{m}" for m in range(1, CH)])
        for name in ("c_SU", "c_S"):
            s.series(name, [f"{name}{m}" for m in range(CH - 1)])
        for name in ("c_Z", "c_u", "c_O", "c_sq", "c_y", "c_ss", "c_out", "c_m", "c_me", "c_p", "c_r", "c_acch",
                     "c_acc"):
            s.series(name, [f"{name}{m}" for m in range(CH)])

        sp.dma_start(normw[:], norm_w).then_inc(s.sem("normw_in"), 16)

        def load_x(i, b, par):
            s.need(sp, i - 2, "b_g1")
            s.loaded(sp.dma_start(xin[par][:], xT_dram[bass.ds(b, 1)].rearrange("a p k t -> p (a k) t")),
                     f"xin_in{par}")

        def load_rows(i):
            s.need(sp, i - 1, "b_d", "b_dc", "b_gam")
            s.loaded(sp.dma_start(grow[:], g_dram[bass.ds(i * NU, NU), :].partition_broadcast(P)), "grow_in")

        def load_pair(hp):
            i = hp * NB
            s.need(sp, i - 1, "a_proj3", "a_tap32", "a_evac3")
            s.loaded(sp.dma_start(wq[:], w_qkv[bass.ds(hp, 1)].rearrange("a p n -> p (a n)")), "wqkv_in")
            load_x(i, 0, 0)
            s.need(sp, i - 1, "b_g1")
            s.loaded(sp.dma_start(wg[:], w_gate[bass.ds(hp, 1)].rearrange("a p k n -> p (a k) n")), "wg_in")
            load_rows(i)
            load_x(i + 1, 1, 1)
            load_rows(i + 1)
            s.need(sp, i - 1, f"c_out{CH - 1}")
            s.loaded(sp.dma_start(wo[:], w_out[bass.ds(hp, 1)].rearrange("a p h d -> p (a h) d")), "wo_in")
            with sp.Fori(2, NB, 2) as b:
                for par in range(2):
                    load_x(i + b + par, b + par, par)
                    load_rows(i + b + par)

        def stage_a(i, p):
            steps = []
            dest = [kq[p][:, 1, :], kq[p][:, 0, :], vch[p][:, 0, :], vch[p][:, 1, :]]
            hp = i // NB

            def project(j):
                if j == 0:
                    s.need_dma_of(pe, i, "xin_in", p)
                    s.need_dma(pe, hp, "wqkv_in")
                free(pe, A_USERS, f"a_evac{j}", i)
                for k in range(KT):
                    ins = pe.matmul(ps_a[:], wqkv[:, k, j * P:(j + 1) * P], xin[p][:, k, :], start=k == 0,
                                    stop=k == KT - 1)
                s.done(ins, f"a_proj{j}")
                if j == 0:
                    s.need_dma(act, hp, "wqkv_in")
                s.need(act, i if j > 1 else i - 1, f"a_silu{(j - 2) % 4}")
                s.need(act, i, f"a_proj{j}")
                s.done(act.copy(pad[j % 2][:, PAD:], ps_a[:]), f"a_pad{j}")
                s.done(act.activation(cv[j % 2][:], ps_a[:], ACT.Copy, scale=tap[:, j, TAPS - 1:TAPS]), f"a_evac{j}")

            def convolve(j, r):
                if r == 0:
                    if j == 0:
                        s.need_dma(dve, hp, "wqkv_in")
                    s.need(dve, i, f"a_pad{j}", f"a_evac{j}")
                else:
                    s.need(dve, i, f"a_tap{j}{r - 1}")
                s.done(dve.scalar_tensor_tensor(cv[j % 2][:], pad[j % 2][:, r:r + T], tap[:, j, r:r + 1], cv[j % 2][:],
                                                ALU.mult, ALU.add), f"a_tap{j}{r}")
                if r == PAD - 1:
                    s.need(act, i, f"a_tap{j}{r}")
                    s.need(act, i if j else i - 1, f"a_silu{(j - 1) % 4}")
                    s.done(act.activation(th[:], cv[j % 2][:], ACT.Tanh, scale=0.5), f"a_tanh{j}")

            def silu(j):
                s.need(dve, i, f"a_tanh{j}")
                if j < 2:
                    s.need(dve, i - 2, "b_sq", "b_kqs", "b_kk11", "b_kT")
                else:
                    s.need(dve, i - 2, f"b_vT{j - 2}")
                s.done(dve.scalar_tensor_tensor(dest[j], th[:], 1.0, cv[j % 2][:], ALU.add, ALU.mult),
                       f"a_silu{j}")

            for j in range(4):
                steps.append(lambda j=j: project(j))
                if j:
                    steps.append(lambda j=j: silu(j - 1))
                for r in range(PAD):
                    steps.append(lambda j=j, r=r: convolve(j, r))
            steps.append(lambda: silu(3))
            return steps

        def stage_b(i, p):
            tok = lambda k: gate_tok[k][:, bass.ds(i * NU, NU)]
            col = lambda t, u: t[:, u:u + 1]

            def squares():
                s.need(act, i, "a_silu0", "a_silu1")
                s.need(act, i - 1, "b_stat")
                s.done(act.activation(sq[:], kq[p][:], ACT.Square), "b_sq")

            def decays():
                s.done(dve.tensor_copy(g_it[:], tok(0)), "b_git")
                s.need(dve, i, "b_git")
                s.need_dma(dve, i, "grow_in")
                s.done(dve.tensor_tensor(dec[:], grow[:], g_it[:].unsqueeze(2).broadcast_to([P, NU, P]), ALU.subtract),
                       "b_d")
                s.done(dve.tensor_tensor(dend[:], grow[:, :, P - 1], g_it[:], ALU.subtract), "b_dc")
                s.need(pool, i, "b_d")
                settle(pool, c["settle_pool"])
                s.done(pool.affine_select(out=dec[:], in_=dec[:], pattern=[[0, NU], [1, P]], compare_op=ALU.is_ge,
                                          fill=NEG, base=0, channel_multiplier=-1), "b_sel")

            def exponentials():
                s.need_dma(act, i, "grow_in")
                s.need(act, i - 1, "b_kqs", "b_gend")
                for h in range(2):
                    rows = slice(h * DK, (h + 1) * DK)
                    src = grow[rows].rearrange("p (c h) t -> p c h t", h=2)[:, :, h, :]
                    ins = act.activation(gam[rows, :].rearrange("p (c t) -> p c t", t=P), src, ACT.Exp)
                s.done(ins, "b_gam")
                s.need(act, i, "b_dc")
                s.done(act.activation(dend[:], dend[:], ACT.Exp), "b_ed")
                s.need(act, i, "b_sel")
                s.done(act.activation(dec[:], dec[:], ACT.Exp), "b_E")
                s.need(dve, i, "b_gam")
                s.done(dve.tensor_copy(gend[p][:], gam[:].rearrange("p (c t) -> p c t", t=P)[:, :, P - 1]), "b_gend")

            def stats():
                s.need(pe, i, "b_sq")
                free(pe, PB_USERS, "b_ss", i)
                for n in range(2):
                    for m in range(CH):
                        o = n * NU + 2 * m
                        ins = pe.matmul(ps_b[:, o:o + 2], sq[:, n, m * P:(m + 1) * P], c["head_sel"][:], start=True,
                                        stop=True)
                s.done(ins, "b_stat")
                s.need(dve, i, "b_stat")
                s.need(dve, i - 1, "b_root")
                s.done(dve.tensor_scalar(ss[:], ps_b[:, 0:16], 4e-6, None, ALU.add), "b_ss")
                s.need(pool, i, "b_ss")
                s.need(pool, i - 1, "b_s2", "b_vtok0", "b_vtok1")
                s.done(pool.tensor_tensor(root[:], ss[:], c["half"][:, 0:16], ALU.pow), "b_root")
                s.need(dve, i, "b_ss")
                s.done(dve.reciprocal(rc[:], ss[:]), "b_rc")

            def scales():
                s.need(dve, i, "b_rc", "b_root")
                s.need(dve, i - 2, f"c_u{CH - 1}", f"c_r{CH - 1}")
                s.done(dve.tensor_tensor(w1[p][:], rc[:, 0:NU], tok(1), ALU.mult), "b_w1")
                s.done(dve.tensor_scalar(s2sq[p][:], rc[:, NU:], 1.0 / (256 * DV), None, ALU.mult), "b_s2sq")
                s.done(dve.scalar_tensor_tensor(s2[p][:], rc[:, NU:], 1.0 / 16, root[:, NU:], ALU.mult, ALU.mult),
                       "b_s2")

            def decayed_kq():
                s.need(pool, i, "b_gam", "a_silu0", "a_silu1")
                s.need(pool, i - 2, f"c_O{CH - 1}")
                s.done(pool.tensor_tensor(kqs[p][:], kq[p][:], gam[:].unsqueeze(1).broadcast_to([P, 2, T]), ALU.mult),
                       "b_kqs")

            def gate(h):
                free(pe, PB_USERS, f"b_sg{h}", i)
                if h == 0:
                    s.need_dma(pe, i // NB, "wg_in")
                for k in range(KT):
                    ins = pe.matmul(ps_b[:], wg[:, k, h * P:(h + 1) * P], xin[p][:, k, :], start=k == 0,
                                    stop=k == KT - 1)
                s.done(ins, f"b_g{h}")
                s.need(act, i, f"b_g{h}")
                s.need(act, i - 2, f"c_y{CH - 1}")
                s.done(act.activation(sg[p][:, h, :], ps_b[:], ACT.Tanh, scale=0.5), f"b_tg{h}")
                s.need(dve, i, f"b_tg{h}")
                s.done(dve.scalar_tensor_tensor(sg[p][:, h, :], sg[p][:, h, :], 1.0, ps_b[:], ALU.add, ALU.mult),
                       f"b_sg{h}")

            def turn_k():
                s.need(pe, i, "a_silu1")
                free(pe, PB_USERS, "b_ktok", i)
                for m in range(CH):
                    ins = pe.transpose(ps_b[:, m * P:(m + 1) * P], kq[p][:, 0, m * P:(m + 1) * P], c["ident"][:])
                s.done(ins, "b_kT")
                s.need(dve, i, "b_kT", "b_ed")
                s.need(dve, i - 2, f"c_SU{CH - 2}")
                s.done(dve.tensor_tensor(ktok[p][:], ps_b[:].rearrange("p (u e) -> p u e", e=DK),
                                         dend[:].unsqueeze(2).broadcast_to([P, NU, DK]), ALU.mult), "b_ktok")

            def turn_v(h):
                s.need(pe, i, f"a_silu{2 + h}")
                free(pe, PB_USERS, f"b_vtok{h}", i)
                for m in range(CH):
                    ins = pe.transpose(ps_b[:, m * P:(m + 1) * P], vch[p][:, h, m * P:(m + 1) * P], c["ident"][:])
                s.done(ins, f"b_vT{h}")
                s.need(dve, i, f"b_vT{h}", "b_root")
                s.need(dve, i - 2, f"c_Z{CH - 1}")
                scale = root[:, 0:NU].rearrange("p (c h) -> p c h", h=2)[:, :, h:h + 1].broadcast_to([P, CH, DV])
                s.done(dve.tensor_tensor(vtok[p][:].rearrange("p (c h) e -> p c h e", h=2)[:, :, h, :],
                                         ps_b[:].rearrange("p (c e) -> p c e", e=DV), scale, ALU.mult), f"b_vtok{h}")

            def products(g, k):
                users, ps, rows = BH_USERS[k], halves[k], slice(k * DK, (k + 1) * DK)
                s.need(pe, i, "a_silu0", "a_silu1")
                free(pe, users, f"b_ev{g}{k}", i)
                for n in range(2):
                    t = slice((2 * g + n) * P, (2 * g + n + 1) * P)
                    ins = pe.matmul(ps[:, n * 2 * P:(n + 1) * 2 * P], kq[p][rows, 0, t], kq[p][rows, :, t],
                                    start=True, stop=True)
                s.done(ins, f"b_kk{g}{k}")
                s.need(dve, i, f"b_kk{g}{k}", "b_E", "b_w1")
                s.need(dve, i - 1, f"b_P{g}", f"b_bm{NLEV - 1}{g}")
                for n in range(2):
                    u = 4 * g + 2 * n + k
                    dve.scalar_tensor_tensor(bt[:, u, :], ps[:, n * 2 * P:n * 2 * P + P], col(w1[p], u), dec[:, u, :],
                                             ALU.mult, ALU.mult)
                of_head = lambda t: t[:, 4 * g:4 * g + 4, :].rearrange("p (n h) t -> p n h t", h=2)[:, :, k, :]
                s.need(dve, i - 2, f"c_O{CH - 1}")
                s.done(dve.tensor_tensor(of_head(at[p]), ps[:].rearrange("p (n q t) -> p n q t", n=2, q=2)[:, :, 1, :],
                                         of_head(dec), ALU.mult), f"b_ev{g}{k}")

            def masks(g):
                u = slice(4 * g, 4 * g + 4)
                s.need(pool, i, f"b_ev{g}0", f"b_ev{g}1")
                settle(pool, c["settle_pool"])
                s.done(pool.affine_select(out=bt[:, u, :], in_=bt[:, u, :], pattern=[[0, 4], [1, P]],
                                          compare_op=ALU.not_equal, fill=1.0, base=0, channel_multiplier=-1),
                       f"b_diag{g}")
                s.need(pool, i, f"b_diag{g}")
                s.need(pool, i - 1, f"b_T{g}")
                s.done(pool.tensor_tensor(tt[:, u, 1, :], bt[:, u, :],
                                          c["first"][:].unsqueeze(1).broadcast_to([P, 4, P]), ALU.mult), f"b_t2{g}")

            def mask(g, l):
                u = slice(4 * g, 4 * g + 4)
                s.need(pool, i - 1, f"b_M{l}{g}")
                s.done(pool.tensor_tensor(bm[:, l, u, :], bt[:, u, :],
                                          c["mask"][:, l, :].unsqueeze(1).broadcast_to([P, 4, P]), ALU.mult),
                       f"b_bm{l}{g}")

            def first_turn(g):
                s.need(pe, i, f"b_t2{g}")
                free(pe, B0_USERS, f"b_T2e{g}", i)
                ps = b0[:].bitcast(F16)
                for k in range(4):
                    ins = pe.transpose(ps[:, k * P:(k + 1) * P], tt[:, 4 * g + k, 1, :], c["ident16"][:])
                s.done(ins, f"b_T2p{g}")
                s.need(act, i, f"b_T2p{g}")
                s.done(act.copy(tt[:, 4 * g:4 * g + 4, 0, :], ps[:, 0:4 * P].rearrange("p (u t) -> p u t", t=P)),
                       f"b_T2e{g}")

            def joined(l, g):
                s.need(pe, i, f"b_bm{l}{g}")
                s.need(pe, i, *((["b_T2e1"] if g else []) if l == 0 else [f"b_Ue{l - 1}{g}1"]))
                free(pe, B0_USERS, f"b_Me{l}{g}", i)
                for k in range(4):
                    ins = pe.matmul(b0[:, k * P:(k + 1) * P], bm[:, l, 4 * g + k, :], tt[:, 4 * g + k, 0, :],
                                    start=True, stop=True)
                s.done(ins, f"b_M{l}{g}")
                s.need(act, i, f"b_M{l}{g}")
                s.done(act.copy(m1[:, 4 * g:4 * g + 4, :], b0[:].rearrange("p (u t) -> p u t", t=P)), f"b_Me{l}{g}")

            def update(l, g):
                s.need(pe, i, f"b_Me{l}{g}")
                for k in range(2):
                    free(pe, BH_USERS[k], f"b_Ue{l}{g}{k}", i)
                    for h in range(2):
                        u = 4 * g + 2 * k + h
                        pe.matmul(halves[k][:, h * 2 * P:h * 2 * P + P], tt[:, u, 1, :], m1[:, u, :], start=True,
                                  stop=True)
                        ins = pe.matmul(halves[k][:, h * 2 * P + P:(h + 1) * 2 * P], m1[:, u, :], tt[:, u, 1, :],
                                        start=True, stop=True)
                    s.done(ins, f"b_U{l}{g}{k}")
                for k in range(2):
                    s.need(dve, i, f"b_U{l}{g}{k}")
                    v = tt[:, 4 * g + 2 * k:4 * g + 2 * k + 2, :, :].rearrange("p u n t -> p (u n t)")
                    s.done(dve.tensor_tensor(v, v, halves[k][:], ALU.subtract), f"b_Ue{l}{g}{k}")

            def residual(g):
                s.need(act, i, f"b_Ue{NLEV - 1}{g}0", f"b_Ue{NLEV - 1}{g}1")
                s.need(act, i if g else i - 1, f"b_P{1 - g}")
                s.done(act.copy(t32[:], tt[:, 4 * g:4 * g + 4, 0, :]), f"b_t32{g}")
                s.need(pe, i, f"b_t32{g}")
                free(pe, B0_USERS, f"b_R{g}", i)
                for k in range(4):
                    ins = pe.matmul(b0[:, k * P:(k + 1) * P], bt[:, 4 * g + k, :], t32[:, k, :], start=True, stop=True)
                s.done(ins, f"b_P{g}")
                s.need(dve, i, f"b_P{g}")
                s.need(dve, i if g else i - 1, f"b_F{1 - g}")
                s.done(dve.tensor_tensor(r16[:], c["ident"][:].unsqueeze(1).broadcast_to([P, 4, P]),
                                         b0[:].rearrange("p (u t) -> p u t", t=P), ALU.subtract), f"b_R{g}")

            def corrected(g):
                s.need(pe, i, f"b_R{g}")
                free(pe, BH_USERS[g], f"b_T{g}", i)
                for k in range(4):
                    ins = pe.matmul(halves[g][:, k * P:(k + 1) * P], r16[:, k, :], tt[:, 4 * g + k, 1, :], start=True,
                                    stop=True)
                s.done(ins, f"b_F{g}")
                s.need(dve, i, f"b_F{g}")
                s.need(dve, i - 2, f"c_Z{CH - 1}")
                s.done(dve.tensor_tensor(tinv[p][:, 4 * g:4 * g + 4, :], tt[:, 4 * g:4 * g + 4, 1, :],
                                         halves[g][:].rearrange("p (u t) -> p u t", t=P), ALU.add), f"b_T{g}")

            L = lambda f, *a: (lambda: f(*a))
            steps = [squares, decays, exponentials, stats, scales]
            for g in range(2):
                steps += [L(products, g, 0), L(products, g, 1), L(masks, g), L(mask, g, 0)]
            steps += [L(first_turn, 0), L(first_turn, 1), decayed_kq]
            extra = [L(gate, 0), L(gate, 1), turn_k, L(turn_v, 0), L(turn_v, 1)]
            for l in range(NLEV):
                if l + 1 < NLEV:
                    steps += [L(mask, 0, l + 1), L(mask, 1, l + 1)]
                steps += [L(joined, l, 0), L(joined, l, 1), L(update, l, 0), L(update, l, 1)]
                if extra:
                    steps.append(extra.pop(0))
            steps += [L(residual, 0), L(residual, 1), L(corrected, 0), L(corrected, 1)]
            return steps

        def stage_c(i, p):
            def read_state(m):
                if m == 0:
                    return
                s.need(pe, i, f"c_S{m - 1}", "b_kqs")
                free(pe, CK_USERS, f"c_R{m}", i)
                ins = pe.matmul(ck[:, 0:2 * DV], kqs[p][:, 0, m * P:(m + 1) * P], state[:].rearrange("p h e -> p (h e)"),
                                start=True, stop=True)
                s.done(ins, f"c_KS{m}")
                s.need(dve, i, f"c_KS{m}", "b_vtok0", "b_vtok1")
                s.done(dve.tensor_tensor(rr[:], vtok[p][:, 2 * m:2 * m + 2, :],
                                         ck[:, 0:2 * DV].rearrange("p (h e) -> p h e", h=2), ALU.subtract), f"c_R{m}")

            def solve(m):
                if m == 0:
                    s.need(pe, i, "b_T0", "b_vtok0", "b_vtok1")
                else:
                    s.need(pe, i, f"c_R{m}", f"b_T{m // 2}")
                free(pe, CZ_USERS, f"c_u{m}", i)
                for h in range(2):
                    rhs = rr[:, h, :] if m else vtok[p][:, h, :]
                    ins = pe.matmul(cz[:, h * DV:(h + 1) * DV], tinv[p][:, 2 * m + h, :], rhs, start=True, stop=True)
                s.done(ins, f"c_Z{m}")
                s.need(act, i, f"c_Z{m}", "b_w1")
                for h in range(2):
                    ins = act.activation(uu[:, h, :], cz[:, h * DV:(h + 1) * DV], ACT.Copy,
                                         scale=w1[p][:, 2 * m + h:2 * m + h + 1])
                s.done(ins, f"c_u{m}")

            def outputs(m):
                s.need(pe, i, f"c_u{m}", "b_ktok", "b_kqs", f"b_ev{m // 2}{m % 2}")
                free(pe, CO_USERS, f"c_y{m}", i)
                for h in range(2):
                    if m:
                        pe.matmul(co[:, h * P:(h + 1) * P], state[:, h, :], kqs[p][:, 1, m * P:(m + 1) * P],
                                  start=True, stop=False)
                    ins = pe.matmul(co[:, h * P:(h + 1) * P], uu[:, h, :], at[p][:, 2 * m + h, :], start=m == 0,
                                    stop=True)
                s.done(ins, f"c_O{m}")
                if m < CH - 1:
                    free(pe, CK_USERS, f"c_S{m}", i)
                    for h in range(2):
                        ins = pe.matmul(ck[h * DK:(h + 1) * DK, 2 * DV:3 * DV], ktok[p][:, 2 * m + h, :],
                                        uu[:, h, :], start=True, stop=True)
                    s.done(ins, f"c_SU{m}")
                    s.need(dve, i, f"c_SU{m}", "b_gend")
                    for h in range(2):
                        rows = slice(h * DK, (h + 1) * DK)
                        if m == 0:
                            ins = dve.tensor_copy(state[rows, h, :], ck[rows, 2 * DV:3 * DV])
                        else:
                            ins = dve.scalar_tensor_tensor(state[rows, h, :], state[rows, h, :], gend[p][rows, m:m + 1],
                                                           ck[rows, 2 * DV:3 * DV], ALU.mult, ALU.add)
                    s.done(ins, f"c_S{m}")
                s.need(act, i, f"c_O{m}")
                s.done(act.activation(sqo[:], co[:, 0:2 * P].rearrange("p (h t) -> p h t", h=2), ACT.Square),
                       f"c_sq{m}")
                s.need(dve, i, f"c_sq{m}", "b_sg0", "b_sg1")
                s.done(dve.scalar_tensor_tensor(yy[:], co[:, 0:2 * P].rearrange("p (h t) -> p h t", h=2),
                                                normw[:, 0:1], sg[p][:, :, m * P:(m + 1) * P], ALU.mult, ALU.mult),
                       f"c_y{m}")

            def project_out(m):
                s.need(pe, i, f"c_sq{m}")
                free(pe, CK_USERS, f"c_m{m}", i)
                for h in range(2):
                    ins = pe.matmul(ck[:, 3 * DV + h:3 * DV + h + 1], sqo[:, h, :], c["ones_col"][:], start=True,
                                    stop=True)
                s.done(ins, f"c_ss{m}")
                s.need(pe, i, f"c_y{m}")
                if m == 0:
                    s.need_dma(pe, i // NB, "wo_in")
                free(pe, CZ_USERS, f"c_acc{m}", i)
                for h in range(2):
                    ins = pe.matmul(cz[:, h * D:(h + 1) * D], yy[:, h, :], wo[:, h, :], start=True, stop=True)
                s.done(ins, f"c_out{m}")
                s.need(dve, i, f"c_ss{m}", "b_s2sq", "b_s2")
                if m:
                    s.need(dve, i, f"c_r{m - 1}")
                else:
                    s.need(dve, i - 1, f"c_r{CH - 1}")
                s.done(dve.tensor_tensor(msq[:], ck[:, 3 * DV:3 * DV + 2], s2sq[p][:, 2 * m:2 * m + 2], ALU.mult),
                       f"c_m{m}")
                s.need(dve, i, f"c_m{m}")
                s.done(dve.tensor_scalar(msq[:], msq[:], LN_EPS, None, ALU.add), f"c_me{m}")
                s.need(pool, i, f"c_me{m}")
                if m:
                    s.need(pool, i, f"c_acc{m - 1}")
                else:
                    s.need(pool, i - 1, f"c_acc{CH - 1}")
                s.done(pool.tensor_tensor(rms[:], msq[:], c["minus_half"][:, 0:2], ALU.pow), f"c_p{m}")
                s.need(pool, i, f"c_p{m}")
                s.done(pool.tensor_tensor(rms[:], rms[:], s2[p][:, 2 * m:2 * m + 2], ALU.mult), f"c_r{m}")

            def accumulate(m):
                s.need(dve, i, f"c_out{m}", f"c_r{m}")
                a = acc[:, bass.ds((i % NB) * CH + m, 1), :].rearrange("p a d -> p (a d)")
                for h in range(2):
                    if h:
                        s.need(dve, i, f"c_acch{m}")
                    ins = dve.scalar_tensor_tensor(a, cz[:, h * D:(h + 1) * D], rms[:, h:h + 1], a, ALU.mult, ALU.add)
                    s.done(ins, f"c_acc{m}" if h else f"c_acch{m}")

            L = lambda f, *a: (lambda: f(*a))
            steps = []
            for m in range(CH):
                steps += [L(read_state, m)]
                if m:
                    steps += [L(accumulate, m - 1)]
                steps += [L(solve, m), L(outputs, m), L(project_out, m)]
            steps += [L(accumulate, CH - 1)]
            return steps

        def body(t, par):
            stages = []
            if active(t, NIT):
                stages.append(stage_a(t, par))
            if active(t - 1, NIT):
                stages.append(stage_b(t - 1, 1 - par))
            if active(t - 2, NIT):
                stages.append(stage_c(t - 2, par))
            for step in merged(*stages):
                step()

        for p in range(2):
            ins = pool.memset(pad[p][:, 0:PAD], 0.0)
        ins.then_inc(s.sem("pad_zero"), 1)
        dve.wait_ge(s.sem("pad_zero"), 1)
        dve.memset(state[:], 0.0).then_inc(s.sem("state_zero"), 1)
        pe.wait_ge(s.sem("state_zero"), 1)
        dve.memset(acc[:], 0.0).then_inc(s.sem("acc_zero"), 1)
        dve.wait_ge(s.sem("acc_zero"), 1)
        dve.wait_ge(s.sem("normw_in"), 16)
        dve.tensor_scalar(normw[:], normw[:], 0.5, None, ALU.mult).then_inc(s.sem("normw_half"), 1)
        dve.wait_ge(s.sem("normw_half"), 1)
        load_pair(0)
        with sp.Fori(1, NP) as hp:
            load_pair(hp)
        in_slots(nc, NIT, 2, 4, COMPUTE, body)
        ctx.finish()


def build(nc, a, out):
    with ExitStack() as ctx:
        sb = lambda name, shape, dt=F32: ctx.enter_context(nc.sbuf_tensor(name, shape, dt))
        xT_dram = nc.dram_tensor("xT_scratch", [NB + 1, P, KT, T], F32).ap()
        g_dram = nc.dram_tensor("g_scratch", [(NIT + 1) * NU, P], F32).ap()
        acc = sb("acc", [P, NTILE, D])
        c, s_const, n_const = make_constants(nc, ctx, sb)
        for eng in (nc.tensor, nc.vector, nc.scalar):
            eng.wait_ge(s_const, n_const)
        with ExitStack() as gates:
            gate_tok = [gates.enter_context(nc.sbuf_tensor(f"gate_tok{k}", [P, NIT * NU + NU], F32)) for k in range(2)]
            phase_norm(nc, c, a["x"], a["w_ab"], xT_dram, [g[:, 0:NIT * NU] for g in gate_tok])
            phase_gates(nc, c, a["A_log"], a["dt_bias"], [g[:, 0:NIT * NU] for g in gate_tok], g_dram)
            phase_delta(nc, c, a["w_qkv"], a["w_gate"], a["w_out"], None, a["norm_w"], xT_dram, g_dram, gate_tok, acc)
        phase_experts(nc, c, a, acc, out)


def phase_experts(nc, c, a, acc, out):
    with Phase(nc) as ctx:
        sb = lambda name, shape, dt=F32: ctx.enter_context(nc.sbuf_tensor(name, shape, dt))
        two = lambda name, shape, dt=F32: [sb(f"{name}{p}", shape, dt) for p in range(2)]
        bank = lambda name: ctx.enter_context(nc.psum_tensor(name, [P, 512], F32))
        pe, act, dve, pool, sp = nc.tensor, nc.scalar, nc.vector, nc.gpsimd, nc.sync
        s = Steps(nc, ctx)
        NR = E + E * PP
        wv = sb("e_wv", [P, KT, D])
        wr = sb("e_wr", [P, KT, NR])
        w1 = sb("e_w1", [P, KT, E * INNER])
        w2 = sb("e_w2", [P, KT, D])
        b2v = sb("e_b2v", [E + 1, D])
        bvc = sb("e_bvc", [P, KT])
        b1c = sb("e_b1c", [P, KT])
        b1h = sb("e_b1h", [P, KT])
        spread = sb("e_spread", [E, E * INNER])
        rows = sb("e_rows", [P, 5, E])
        alpha = sb("e_alpha", [P, 1])
        expert = sb("e_expert", [P, CH, E])
        x_in = two("e_x", [P, CH, D])
        x1 = two("e_x1_", [P, CH, D])
        xT = two("e_xT", [P, KT, T])
        xf = sb("e_xf", [P, CH, D])
        stats, mv, rstd = sb("e_stats", [P, CH, 6]), sb("e_mv", [P, CH, 2]), sb("e_rstd", [P, CH])
        o_stats, o_mv, o_rstd = sb("e_ostats", [P, CH, 6]), sb("e_omv", [P, CH, 2]), sb("e_orstd", [P, CH])
        vT = sb("e_vT", [P, KT, T])
        rc = sb("e_rc", [P, 2, CH, E])
        pv2 = sb("e_pv2", [P, CH, E, PP])
        c2 = sb("e_c2", [P, CH, E])
        mean, cen2 = sb("e_mean", [P, 2 * CH]), sb("e_cen2", [P, 2 * CH, E])
        var = sb("e_var", [P, 2 * CH])
        score = sb("e_score", [P, CH, E])
        top, idx = sb("e_top", [P, CH, 8]), sb("e_idx", [P, CH, 8], U32)
        idxf = sb("e_idxf", [P, CH, 8])
        gap, e2 = sb("e_gap", [P, CH]), sb("e_e2", [P, CH])
        share = sb("e_share", [P, CH, 2])
        hot = sb("e_hot", [P, 2, CH, E])
        we = sb("e_we", [P, CH, E + 1])
        weT = sb("e_weT", [E + 1, T])
        hz, hth, hw = sb("e_hz", [P, KT, T]), sb("e_hth", [P, KT, T]), sb("e_hw", [P, KT, T])
        yo = two("e_yo", [P, CH, D])
        turn = [bank(f"e_turn{k}") for k in range(KT)]
        vb = [bank(f"e_vb{k}") for k in range(KT)]
        rb, wb = bank("e_rb"), bank("e_wb")
        ob = [bank(f"e_ob{k}") for k in range(2)]

        s_w = ctx.semaphore("e_w_in")
        loads = [(wv[:], a["Wv"]), (wr[:], a["Wr"]), (w1[:], a["W1"]), (w2[:], a["W2"]), (b2v[:], a["b2v"]),
                 (bvc[:], a["bv"]), (b1c[:], a["b1"]), (rows[:], a["router_rows"].partition_broadcast(P)),
                 (alpha[:], a["alpha"].partition_broadcast(P))]
        for dst, src in loads:
            sp.dma_start(dst, src).then_inc(s_w, 16)
        s_k = ctx.semaphore("e_const")
        nk = [0]

        def build_step(ins):
            ins.then_inc(s_k, 1)
            nk[0] += 1
            pool.wait_ge(s_k, nk[0])

        build_step(pool.memset(spread[:], 0.5))
        build_step(pool.affine_select(out=spread[:], in_=spread[:], pattern=[[1, E * INNER]], compare_op=ALU.is_ge,
                                      fill=0.0, base=0, channel_multiplier=-INNER))
        build_step(pool.affine_select(out=spread[:], in_=spread[:], pattern=[[-1, E * INNER]], compare_op=ALU.is_ge,
                                      fill=0.0, base=INNER - 1, channel_multiplier=INNER))
        build_step(pool.iota(expert[:].bitcast(mybir.dt.int32), pattern=[[0, CH], [1, E]], base=0,
                             channel_multiplier=0))
        build_step(pool.tensor_copy(expert[:], expert[:].bitcast(mybir.dt.int32)))
        build_step(pool.memset(we[:, :, E:E + 1], 1.0))
        for eng in (pe, act, dve, pool):
            eng.wait_ge(s_w, 16 * len(loads))
            eng.wait_ge(s_k, nk[0])
        s_0 = ctx.semaphore("e_alpha_done")
        act.activation(alpha[:], alpha[:], ACT.Tanh, scale=0.5).then_inc(s_0, 1)
        act.mul(b1h[:], b1c[:], 0.5).then_inc(s_0, 1)
        act.wait_ge(s_0, 2)
        dve.wait_ge(s_0, 2)
        dve.tensor_scalar(alpha[:], alpha[:], 1.0, 0.5, ALU.add, ALU.mult).then_inc(s_0, 1)
        dve.wait_ge(s_0, 3)
        dve.tensor_scalar(rows[:, 2, :], rows[:, 2, :], alpha[:, 0:1], None, ALU.mult).then_inc(s_0, 1)
        dve.tensor_scalar(rows[:, 4, :], rows[:, 4, :], alpha[:, 0:1], None, ALU.mult).then_inc(s_0, 1)
        dve.wait_ge(s_0, 5)

        def chained(eng, i, name, ins):
            s.done(ins, name)
            s.need(eng, i, name)

        def norm_x(i, p):
            s.need(sp, i - 2, "x_x1")
            s.loaded(sp.dma_start(x_in[p][:], a["x"][bass.ds(i, 1)].rearrange("a p c d -> p (a c) d")),
                     f"x_in{p}")
            tiles = acc[:, bass.ds(i * CH, CH), :]
            for half in range(2):
                src = tiles if half == 0 else x1[p][:]
                for k in range(CH):
                    ins = dve.bn_stats(stats[:, k, :], src[:, k, :])
                chained(dve, i, f"x_bn{half}", ins)
                settle(dve, c["settle_dve"])
                for k in range(CH):
                    ins = dve.bn_aggr(mv[:, k, :], stats[:, k, :])
                chained(dve, i, f"x_mv{half}", ins)
                s.done(dve.tensor_scalar(rstd[:], mv[:, :, 1], LN_EPS, None, ALU.add), f"x_ve{half}")
                s.need(pool, i, f"x_ve{half}")
                s.done(pool.tensor_tensor(rstd[:], rstd[:], c["minus_half"][:, 0:CH], ALU.pow), f"x_rs{half}")
                s.need(dve, i, f"x_rs{half}")
                if half:
                    s.need(dve, i - 1, "x_turn")
                for k in range(CH):
                    ins = dve.tensor_scalar(xf[:, k, :] if half else tiles[:, k, :], src[:, k, :], mv[:, k, 0:1],
                                            rstd[:, k:k + 1], ALU.subtract, ALU.mult)
                if half == 0:
                    chained(dve, i, "x_y1", ins)
                    s.need_dma_of(dve, i, "x_in", p)
                    s.need(dve, i - 2, "o_sum")
                    chained(dve, i, "x_x1", dve.tensor_tensor(x1[p][:], tiles, x_in[p][:], ALU.add))
                else:
                    s.done(ins, "x_xf")
            s.need(pe, i, "x_xf")
            s.need(pe, i - 1, "x_xT")
            for k in range(KT):
                for m in range(CH):
                    ins = pe.transpose(turn[k][:, m * P:(m + 1) * P], xf[:, m, k * P:(k + 1) * P], c["ident"][:])
            s.done(ins, "x_turn")
            s.need(act, i, "x_turn")
            s.need(act, i - 2, "o_out1")
            for k in range(KT):
                ins = act.copy(xT[p][:, k, :], turn[k][:])
            s.done(ins, "x_xT")

        def experts(i, p):
            s.need(pe, i, "x_xT")
            s.need(pe, i - 1, "h_th1", "h_z1")
            for m in range(KT):
                for k in range(KT):
                    ins = pe.matmul(vb[m][:], wv[:, k, m * P:(m + 1) * P], xT[p][:, k, :], start=k == 0,
                                    stop=k == KT - 1)
            s.done(ins, "v_mm")
            s.need(act, i, "v_mm")
            s.need(act, i - 1, "h_mm1", "r_mm")
            for m in range(KT):
                ins = act.activation(vT[:, m, :], vb[m][:], ACT.Identity, bias=bvc[:, m:m + 1])
            s.done(ins, "v_T")
            s.need(pe, i, "v_T")
            s.need(pe, i - 1, "r_sq", "r_s")
            for m in range(CH):
                for k in range(KT):
                    ins = pe.matmul(rb[:, m * P:m * P + NR], vT[:, k, m * P:(m + 1) * P], wr[:, k, :], start=k == 0,
                                    stop=k == KT - 1)
            s.done(ins, "r_mm")
            for m in range(KT):
                for k in range(KT):
                    ins = pe.matmul(vb[m][:], w1[:, k, m * P:(m + 1) * P], vT[:, k, :], start=k == 0,
                                    stop=k == KT - 1)
                s.done(ins, f"h_mm{m}")
            r = rb[:].rearrange("p (c n) -> p c n", c=CH)
            s.need(act, i, "r_mm")
            s.need(act, i - 1, "r_c2")
            s.done(act.activation(pv2[:].rearrange("p c e n -> p c (e n)"), r[:, :, E:NR], ACT.Square), "r_sq")
            s.need(act, i - 1, "h_s1")
            for m in range(KT):
                s.need(act, i, f"h_mm{m}")
                s.done(act.activation(hth[:, m, :], vb[m][:], ACT.Tanh, bias=b1h[:, m:m + 1], scale=0.5), f"h_th{m}")
                s.done(act.activation(hz[:, m, :], vb[m][:], ACT.Identity, bias=b1c[:, m:m + 1]), f"h_z{m}")
            s.need(dve, i, "r_sq")
            s.need(dve, i - 1, "r_score")
            s.done(dve.tensor_tensor(rc[:, 0], r[:, :, 0:E], rows[:, 0, :].unsqueeze(1).broadcast_to([P, CH, E]),
                                     ALU.add), "r_s")
            s.need(dve, i - 1, "r_cn")
            s.done(dve.tensor_reduce(c2[:], pv2[:], AX.X, ALU.add), "r_c2")
            s.need(dve, i, "r_c2")
            s.done(dve.tensor_scalar(c2[:], c2[:], 1.0 / PP, None, ALU.mult), "r_c3")
            s.need(pool, i, "r_c3")
            s.need(pool, i - 1, "r_score")
            s.done(pool.tensor_tensor(rc[:, 1], c2[:], c["half"][:].unsqueeze(1)[:, :, 0:E].broadcast_to([P, CH, E]),
                                      ALU.pow), "r_cn")
            for m in range(KT):
                s.need(dve, i, f"h_z{m}", f"h_th{m}")
                s.need(dve, i - 1, "o_out1")
                s.done(dve.scalar_tensor_tensor(hw[:, m, :], hth[:, m, :], 1.0, hz[:, m, :], ALU.add, ALU.mult),
                       f"h_s{m}")
            flat = rc[:].rearrange("p n c e -> p (n c) e")
            along = lambda t: t[:].unsqueeze(2).broadcast_to([P, 2 * CH, E])
            per_kind = lambda k: rows[:, k:k + 2, :].unsqueeze(2).broadcast_to([P, 2, CH, E])
            s.need(dve, i, "r_cn", "r_s")
            chained(dve, i, "r_sum", dve.tensor_reduce(mean[:], flat, AX.X, ALU.add))
            chained(dve, i, "r_mean", dve.tensor_scalar(mean[:], mean[:], 1.0 / E, None, ALU.mult))
            chained(dve, i, "r_cen", dve.tensor_tensor(flat, flat, along(mean), ALU.subtract))
            chained(dve, i, "r_cen2", dve.tensor_tensor(cen2[:], flat, flat, ALU.mult))
            chained(dve, i, "r_var", dve.tensor_reduce(var[:], cen2[:], AX.X, ALU.add))
            s.done(dve.tensor_scalar(var[:], var[:], 1.0 / E, LN_EPS, ALU.mult, ALU.add), "r_vare")
            s.need(pool, i, "r_vare")
            s.done(pool.tensor_tensor(var[:], var[:], c["minus_half"][:, 0:2 * CH], ALU.pow), "r_rstd")
            s.need(dve, i, "r_rstd")
            chained(dve, i, "r_n0", dve.tensor_tensor(flat, flat, along(var), ALU.mult))
            chained(dve, i, "r_n1", dve.tensor_tensor(rc[:], rc[:], per_kind(1), ALU.mult))
            chained(dve, i, "r_n2", dve.tensor_tensor(rc[:], rc[:], per_kind(3), ALU.add))
            chained(dve, i, "r_score", dve.tensor_tensor(score[:], rc[:, 0], rc[:, 1], ALU.add))
            settle(dve, c["settle_dve"])
            for m in range(CH):
                ins = dve.max(top[:, m, :], score[:, m, :])
            chained(dve, i, "t_max", ins)
            settle(dve, c["settle_dve"])
            for m in range(CH):
                ins = dve.max_index(idx[:, m, :], top[:, m, :], score[:, m, :])
            chained(dve, i, "t_idx", ins)
            s.need(dve, i - 1, "t_e2")
            s.done(dve.tensor_tensor(gap[:], top[:, :, 1], top[:, :, 0], ALU.subtract), "t_gap")
            chained(dve, i, "t_idxf", dve.tensor_copy(idxf[:], idx[:]))
            s.need(act, i, "t_gap")
            s.need(act, i - 1, "t_sh1")
            s.done(act.activation(e2[:], gap[:], ACT.Exp), "t_e2")
            for k in range(2):
                ins = dve.tensor_tensor(hot[:, k], expert[:], idxf[:, :, k:k + 1].broadcast_to([P, CH, E]),
                                        ALU.is_equal)
            s.done(ins, "t_hot")
            s.need(dve, i, "t_e2")
            chained(dve, i, "t_den", dve.tensor_scalar(share[:, :, 0], e2[:], 1.0, None, ALU.add))
            chained(dve, i, "t_sh0", dve.reciprocal(share[:, :, 0], share[:, :, 0]))
            s.done(dve.tensor_tensor(share[:, :, 1], share[:, :, 0], e2[:], ALU.mult), "t_sh1")
            s.need(dve, i, "t_hot", "t_sh1")
            for k in range(2):
                ins = dve.tensor_tensor(hot[:, k], hot[:, k], share[:, :, k:k + 1].broadcast_to([P, CH, E]), ALU.mult)
            chained(dve, i, "t_w", ins)
            s.need(dve, i - 1, "w_turn")
            s.done(dve.tensor_tensor(we[:, :, 0:E], hot[:, 0], hot[:, 1], ALU.add), "t_we")
            s.need(pe, i, "t_we")
            s.need(pe, i - 1, "w_hw1")
            for m in range(CH):
                ins = pe.transpose(wb[0:E + 1, m * P:(m + 1) * P], we[:, m, :], c["ident"][:])
            s.done(ins, "w_turn")
            s.need(act, i, "w_turn")
            s.need(act, i - 1, "o_out1")
            s.done(act.copy(weT[:], wb[0:E + 1, :]), "w_T")
            for m in range(KT):
                s.need(pe, i, "w_T" if m == 0 else "w_hw0")
                s.done(pe.matmul(wb[:], spread[:, m * P:(m + 1) * P], weT[0:E, :], start=True, stop=True), f"w_mm{m}")
                s.need(dve, i, f"w_mm{m}", f"h_s{m}")
                s.done(dve.tensor_tensor(hw[:, m, :], hw[:, m, :], wb[:], ALU.mult), f"w_hw{m}")
            for half in range(2):
                s.need(pe, i, "w_hw1", "w_T")
                s.need(pe, i - 1, f"o_n{half}")
                for m in (2 * half, 2 * half + 1):
                    o = ob[half][:, (m % 2) * D:(m % 2 + 1) * D]
                    tok = slice(m * P, (m + 1) * P)
                    for k in range(KT):
                        pe.matmul(o, xT[p][:, k, tok], wv[:, k, :], start=k == 0, stop=False)
                    for k in range(KT):
                        pe.matmul(o, hw[:, k, tok], w2[:, k, :], start=False, stop=False)
                    ins = pe.matmul(o, weT[:, tok], b2v[:], start=False, stop=True)
                s.done(ins, f"o_out{half}")
            for half in range(2):
                s.need(dve, i, f"o_out{half}")
                for m in (2 * half, 2 * half + 1):
                    ins = dve.bn_stats(o_stats[:, m, :], ob[half][:, (m % 2) * D:(m % 2 + 1) * D])
            chained(dve, i, "o_bn", ins)
            settle(dve, c["settle_dve"])
            for m in range(CH):
                ins = dve.bn_aggr(o_mv[:, m, :], o_stats[:, m, :])
            chained(dve, i, "o_mv", ins)
            s.done(dve.tensor_scalar(o_rstd[:], o_mv[:, :, 1], LN_EPS, None, ALU.add), "o_ve")
            s.need(pool, i, "o_ve")
            s.done(pool.tensor_tensor(o_rstd[:], o_rstd[:], c["minus_half"][:, 0:CH], ALU.pow), "o_rs")
            s.need(dve, i, "o_rs")
            s.need_dma_of(dve, i - 2, "y_out", p)
            for half in range(2):
                for m in (2 * half, 2 * half + 1):
                    ins = dve.tensor_scalar(yo[p][:, m, :], ob[half][:, (m % 2) * D:(m % 2 + 1) * D],
                                            o_mv[:, m, 0:1], o_rstd[:, m:m + 1], ALU.subtract, ALU.mult)
                s.done(ins, f"o_n{half}")
            s.need(dve, i, "o_n1")
            s.done(dve.tensor_tensor(yo[p][:], yo[p][:], x1[p][:], ALU.add), "o_sum")
            s.need(sp, i, "o_sum")
            s.loaded(sp.dma_start(out[bass.ds(i, 1)].rearrange("a p c d -> p (a c) d"), yo[p][:]),
                     f"y_out{p}")

        def body(t, par):
            if active(t, NB):
                norm_x(t, par)
            if active(t - 1, NB):
                experts(t - 1, 1 - par)

        in_slots(nc, NB, 1, 3, EVERY, body)
        for p in range(2):
            sp.wait_ge(s.sem(f"y_out{p}"), 16 * NB // 2)


def kernel(**inputs):
    import numpy as np
    import concourse.bacc as bacc
    from concourse.bass_utils import run_bass_kernel_spmd

    v = {k: np.asarray(x) for k, x in inputs.items()}
    at = lambda name: v["L0_attn_" + name]
    ff = lambda name: v["L0_ffn_" + name]
    rows = lambda w: w.reshape(KT, P, -1).transpose(1, 0, 2)
    by_pair = lambda w, n: rows(w).reshape(P, KT, NP, n).transpose(2, 0, 1, 3)
    tap_of = lambda w, n: w.reshape(NP, n, P, TAPS).transpose(0, 2, 1, 3)
    wqkv = np.concatenate([by_pair(at("w_q"), P), by_pair(at("w_k"), P), by_pair(at("w_v"), 2 * P)], axis=3)
    taps = np.concatenate([tap_of(at("conv_q"), 1), tap_of(at("conv_k"), 1), tap_of(at("conv_v"), 2)], axis=2)
    arrays = {
        "x": at("x").reshape(NB, CH, P, D).transpose(0, 2, 1, 3),
        "w_ab": rows(np.concatenate([at("w_a"), at("w_b")], axis=1)),
        "A_log": at("A_log"),
        "dt_bias": at("dt_bias"),
        "w_qkv": np.concatenate([wqkv.reshape(NP, P, -1), taps.reshape(NP, P, -1)], axis=2),
        "w_gate": by_pair(at("w_g"), 2 * P),
        "w_out": at("w_out").reshape(NP, 2, P, D).transpose(0, 2, 1, 3),
        "norm_w": at("norm_w").reshape(P, 1),
        "Wv": rows(ff("Wv").T),
        "Wr": rows(np.concatenate([ff("Wg").T, ff("Wp").reshape(E * PP, D).T], axis=1)),
        "W1": rows(ff("W1").reshape(E * INNER, D).T),
        "W2": rows(ff("W2").transpose(0, 2, 1).reshape(E * INNER, D)),
        "b2v": np.concatenate([ff("b2"), ff("bv")[None]], axis=0),
        "bv": ff("bv").reshape(KT, P).T,
        "b1": ff("b1").reshape(KT, P).T,
        "router_rows": np.stack([ff("bg"), ff("g_r"), ff("g_c"), ff("b_r"), ff("b_c")]),
        "alpha": ff("alpha").reshape(1),
    }
    nc = bacc.Bacc("TRN2", target_bir_lowering=False, num_devices=1)
    arrays = {k: np.ascontiguousarray(x) for k, x in arrays.items()}
    aps = {k: nc.dram_tensor("in_" + k, x.shape, mybir.dt.from_np(x.dtype), kind="ExternalInput").ap()
           for k, x in arrays.items()}
    out = nc.dram_tensor("out_y", (NB, P, CH, D), F32, kind="ExternalOutput").ap()
    build(nc, aps, out)
    r = run_bass_kernel_spmd(nc, [{"in_" + k: x for k, x in arrays.items()}], core_ids=[0])
    y = r.results[0]["out_y"]
    return y.transpose(0, 2, 1, 3).reshape(NB, T, D)
```

```python
from contextlib import ExitStack

import concourse.bass as bass
from concourse import mybir

ALU = mybir.AluOpType
ACT = mybir.ActivationFunctionType
AX = mybir.AxisListType
F32 = mybir.dt.float32
F16 = mybir.dt.float16
U32 = mybir.dt.uint32

P = 128
D = 256
KT = D // P
NB, T = 16, 512
H, DK, DV = 16, 64, 128
NP = H // 2
NIT = NP * NB
CH = T // P
NU = 2 * CH
TAPS = 4
PAD = TAPS - 1
NLEV = 6
NTILE = NB * CH
E, INNER, PP = 8, 32, 8
COMPUTE = (mybir.EngineType.PE, mybir.EngineType.Activation, mybir.EngineType.DVE, mybir.EngineType.Pool)
EVERY = COMPUTE + (mybir.EngineType.SP,)
NEG = -1.0e4
LN_EPS = 1e-5
N_QKV = 2 * P + 2 * P


SLOT_ORDER = """
    b_kk00 b_d b_sq b_stat b_ss b_gam b_kk01 b_sel b_w1 b_E a_proj0 a_evac0 b_g0 c_Z0 b_ev00 b_kk10 b_ev01
    a_tap00 b_ev10 b_diag0 c_u0 b_kk11 a_tap01 b_t20 b_ev11 b_bm00 c_SU0 b_gend c_O0 b_Tq0 a_proj1 b_tg0
    b_diag1 c_S0 b_Tf0 b_t21 a_tap02 b_bm01 b_M00 c_sq0 b_sg0 c_KS1 b_Tq1 b_bm10 a_tanh0 b_Me00 c_R1 b_U00
    b_Tf1 c_y0 c_ss0 b_bm11 c_Z1 a_evac1 c_m0 b_Ue00 b_M01 c_u1 b_bm20 b_g1 a_silu0 b_Me01 c_me0 b_Tp00 b_U01
    b_Ue01 c_SU1 a_tap10 a_tap11 b_bm21 c_O1 b_Te00 b_M10 a_tap12 b_Tp01 b_Me10 b_Te01 c_S1 a_proj2 b_tg1
    a_tanh1 b_M11 b_U10 c_KS2 b_sg1 c_p0 b_Ue10 b_Me11 b_U11 b_root a_evac2 b_Tp10 b_bm30 b_Te10 b_Ue11 c_sq1
    b_bm31 c_out0 c_acch0 b_Tp11 b_M20 a_proj3 a_tap20 b_Te11 b_Me20 c_R2 c_acc0 b_U20 a_tap21 b_Ue20 b_M21
    b_kT b_kqs b_bm40 b_Me21 c_y1 b_Tp20 b_U21 c_Z2 c_ss1 b_Te20 b_Ue21 c_m1 b_M30 b_Tp21 a_silu1 c_u2 c_SU2
    c_me1 b_Me30 b_U30 b_Te21 b_M31 b_bm41 c_O2 b_Me31 c_p1 a_evac3 b_bm50 b_ktok b_Ue30 b_U31 b_Tp30 a_tap22
    c_S2 b_Ue31 b_Te30 c_out1 b_M40 b_Tp31 c_KS3 a_tanh2 b_s2 b_Me40 c_acch1 b_Te31 c_acc1 c_sq2 b_U40 b_M41
    c_R3 b_Ue40 b_vT0 b_Tp40 b_Me41 c_Z3 b_Te40 b_U41 a_tap30 c_y2 b_M50 c_ss2 b_Ue41 c_m2 b_Tp41 c_u3 b_Me50
    c_me2 b_Te41 b_U50 c_O3 c_sq3 b_bm51 b_M51 a_silu2 c_p2 b_Ue50 a_tap31 b_vtok0 b_Tp50 c_out2 b_Me51 a_tap32
    c_y3 b_U51 b_Te50 b_Ue51 c_acch2 a_tanh3 b_P0 c_ss3 b_Tp51 b_R0 c_m3 c_acc2 c_me3 b_vT1 b_vtok1 c_p3 b_Te51
    b_F0 b_T0 b_P1 a_silu3 c_out3 b_R1 c_acch3 b_F1 b_T1 c_acc3
""".split()


class Phase(ExitStack):

    def __init__(self, nc):
        super().__init__()
        self.nc, self.sems = nc, []

    def semaphore(self, name):
        self.sems.append(self.nc.alloc_semaphore(name=name))
        return self.sems[-1]

    def finish(self):
        self.nc.all_engine_barrier()
        self.nc.clear_and_free_semaphores(self.sems)
        self.nc.all_engine_barrier()


class Steps:

    def __init__(self, nc, ctx):
        self.nc, self.ctx, self.at, self.last = nc, ctx, {}, {}

    def series(self, name, steps):
        sem = self.ctx.semaphore(name)
        self.last[name] = len(steps) - 1
        for k, step in enumerate(steps):
            self.at[step] = (sem, name, k, len(steps))

    def find(self, name):
        if name not in self.at:
            self.series(name, [name])
        return self.at[name]

    def sem(self, name):
        return self.find(name)[0]

    def done(self, instruction, name):
        sem, series, k, n = self.find(name)
        assert k == (self.last[series] + 1) % n, (name, self.last[series])
        self.last[series] = k
        instruction.then_inc(sem, 1)

    def loaded(self, dma, name):
        dma.then_inc(self.sem(name), 16)

    def need(self, eng, i, *names):
        if isinstance(i, int) and i < 0:
            return
        latest = {}
        for name in names:
            sem, series, k, n = self.find(name)
            if series not in latest or latest[series][1] < k:
                latest[series] = (sem, k, n)
        for sem, k, n in latest.values():
            eng.wait_ge(sem, i * n + (k + 1))

    def need_dma(self, eng, i, name):
        if isinstance(i, int) and i < 0:
            return
        eng.wait_ge(self.sem(name), (i + 1) * 16)

    def need_dma_of(self, eng, i, name, par):
        if isinstance(i, int) and i < 0:
            return
        eng.wait_ge(self.sem(f"{name}{par}"), (i // 2 + 1) * 16)


class Chain:

    def __init__(self, nc, ctx, name, per):
        self.sem, self.per, self.k = ctx.semaphore(name), per, 0

    def start(self, i):
        self.i, self.k = i, 0

    def inc(self, instruction):
        instruction.then_inc(self.sem, 1)
        self.k += 1
        return self.i * self.per + self.k

    def end(self):
        assert self.k == self.per, (self.k, self.per)

    def last_of(self, i):
        return (i + 1) * self.per


def in_slots(nc, n, lag, first, engines, body):
    for t in range(first):
        body(t, t % 2)
    end = first + (n - first) // 2 * 2
    with nc.Fori(first, end, 2, engines=engines) as t:
        body(t, first % 2)
        body(t + 1, (first + 1) % 2)
    for t in range(end, n + lag):
        body(t, t % 2)


def active(i, n):
    return not isinstance(i, int) or 0 <= i < n


def issue(order, threads):
    pending = {next(thread): thread for thread in threads}
    for name in order:
        if name in pending:
            thread = pending.pop(name)
            following = next(thread, None)
            if following:
                pending[following] = thread
    assert not pending, sorted(pending)


def settle(eng, scratch):
    eng.tensor_tensor(scratch[0:1, 0:1], scratch[0:1, 1:2], scratch[0:1, 1:2], ALU.add)


def make_constants(nc, ctx, sb):
    pool = nc.gpsimd
    s_const = ctx.enter_context(nc.semaphore("const_built"))
    n = [0]

    def step(ins):
        ins.then_inc(s_const, 1)
        n[0] += 1
        pool.wait_ge(s_const, n[0])

    c = {}
    c["ident"] = sb("ident", [P, P], F32)
    step(pool.memset(c["ident"][:], 1.0))
    step(pool.affine_select(out=c["ident"][:], in_=c["ident"][:], pattern=[[-1, P]], compare_op=ALU.is_equal,
                            fill=0.0, base=0, channel_multiplier=1))
    c["ident16"] = sb("ident16", [P, P], F16)
    step(pool.tensor_copy(c["ident16"][:], c["ident"][:]))
    c["upper"] = sb("upper", [P, P], F32)
    step(pool.memset(c["upper"][:], 1.0))
    step(pool.affine_select(out=c["upper"][:], in_=c["upper"][:], pattern=[[1, P]], compare_op=ALU.is_ge,
                            fill=0.0, base=0, channel_multiplier=-1))
    c["ones_col"] = sb("ones_col", [P, 1], F32)
    step(pool.memset(c["ones_col"][:], 1.0))
    c["head_sel"] = sb("head_sel", [P, 2], F32)
    step(pool.memset(c["head_sel"][:], 0.0))
    step(pool.memset(c["head_sel"][0:DK, 0:1], 1.0))
    step(pool.memset(c["head_sel"][DK:P, 1:2], 1.0))
    for name in ("settle_dve", "settle_pool"):
        c[name] = sb(name, [P, 2], F32)
        step(pool.memset(c[name][:], 0.0))
    for name, value in (("half", 0.5), ("minus_half", -0.5)):
        c[name] = sb(name, [P, 16], F32)
        step(pool.memset(c[name][:], value))

    def block_mask(view_of, size, value):
        nblk = P // (2 * size)
        v = view_of.rearrange("p (b t r) -> p b t r", t=2, r=size)[:, :, 1, :]
        step(pool.memset(v, value))
        step(pool.affine_select(out=v, in_=v, pattern=[[-2 * size, nblk], [0, size]], compare_op=ALU.is_ge,
                                fill=0.0, base=0, channel_multiplier=1))
        step(pool.affine_select(out=v, in_=v, pattern=[[2 * size, nblk], [0, size]], compare_op=ALU.is_ge,
                                fill=0.0, base=size - 1, channel_multiplier=-1))

    c["mask"] = sb("mask", [P, NLEV, P], F16)
    step(pool.memset(c["mask"][:], 0.0))
    for lev in range(NLEV):
        block_mask(c["mask"][:, lev, :], 2 << lev, 1.0)
    c["first"] = sb("first", [P, P], F16)
    step(pool.memset(c["first"][:], 0.0))
    block_mask(c["first"][:], 1, -1.0)
    step(pool.tensor_tensor(c["first"][:], c["first"][:], c["ident16"][:], ALU.add))
    return c, s_const, n[0]


def phase_norm(nc, c, x, w_ab, xT_dram, gate_tok):
    with Phase(nc) as ctx:
        sb = lambda name, shape, dt=F32: ctx.enter_context(nc.sbuf_tensor(name, shape, dt))
        x_in = [sb(f"n_x{p}", [P, CH, D]) for p in range(2)]
        xn = [sb(f"n_xn{p}", [P, CH, D]) for p in range(2)]
        xT = [sb(f"n_xT{p}", [P, KT, T]) for p in range(2)]
        stats = sb("n_stats", [P, CH, 6])
        mv = sb("n_mv", [P, CH, 2])
        rstd = sb("n_rstd", [P, CH])
        wab = sb("n_wab", [P, KT, 2 * H])
        turn_ps = [ctx.enter_context(nc.psum_tensor(f"n_turn{k}", [P, T], F32)) for k in range(KT)]
        ab_ps = ctx.enter_context(nc.psum_tensor("n_ab", [P, CH, P], F32))
        s = Steps(nc, ctx)
        dve = Chain(nc, ctx, "n_dve", 3 * CH)

        nc.sync.dma_start(wab[:], w_ab).then_inc(s.sem("n_wab_in"), 16)

        def body(t, par):
            i, j = t, t - 1
            if active(i, NB):
                s.need(nc.sync, i - 2, "n_xn")
                s.loaded(nc.sync.dma_start(x_in[par][:], x[bass.ds(i, 1)].rearrange("a p c d -> p (a c) d")), f"n_x_in{par}")
                s.need_dma_of(nc.vector, i, "n_x_in", par)
                dve.start(i)
                for k in range(CH):
                    v = dve.inc(nc.vector.bn_stats(stats[:, k, :], x_in[par][:, k, :]))
                nc.vector.wait_ge(dve.sem, v)
                settle(nc.vector, c["settle_dve"])
                for k in range(CH):
                    v = dve.inc(nc.vector.bn_aggr(mv[:, k, :], stats[:, k, :]))
                nc.vector.wait_ge(dve.sem, v)
                s.need(nc.vector, i - 1, "n_rstd")
                v = dve.inc(nc.vector.tensor_scalar(rstd[:], mv[:, :, 1], LN_EPS, None, ALU.add))
                nc.gpsimd.wait_ge(dve.sem, v)
                s.done(nc.gpsimd.tensor_tensor(rstd[:], rstd[:], c["minus_half"][:, 0:CH], ALU.pow), "n_rstd")
                s.need(nc.vector, i, "n_rstd")
                s.need(nc.vector, i - 2, "n_turn")
                for k in range(CH):
                    ins = nc.vector.tensor_scalar(xn[par][:, k, :], x_in[par][:, k, :], mv[:, k, 0:1],
                                                  rstd[:, k:k + 1], ALU.subtract, ALU.mult)
                    if k < CH - 1:
                        dve.inc(ins)
                s.done(ins, "n_xn")
            if active(j, NB):
                q = 1 - par
                s.need(nc.tensor, j, "n_xn")
                s.need(nc.tensor, j - 1, "n_xT")
                for k in range(KT):
                    for m in range(CH):
                        ins = nc.tensor.transpose(turn_ps[k][:, m * P:(m + 1) * P], xn[q][:, m, k * P:(k + 1) * P],
                                                  c["ident"][:])
                s.done(ins, "n_turn")
                s.need_dma_of(nc.scalar, j - 2, "n_xT_out", q)
                s.need(nc.scalar, j - 2, "n_ab")
                s.need(nc.scalar, j, "n_turn")
                for k in range(KT):
                    ins = nc.scalar.copy(xT[q][:, k, :], turn_ps[k][:])
                s.done(ins, "n_xT")
                s.need(nc.sync, j, "n_xT")
                s.loaded(nc.sync.dma_start(xT_dram[bass.ds(j, 1)].rearrange("a p k t -> p (a k) t"), xT[q][:]),
                         f"n_xT_out{q}")
                s.need(nc.tensor, j, "n_xT")
                if isinstance(j, int) and j == 0:
                    nc.tensor.wait_ge(s.sem("n_wab_in"), 16)
                s.need(nc.tensor, j - 1, "n_ab_out")
                for m in range(CH):
                    for k in range(KT):
                        ins = nc.tensor.matmul(ab_ps[:, m, 0:2 * H], xT[q][:, k, m * P:(m + 1) * P], wab[:, k, :],
                                               start=k == 0, stop=k == KT - 1)
                s.done(ins, "n_ab")
                s.need(nc.vector, j, "n_ab")
                dve2_in = ab_ps[:, :, 0:2 * H].rearrange("p c (n q h) -> p n c q h", n=2, h=2)
                for n in range(2):
                    for m in range(CH):
                        dst = gate_tok[n][:].rearrange("p (q x) -> p q x", q=NP)[:, :, bass.ds(j * NU + 2 * m, 2)]
                        ins = nc.vector.tensor_copy(dst, dve2_in[:, n, m])
                s.done(ins, "n_ab_out")

        in_slots(nc, NB, 1, 3, EVERY, body)
        for p in range(2):
            nc.sync.wait_ge(s.sem(f"n_xT_out{p}"), 16 * NB // 2)
        ctx.finish()


def phase_gates(nc, c, a_log, dt_bias, gate_tok, g_dram):
    with Phase(nc) as ctx:
        sb = lambda name, shape, dt=F32: ctx.enter_context(nc.sbuf_tensor(name, shape, dt))
        W = NIT * NU
        alog = sb("g_alog", [P, H])
        nega = sb("g_nega", [P, H])
        dtb = sb("g_dtb", [P, H])
        z, az, rows = sb("g_z", [P, W]), sb("g_az", [P, W]), sb("g_rows", [P, W // P, P])
        ps = [ctx.enter_context(nc.psum_tensor(f"g_ps{k}", [P, 512], F32)) for k in range(2)]
        s_in = ctx.semaphore("g_in")
        s_v = ctx.semaphore("g_dve")
        s_a = ctx.semaphore("g_act")
        s_p = ctx.semaphore("g_pe")
        s_out = ctx.semaphore("g_out")
        by_head = lambda t: t[:].rearrange("p (q x h) -> p q x h", q=NP, h=2)
        spread = lambda t: t[:].rearrange("p (q x h) -> p q x h", x=1, h=2).broadcast_to([P, NP, W // H, 2])

        nc.sync.dma_start(alog[:], a_log.partition_broadcast(P)).then_inc(s_in, 16)
        nc.sync.dma_start(dtb[:], dt_bias.partition_broadcast(P)).then_inc(s_in, 16)
        nc.vector.wait_ge(s_in, 32)
        nc.scalar.wait_ge(s_in, 32)
        nc.vector.tensor_tensor(by_head(z), by_head(gate_tok[0]), spread(dtb), ALU.add).then_inc(s_v, 1)
        nc.scalar.wait_ge(s_v, 1)
        nc.scalar.activation(az[:], z[:], ACT.Abs).then_inc(s_a, 1)
        nc.scalar.wait_ge(s_a, 1)
        nc.scalar.activation(az[:], az[:], ACT.Exp, scale=-1.0).then_inc(s_a, 1)
        nc.scalar.activation(nega[:], alog[:], ACT.Exp).then_inc(s_a, 1)
        nc.scalar.wait_ge(s_a, 2)
        nc.scalar.activation(az[:], az[:], ACT.Ln, bias=1.0).then_inc(s_a, 1)
        nc.vector.wait_ge(s_v, 1)
        nc.vector.wait_ge(s_a, 4)
        nc.vector.scalar_tensor_tensor(z[:], z[:], 0.0, az[:], ALU.max, ALU.add).then_inc(s_v, 1)
        nc.vector.tensor_scalar(nega[:], nega[:], -1.0, None, ALU.mult).then_inc(s_v, 1)
        nc.vector.wait_ge(s_v, 3)
        nc.vector.tensor_tensor(by_head(z), by_head(z), spread(nega), ALU.mult).then_inc(s_v, 1)
        nc.scalar.activation(gate_tok[1][:], gate_tok[1][:], ACT.Tanh, scale=0.5).then_inc(s_a, 1)
        nc.vector.wait_ge(s_a, 5)
        nc.vector.tensor_scalar(gate_tok[1][:], gate_tok[1][:], 1.0, None, ALU.add).then_inc(s_v, 1)
        nc.tensor.wait_ge(s_v, 4)
        for k in range(2):
            nc.tensor.matmul(ps[k][:], c["upper"][:], z[:, k * 512:(k + 1) * 512], start=True,
                             stop=True).then_inc(s_p, 1)
        for k in range(2):
            nc.vector.wait_ge(s_p, k + 1)
            nc.vector.tensor_copy(gate_tok[0][:, k * 512:(k + 1) * 512], ps[k][:]).then_inc(s_v, 1)
        for k in range(2):
            nc.tensor.wait_ge(s_v, 6 + k)
            for m in range(4):
                col = k * 512 + m * P
                ins = nc.tensor.transpose(ps[k][:, m * P:(m + 1) * P], gate_tok[0][:, col:col + P], c["ident"][:])
            ins.then_inc(s_p, 1)
        for k in range(2):
            nc.scalar.wait_ge(s_p, 3 + k)
            nc.scalar.copy(rows[:, 4 * k:4 * k + 4, :], ps[k][:].rearrange("p (a b) -> p a b", a=4)).then_inc(s_a, 1)
        nc.sync.wait_ge(s_a, 7)
        nc.sync.dma_start(g_dram[0:NIT * NU].rearrange("(a r) t -> r a t", r=P), rows[:]).then_inc(s_out, 16)
        nc.sync.wait_ge(s_out, 16)
        ctx.finish()


def phase_delta(nc, c, w_qkv, w_gate, w_out, taps, norm_w, xT_dram, g_dram, gate_tok, acc):
    with Phase(nc) as ctx:
        sb = lambda name, shape, dt=F32: ctx.enter_context(nc.sbuf_tensor(name, shape, dt))
        two = lambda name, shape, dt=F32: [sb(f"{name}{p}", shape, dt) for p in range(2)]
        bank = lambda name: ctx.enter_context(nc.psum_tensor(name, [P, 512], F32))
        pe, act, dve, pool, sp = nc.tensor, nc.scalar, nc.vector, nc.gpsimd, nc.sync
        s = Steps(nc, ctx)

        wq = sb("wqkv", [P, KT * N_QKV + 4 * TAPS])
        wqkv = wq[:, 0:KT * N_QKV].rearrange("p (k n) -> p k n", k=KT)
        tap = wq[:, KT * N_QKV:].rearrange("p (j r) -> p j r", r=TAPS)
        wg = sb("wgate", [P, KT, 2 * P])
        wo = sb("wout", [P, 2, D])
        normw = sb("normw", [P, 1])
        xin = two("xin", [P, KT, T])
        kq = two("kq", [P, 2, T])
        vch = two("vch", [P, 2, T])
        pad = two("pad", [P, PAD + T])
        cv = two("cv", [P, T])
        th = sb("th", [P, T])
        grow = sb("grow", [P, NU, P])
        g_it = sb("g_it", [P, NU])
        dec = sb("dec", [P, NU, P])
        dend = sb("dend", [P, NU])
        gam = sb("gam", [P, T])
        sq = sb("sq", [P, 2, T])
        ss, rc, root = sb("ss", [P, 16]), sb("rc", [P, 16]), sb("root", [P, 16])
        bt = sb("bt", [P, NU, P])
        bm = sb("bm", [P, NLEV, NU, P], F16)
        tt = sb("tt", [P, 2, NU, P], F16)
        m1 = sb("m1", [P, NU, P], F16)
        t32 = sb("t32", [P, 4, P])
        r16 = sb("r16", [P, 4, P], F16)
        kqs = two("kqs", [P, 2, T])
        ktok = two("ktok", [P, NU, DK])
        vtok = two("vtok", [P, NU, DV])
        w1 = two("w1", [P, NU])
        s2 = two("s2", [P, NU])
        s2sq = two("s2sq", [P, NU])
        gend = two("gend", [P, CH])
        sg = two("sg", [P, 2, T])
        at = two("at", [P, NU, P])
        tinv = two("tinv", [P, NU, P])
        state = sb("state", [P, 2, DV])
        rr = sb("rr", [P, 2, DV])
        uu = sb("uu", [P, 2, DV])
        yy = sb("yy", [P, 2, P])
        sqo = sb("sqo", [P, 2, P])
        msq, rms = sb("msq", [P, 2]), sb("rms", [P, 2])

        ps_a, ps_b = bank("ps_a"), bank("ps_b")
        b0, b1, b2 = bank("b0"), bank("b1"), bank("b2")
        ck, cz, co = bank("ck"), bank("cz"), bank("co")
        halves = (b1, b2)

        def free(eng, users, name, i):
            k = users.index(name)
            if k:
                s.need(eng, i, users[k - 1])
            else:
                s.need(eng, i - 1, users[-1])

        A_USERS = [f"a_evac{j}" for j in range(4)]
        PB_USERS = ["b_ss", "b_sg0", "b_sg1", "b_ktok", "b_vtok0", "b_vtok1"]
        levels = [(l, g) for l in range(NLEV) for g in range(2)]
        B0_USERS = [f"b_Me{l}{g}" for l, g in levels] + [f"b_R{g}" for g in range(2)]
        BH_USERS = [[f"b_ev0{k}", f"b_ev1{k}", f"b_Tf{k}"] + [f"{n}{l}{k}" for l in range(NLEV) for n in ("b_Ue", "b_Te")]
                    + [f"b_T{k}"] for k in range(2)]
        CK_USERS = ["c_S0"] + [n for m in range(1, CH) for n in ([f"c_R{m}", f"c_m{m - 1}"]
                                                                 + ([f"c_S{m}"] if m < CH - 1 else []))]
        CK_USERS += [f"c_m{CH - 1}"]
        CZ_USERS = ["c_u0"] + [n for m in range(1, CH) for n in (f"c_u{m}", f"c_acc{m - 1}")] + [f"c_acc{CH - 1}"]
        CO_USERS = [f"c_y{k}" for k in range(CH)]
        for name in ("a_proj", "a_pad", "a_evac", "a_tanh", "a_silu"):
            s.series(name, [f"{name}{j}" for j in range(4)])
        s.series("a_tap", [f"a_tap{j}{r}" for j in range(4) for r in range(PAD)])
        for name in ("b_M", "b_Me", "b_U", "b_Ue", "b_bm"):
            s.series(name, [f"{name}{l}{g}" for l, g in levels])
        s.series("b_Tp", ["b_Tq0", "b_Tq1"] + [f"b_Tp{l}{g}" for l, g in levels])
        s.series("b_Te", ["b_Tf0", "b_Tf1"] + [f"b_Te{l}{g}" for l, g in levels])
        for name in ("b_vT", "b_vtok", "b_g", "b_tg", "b_sg", "b_diag", "b_t2", "b_P", "b_R", "b_F", "b_T"):
            s.series(name, [f"{name}{g}" for g in range(2)])
        for name in ("b_kk", "b_ev"):
            s.series(name, [f"{name}{g}{k}" for g in range(2) for k in range(2)])
        for name in ("c_KS", "c_R"):
            s.series(name, [f"{name}{m}" for m in range(1, CH)])
        for name in ("c_SU", "c_S"):
            s.series(name, [f"{name}{m}" for m in range(CH - 1)])
        for name in ("c_Z", "c_u", "c_O", "c_sq", "c_y", "c_ss", "c_out", "c_m", "c_me", "c_p", "c_r", "c_acch",
                     "c_acc"):
            s.series(name, [f"{name}{m}" for m in range(CH)])

        sp.dma_start(normw[:], norm_w).then_inc(s.sem("normw_in"), 16)

        def load_x(i, b, par):
            s.need(sp, i - 2, "b_g1")
            s.loaded(sp.dma_start(xin[par][:], xT_dram[bass.ds(b, 1)].rearrange("a p k t -> p (a k) t")),
                     f"xin_in{par}")

        def load_rows(i):
            s.need(sp, i - 1, "b_d", "b_dc", "b_gam")
            s.loaded(sp.dma_start(grow[:], g_dram[bass.ds(i * NU, NU), :].partition_broadcast(P)), "grow_in")

        def load_pair(hp):
            i = hp * NB
            s.need(sp, i - 1, "a_proj3", "a_tap32", "a_evac3")
            s.loaded(sp.dma_start(wq[:], w_qkv[bass.ds(hp, 1)].rearrange("a p n -> p (a n)")), "wqkv_in")
            load_x(i, 0, 0)
            s.need(sp, i - 1, "b_g1")
            s.loaded(sp.dma_start(wg[:], w_gate[bass.ds(hp, 1)].rearrange("a p k n -> p (a k) n")), "wg_in")
            load_rows(i)
            load_x(i + 1, 1, 1)
            load_rows(i + 1)
            s.need(sp, i - 1, f"c_out{CH - 1}")
            s.loaded(sp.dma_start(wo[:], w_out[bass.ds(hp, 1)].rearrange("a p h d -> p (a h) d")), "wo_in")
            with sp.Fori(2, NB, 2) as b:
                for par in range(2):
                    load_x(i + b + par, b + par, par)
                    load_rows(i + b + par)

        def stage_a(i, p):
            dest = [kq[p][:, 1, :], kq[p][:, 0, :], vch[p][:, 0, :], vch[p][:, 1, :]]
            hp = i // NB

            def project(j):
                yield f"a_proj{j}"
                if j == 0:
                    s.need_dma_of(pe, i, "xin_in", p)
                    s.need_dma(pe, hp, "wqkv_in")
                free(pe, A_USERS, f"a_evac{j}", i)
                for k in range(KT):
                    ins = pe.matmul(ps_a[:], wqkv[:, k, j * P:(j + 1) * P], xin[p][:, k, :], start=k == 0,
                                    stop=k == KT - 1)
                s.done(ins, f"a_proj{j}")
                yield f"a_evac{j}"
                if j == 0:
                    s.need_dma(act, hp, "wqkv_in")
                s.need(act, i if j > 1 else i - 1, f"a_silu{(j - 2) % 4}")
                s.need(act, i, f"a_proj{j}")
                s.done(act.copy(pad[j % 2][:, PAD:], ps_a[:]), f"a_pad{j}")
                s.done(act.activation(cv[j % 2][:], ps_a[:], ACT.Copy, scale=tap[:, j, TAPS - 1:TAPS]), f"a_evac{j}")
                for r in range(PAD):
                    yield f"a_tap{j}{r}"
                    if r == 0:
                        if j == 0:
                            s.need_dma(dve, hp, "wqkv_in")
                        s.need(dve, i, f"a_pad{j}", f"a_evac{j}")
                    else:
                        s.need(dve, i, f"a_tap{j}{r - 1}")
                    s.done(dve.scalar_tensor_tensor(cv[j % 2][:], pad[j % 2][:, r:r + T], tap[:, j, r:r + 1],
                                                    cv[j % 2][:], ALU.mult, ALU.add), f"a_tap{j}{r}")
                yield f"a_tanh{j}"
                s.need(act, i, f"a_tap{j}{PAD - 1}")
                s.need(act, i if j else i - 1, f"a_silu{(j - 1) % 4}")
                s.done(act.activation(th[:], cv[j % 2][:], ACT.Tanh, scale=0.5), f"a_tanh{j}")
                yield f"a_silu{j}"
                s.need(dve, i, f"a_tanh{j}")
                if j < 2:
                    s.need(dve, i - 2, "b_sq", "b_kqs", "b_kk11", "b_kT")
                else:
                    s.need(dve, i - 2, f"b_vT{j - 2}")
                s.done(dve.scalar_tensor_tensor(dest[j], th[:], 1.0, cv[j % 2][:], ALU.add, ALU.mult),
                       f"a_silu{j}")

            return [project(j) for j in range(4)]

        def stage_b(i, p):
            tok = lambda k: gate_tok[k][:, bass.ds(i * NU, NU)]
            col = lambda t, u: t[:, u:u + 1]
            units = lambda g: slice(4 * g, 4 * g + 4)
            in_units = lambda t: t[:].rearrange("p (u t) -> p u t", t=P)

            def norms():
                yield "b_sq"
                s.need(act, i, "a_silu0", "a_silu1")
                s.need(act, i - 1, "b_stat")
                s.done(act.activation(sq[:], kq[p][:], ACT.Square), "b_sq")
                yield "b_stat"
                s.need(pe, i, "b_sq")
                free(pe, PB_USERS, "b_ss", i)
                for n in range(2):
                    for m in range(CH):
                        o = n * NU + 2 * m
                        ins = pe.matmul(ps_b[:, o:o + 2], sq[:, n, m * P:(m + 1) * P], c["head_sel"][:], start=True,
                                        stop=True)
                s.done(ins, "b_stat")
                yield "b_ss"
                s.need(dve, i, "b_stat")
                s.need(dve, i - 1, "b_root")
                s.done(dve.tensor_scalar(ss[:], ps_b[:, 0:16], 4e-6, None, ALU.add), "b_ss")
                yield "b_w1"
                s.need(dve, i, "b_ss")
                s.done(dve.reciprocal(rc[:], ss[:]), "b_rc")
                s.need(dve, i, "b_rc")
                s.need(dve, i - 2, f"c_u{CH - 1}")
                s.done(dve.tensor_tensor(w1[p][:], rc[:, 0:NU], tok(1), ALU.mult), "b_w1")
                yield "b_root"
                s.need(pool, i, "b_ss")
                s.need(pool, i - 1, "b_s2", "b_vtok0", "b_vtok1")
                s.done(pool.tensor_tensor(root[:], ss[:], c["half"][:, 0:16], ALU.pow), "b_root")
                yield "b_s2"
                s.need(dve, i, "b_rc", "b_root")
                s.need(dve, i - 2, f"c_r{CH - 1}")
                s.done(dve.tensor_scalar(s2sq[p][:], rc[:, NU:], 1.0 / (256 * DV), None, ALU.mult), "b_s2sq")
                s.done(dve.scalar_tensor_tensor(s2[p][:], rc[:, NU:], 1.0 / 16, root[:, NU:], ALU.mult, ALU.mult),
                       "b_s2")

            def decays():
                yield "b_d"
                s.done(dve.tensor_copy(g_it[:], tok(0)), "b_git")
                s.need(dve, i, "b_git")
                s.need_dma(dve, i, "grow_in")
                s.done(dve.tensor_tensor(dend[:], grow[:, :, P - 1], g_it[:], ALU.subtract), "b_dc")
                s.done(dve.tensor_tensor(dec[:], grow[:], g_it[:].unsqueeze(2).broadcast_to([P, NU, P]), ALU.subtract),
                       "b_d")
                yield "b_sel"
                s.need(pool, i, "b_d")
                settle(pool, c["settle_pool"])
                s.done(pool.affine_select(out=dec[:], in_=dec[:], pattern=[[0, NU], [1, P]], compare_op=ALU.is_ge,
                                          fill=NEG, base=0, channel_multiplier=-1), "b_sel")
                yield "b_E"
                s.need(act, i, "b_dc")
                s.done(act.activation(dend[:], dend[:], ACT.Exp), "b_ed")
                s.need(act, i, "b_sel")
                s.done(act.activation(dec[:], dec[:], ACT.Exp), "b_E")

            def decayed_kq():
                yield "b_gam"
                s.need_dma(act, i, "grow_in")
                s.need(act, i - 1, "b_kqs", "b_gend")
                for h in range(2):
                    rows = slice(h * DK, (h + 1) * DK)
                    src = grow[rows].rearrange("p (c h) t -> p c h t", h=2)[:, :, h, :]
                    ins = act.activation(gam[rows, :].rearrange("p (c t) -> p c t", t=P), src, ACT.Exp)
                s.done(ins, "b_gam")
                yield "b_gend"
                s.need(dve, i, "b_gam")
                s.done(dve.tensor_copy(gend[p][:], gam[:].rearrange("p (c t) -> p c t", t=P)[:, :, P - 1]), "b_gend")
                yield "b_kqs"
                s.need(pool, i, "b_gam", "a_silu0", "a_silu1")
                s.need(pool, i - 2, f"c_O{CH - 1}")
                s.done(pool.tensor_tensor(kqs[p][:], kq[p][:], gam[:].unsqueeze(1).broadcast_to([P, 2, T]), ALU.mult),
                       "b_kqs")

            def gate(h):
                yield f"b_g{h}"
                free(pe, PB_USERS, f"b_sg{h}", i)
                if h == 0:
                    s.need_dma(pe, i // NB, "wg_in")
                for k in range(KT):
                    ins = pe.matmul(ps_b[:], wg[:, k, h * P:(h + 1) * P], xin[p][:, k, :], start=k == 0,
                                    stop=k == KT - 1)
                s.done(ins, f"b_g{h}")
                yield f"b_tg{h}"
                s.need(act, i, f"b_g{h}")
                s.need(act, i - 2, f"c_y{CH - 1}")
                s.done(act.activation(sg[p][:, h, :], ps_b[:], ACT.Tanh, scale=0.5), f"b_tg{h}")
                yield f"b_sg{h}"
                s.need(dve, i, f"b_tg{h}")
                s.done(dve.scalar_tensor_tensor(sg[p][:, h, :], sg[p][:, h, :], 1.0, ps_b[:], ALU.add, ALU.mult),
                       f"b_sg{h}")

            def turn_k():
                yield "b_kT"
                s.need(pe, i, "a_silu1")
                free(pe, PB_USERS, "b_ktok", i)
                for m in range(CH):
                    ins = pe.transpose(ps_b[:, m * P:(m + 1) * P], kq[p][:, 0, m * P:(m + 1) * P], c["ident"][:])
                s.done(ins, "b_kT")
                yield "b_ktok"
                s.need(dve, i, "b_kT", "b_ed")
                s.need(dve, i - 2, f"c_SU{CH - 2}")
                s.done(dve.tensor_tensor(ktok[p][:], ps_b[:].rearrange("p (u e) -> p u e", e=DK),
                                         dend[:].unsqueeze(2).broadcast_to([P, NU, DK]), ALU.mult), "b_ktok")

            def turn_v(h):
                yield f"b_vT{h}"
                s.need(pe, i, f"a_silu{2 + h}")
                free(pe, PB_USERS, f"b_vtok{h}", i)
                for m in range(CH):
                    ins = pe.transpose(ps_b[:, m * P:(m + 1) * P], vch[p][:, h, m * P:(m + 1) * P], c["ident"][:])
                s.done(ins, f"b_vT{h}")
                yield f"b_vtok{h}"
                s.need(dve, i, f"b_vT{h}", "b_root")
                s.need(dve, i - 2, f"c_Z{CH - 1}")
                scale = root[:, 0:NU].rearrange("p (c h) -> p c h", h=2)[:, :, h:h + 1].broadcast_to([P, CH, DV])
                s.done(dve.tensor_tensor(vtok[p][:].rearrange("p (c h) e -> p c h e", h=2)[:, :, h, :],
                                         ps_b[:].rearrange("p (c e) -> p c e", e=DV), scale, ALU.mult), f"b_vtok{h}")

            def products(g, k):
                users, ps, rows = BH_USERS[k], halves[k], slice(k * DK, (k + 1) * DK)
                yield f"b_kk{g}{k}"
                s.need(pe, i, "a_silu0", "a_silu1")
                free(pe, users, f"b_ev{g}{k}", i)
                for n in range(2):
                    t = slice((2 * g + n) * P, (2 * g + n + 1) * P)
                    ins = pe.matmul(ps[:, n * 2 * P:(n + 1) * 2 * P], kq[p][rows, 0, t], kq[p][rows, :, t],
                                    start=True, stop=True)
                s.done(ins, f"b_kk{g}{k}")
                yield f"b_ev{g}{k}"
                s.need(dve, i, f"b_kk{g}{k}", "b_E", "b_w1")
                s.need(dve, i - 1, f"b_P{g}", f"b_bm{NLEV - 1}{g}")
                for n in range(2):
                    u = 4 * g + 2 * n + k
                    dve.scalar_tensor_tensor(bt[:, u, :], ps[:, n * 2 * P:n * 2 * P + P], col(w1[p], u), dec[:, u, :],
                                             ALU.mult, ALU.mult)
                of_head = lambda t: t[:, 4 * g:4 * g + 4, :].rearrange("p (n h) t -> p n h t", h=2)[:, :, k, :]
                s.need(dve, i - 2, f"c_O{CH - 1}")
                s.done(dve.tensor_tensor(of_head(at[p]), ps[:].rearrange("p (n q t) -> p n q t", n=2, q=2)[:, :, 1, :],
                                         of_head(dec), ALU.mult), f"b_ev{g}{k}")

            def masks(g):
                yield f"b_diag{g}"
                s.need(pool, i, f"b_ev{g}0", f"b_ev{g}1")
                settle(pool, c["settle_pool"])
                s.done(pool.affine_select(out=bt[:, units(g), :], in_=bt[:, units(g), :], pattern=[[0, 4], [1, P]],
                                          compare_op=ALU.not_equal, fill=1.0, base=0, channel_multiplier=-1),
                       f"b_diag{g}")
                yield f"b_t2{g}"
                s.need(pool, i, f"b_diag{g}")
                s.need(pool, i - 1, f"b_T{g}")
                s.done(pool.tensor_tensor(tt[:, 1, units(g), :], bt[:, units(g), :],
                                          c["first"][:].unsqueeze(1).broadcast_to([P, 4, P]), ALU.mult), f"b_t2{g}")
                for l in range(NLEV):
                    yield f"b_bm{l}{g}"
                    s.need(pool, i - 1, f"b_M{l}{g}")
                    s.done(pool.tensor_tensor(bm[:, l, units(g), :], bt[:, units(g), :],
                                              c["mask"][:, l, :].unsqueeze(1).broadcast_to([P, 4, P]), ALU.mult),
                           f"b_bm{l}{g}")

            def invert(g):
                yield f"b_Tq{g}"
                s.need(pe, i, f"b_t2{g}", f"b_ev1{g}")
                turn_into(g, f"b_Tq{g}")
                yield f"b_Tf{g}"
                s.need(act, i, f"b_Tq{g}")
                evacuate_turn(g, f"b_Tf{g}", tt[:, 0, units(g), :])
                for l in range(NLEV):
                    last = l == NLEV - 1
                    yield f"b_M{l}{g}"
                    s.need(pe, i, f"b_bm{l}{g}", f"b_Te{l - 1}{g}" if l else f"b_Tf{g}")
                    free(pe, B0_USERS, f"b_Me{l}{g}", i)
                    for k in range(4):
                        ins = pe.matmul(b0[:, k * P:(k + 1) * P], bm[:, l, 4 * g + k, :], tt[:, 0, 4 * g + k, :],
                                        start=True, stop=True)
                    s.done(ins, f"b_M{l}{g}")
                    yield f"b_Me{l}{g}"
                    s.need(act, i, f"b_M{l}{g}")
                    s.done(act.mul(m1[:, units(g), :], in_units(b0), -1.0), f"b_Me{l}{g}")
                    yield f"b_U{l}{g}"
                    s.need(pe, i, f"b_Me{l}{g}")
                    for k in range(4):
                        u = 4 * g + k
                        ins = pe.matmul(halves[g][:, k * P:(k + 1) * P], m1[:, u, :], tt[:, 1, u, :], start=True,
                                        stop=True)
                    s.done(ins, f"b_U{l}{g}")
                    yield f"b_Ue{l}{g}"
                    s.need(dve, i, f"b_U{l}{g}")
                    s.done(dve.tensor_tensor(tt[:, 1, units(g), :], tt[:, 1, units(g), :], in_units(halves[g]),
                                             ALU.add), f"b_Ue{l}{g}")
                    yield f"b_Tp{l}{g}"
                    s.need(pe, i, f"b_Ue{l}{g}")
                    turn_into(g, f"b_Tp{l}{g}")
                    yield f"b_Te{l}{g}"
                    s.need(act, i, f"b_Tp{l}{g}")
                    if last:
                        s.need(act, i if g else i - 1, f"b_P{1 - g}")
                    evacuate_turn(g, f"b_Te{l}{g}", t32[:] if last else tt[:, 0, units(g), :])
                yield f"b_P{g}"
                s.need(pe, i, f"b_Te{NLEV - 1}{g}")
                free(pe, B0_USERS, f"b_R{g}", i)
                for k in range(4):
                    ins = pe.matmul(b0[:, k * P:(k + 1) * P], bt[:, 4 * g + k, :], t32[:, k, :], start=True, stop=True)
                s.done(ins, f"b_P{g}")
                yield f"b_R{g}"
                s.need(dve, i, f"b_P{g}")
                s.need(dve, i if g else i - 1, f"b_F{1 - g}")
                s.done(dve.tensor_tensor(r16[:], c["ident"][:].unsqueeze(1).broadcast_to([P, 4, P]), in_units(b0),
                                         ALU.subtract), f"b_R{g}")
                yield f"b_F{g}"
                s.need(pe, i, f"b_R{g}")
                for k in range(4):
                    ins = pe.matmul(halves[g][:, k * P:(k + 1) * P], r16[:, k, :], tt[:, 1, 4 * g + k, :], start=True,
                                    stop=True)
                s.done(ins, f"b_F{g}")
                yield f"b_T{g}"
                s.need(dve, i, f"b_F{g}")
                s.need(dve, i - 2, f"c_Z{CH - 1}")
                s.done(dve.tensor_tensor(tinv[p][:, units(g), :], tt[:, 1, units(g), :], in_units(halves[g]), ALU.add),
                       f"b_T{g}")

            def turn_into(g, name):
                ps = halves[g][:].bitcast(F16)
                for k in range(4):
                    ins = pe.transpose(ps[:, k * P:(k + 1) * P], tt[:, 1, 4 * g + k, :], c["ident16"][:])
                s.done(ins, name)

            def evacuate_turn(g, name, dst):
                s.done(act.copy(dst, halves[g][:].bitcast(F16)[:, 0:4 * P].rearrange("p (u t) -> p u t", t=P)), name)

            threads = [norms(), decays(), decayed_kq(), turn_k()]
            for g in range(2):
                threads += [gate(g), turn_v(g), products(g, 0), products(g, 1), masks(g), invert(g)]
            return threads

        def stage_c(i, p):
            def recur():
                for m in range(CH):
                    if m:
                        yield f"c_KS{m}"
                        s.need(pe, i, f"c_S{m - 1}", "b_kqs")
                        free(pe, CK_USERS, f"c_R{m}", i)
                        ins = pe.matmul(ck[:, 0:2 * DV], kqs[p][:, 0, m * P:(m + 1) * P],
                                        state[:].rearrange("p h e -> p (h e)"), start=True, stop=True)
                        s.done(ins, f"c_KS{m}")
                        yield f"c_R{m}"
                        s.need(dve, i, f"c_KS{m}", "b_vtok0", "b_vtok1")
                        s.done(dve.tensor_tensor(rr[:], vtok[p][:, 2 * m:2 * m + 2, :],
                                                 ck[:, 0:2 * DV].rearrange("p (h e) -> p h e", h=2), ALU.subtract),
                               f"c_R{m}")
                    yield f"c_Z{m}"
                    if m == 0:
                        s.need(pe, i, "b_T0", "b_vtok0", "b_vtok1")
                    else:
                        s.need(pe, i, f"c_R{m}", f"b_T{m // 2}")
                    free(pe, CZ_USERS, f"c_u{m}", i)
                    for h in range(2):
                        rhs = rr[:, h, :] if m else vtok[p][:, h, :]
                        ins = pe.matmul(cz[:, h * DV:(h + 1) * DV], tinv[p][:, 2 * m + h, :], rhs, start=True,
                                        stop=True)
                    s.done(ins, f"c_Z{m}")
                    yield f"c_u{m}"
                    s.need(act, i, f"c_Z{m}", "b_w1")
                    if m:
                        s.need(act, i, f"c_O{m - 1}")
                    else:
                        s.need(act, i - 1, f"c_O{CH - 1}")
                    for h in range(2):
                        ins = act.activation(uu[:, h, :], cz[:, h * DV:(h + 1) * DV], ACT.Copy,
                                             scale=w1[p][:, 2 * m + h:2 * m + h + 1])
                    s.done(ins, f"c_u{m}")
                    if m < CH - 1:
                        yield f"c_SU{m}"
                        s.need(pe, i, f"c_u{m}", "b_ktok")
                        free(pe, CK_USERS, f"c_S{m}", i)
                        for h in range(2):
                            ins = pe.matmul(ck[h * DK:(h + 1) * DK, 2 * DV:3 * DV], ktok[p][:, 2 * m + h, :],
                                            uu[:, h, :], start=True, stop=True)
                        s.done(ins, f"c_SU{m}")
                    yield f"c_O{m}"
                    s.need(pe, i, f"c_u{m}", "b_ktok", "b_kqs", f"b_ev{m // 2}1")
                    free(pe, CO_USERS, f"c_y{m}", i)
                    for h in range(2):
                        if m:
                            pe.matmul(co[:, h * P:(h + 1) * P], state[:, h, :], kqs[p][:, 1, m * P:(m + 1) * P],
                                      start=True, stop=False)
                        ins = pe.matmul(co[:, h * P:(h + 1) * P], uu[:, h, :], at[p][:, 2 * m + h, :], start=m == 0,
                                        stop=True)
                    s.done(ins, f"c_O{m}")
                    if m < CH - 1:
                        yield f"c_S{m}"
                        s.need(dve, i, f"c_SU{m}", f"c_O{m}", "b_gend")
                        for h in range(2):
                            rows = slice(h * DK, (h + 1) * DK)
                            if m == 0:
                                ins = dve.tensor_copy(state[rows, h, :], ck[rows, 2 * DV:3 * DV])
                            else:
                                ins = dve.scalar_tensor_tensor(state[rows, h, :], state[rows, h, :],
                                                               gend[p][rows, m:m + 1], ck[rows, 2 * DV:3 * DV],
                                                               ALU.mult, ALU.add)
                        s.done(ins, f"c_S{m}")

            def emit(m):
                yield f"c_sq{m}"
                s.need(act, i, f"c_O{m}")
                if m:
                    s.need(act, i, f"c_ss{m - 1}")
                else:
                    s.need(act, i - 1, f"c_ss{CH - 1}")
                s.done(act.activation(sqo[:], co[:, 0:2 * P].rearrange("p (h t) -> p h t", h=2), ACT.Square),
                       f"c_sq{m}")
                yield f"c_y{m}"
                s.need(dve, i, f"c_sq{m}", "b_sg0", "b_sg1")
                if m:
                    s.need(dve, i, f"c_out{m - 1}")
                else:
                    s.need(dve, i - 1, f"c_out{CH - 1}")
                s.done(dve.scalar_tensor_tensor(yy[:], co[:, 0:2 * P].rearrange("p (h t) -> p h t", h=2),
                                                normw[:, 0:1], sg[p][:, :, m * P:(m + 1) * P], ALU.mult, ALU.mult),
                       f"c_y{m}")
                yield f"c_ss{m}"
                s.need(pe, i, f"c_sq{m}")
                free(pe, CK_USERS, f"c_m{m}", i)
                for h in range(2):
                    ins = pe.matmul(ck[:, 3 * DV + h:3 * DV + h + 1], sqo[:, h, :], c["ones_col"][:], start=True,
                                    stop=True)
                s.done(ins, f"c_ss{m}")
                yield f"c_m{m}"
                s.need(dve, i, f"c_ss{m}", "b_s2sq", "b_s2")
                if m:
                    s.need(dve, i, f"c_r{m - 1}")
                else:
                    s.need(dve, i - 1, f"c_r{CH - 1}")
                s.done(dve.tensor_tensor(msq[:], ck[:, 3 * DV:3 * DV + 2], s2sq[p][:, 2 * m:2 * m + 2], ALU.mult),
                       f"c_m{m}")
                yield f"c_me{m}"
                s.need(dve, i, f"c_m{m}")
                s.done(dve.tensor_scalar(msq[:], msq[:], LN_EPS, None, ALU.add), f"c_me{m}")
                yield f"c_p{m}"
                s.need(pool, i, f"c_me{m}")
                if m:
                    s.need(pool, i, f"c_acc{m - 1}")
                else:
                    s.need(pool, i - 1, f"c_acc{CH - 1}")
                s.done(pool.tensor_tensor(rms[:], msq[:], c["minus_half"][:, 0:2], ALU.pow), f"c_p{m}")
                s.need(pool, i, f"c_p{m}")
                s.done(pool.tensor_tensor(rms[:], rms[:], s2[p][:, 2 * m:2 * m + 2], ALU.mult), f"c_r{m}")
                yield f"c_out{m}"
                s.need(pe, i, f"c_y{m}")
                if m == 0:
                    s.need_dma(pe, i // NB, "wo_in")
                free(pe, CZ_USERS, f"c_acc{m}", i)
                for h in range(2):
                    ins = pe.matmul(cz[:, h * D:(h + 1) * D], yy[:, h, :], wo[:, h, :], start=True, stop=True)
                s.done(ins, f"c_out{m}")
                yield f"c_acch{m}"
                s.need(dve, i, f"c_out{m}", f"c_r{m}")
                a = acc[:, bass.ds((i % NB) * CH + m, 1), :].rearrange("p a d -> p (a d)")
                s.done(dve.scalar_tensor_tensor(a, cz[:, 0:D], rms[:, 0:1], a, ALU.mult, ALU.add), f"c_acch{m}")
                yield f"c_acc{m}"
                s.need(dve, i, f"c_acch{m}")
                s.done(dve.scalar_tensor_tensor(a, cz[:, D:2 * D], rms[:, 1:2], a, ALU.mult, ALU.add), f"c_acc{m}")

            return [recur()] + [emit(m) for m in range(CH)]

        def body(t, par):
            threads = []
            if active(t, NIT):
                threads += stage_a(t, par)
            if active(t - 1, NIT):
                threads += stage_b(t - 1, 1 - par)
            if active(t - 2, NIT):
                threads += stage_c(t - 2, par)
            issue(SLOT_ORDER, threads)

        for p in range(2):
            ins = pool.memset(pad[p][:, 0:PAD], 0.0)
        ins.then_inc(s.sem("pad_zero"), 1)
        dve.wait_ge(s.sem("pad_zero"), 1)
        dve.memset(state[:], 0.0).then_inc(s.sem("state_zero"), 1)
        pe.wait_ge(s.sem("state_zero"), 1)
        dve.memset(acc[:], 0.0).then_inc(s.sem("acc_zero"), 1)
        dve.wait_ge(s.sem("acc_zero"), 1)
        dve.wait_ge(s.sem("normw_in"), 16)
        dve.tensor_scalar(normw[:], normw[:], 0.5, None, ALU.mult).then_inc(s.sem("normw_half"), 1)
        dve.wait_ge(s.sem("normw_half"), 1)
        load_pair(0)
        with sp.Fori(1, NP) as hp:
            load_pair(hp)
        in_slots(nc, NIT, 2, 4, COMPUTE, body)
        ctx.finish()


def build(nc, a, out):
    with ExitStack() as ctx:
        sb = lambda name, shape, dt=F32: ctx.enter_context(nc.sbuf_tensor(name, shape, dt))
        xT_dram = nc.dram_tensor("xT_scratch", [NB + 1, P, KT, T], F32).ap()
        g_dram = nc.dram_tensor("g_scratch", [(NIT + 1) * NU, P], F32).ap()
        acc = sb("acc", [P, NTILE, D])
        c, s_const, n_const = make_constants(nc, ctx, sb)
        for eng in (nc.tensor, nc.vector, nc.scalar):
            eng.wait_ge(s_const, n_const)
        with ExitStack() as gates:
            gate_tok = [gates.enter_context(nc.sbuf_tensor(f"gate_tok{k}", [P, NIT * NU + NU], F32)) for k in range(2)]
            phase_norm(nc, c, a["x"], a["w_ab"], xT_dram, [g[:, 0:NIT * NU] for g in gate_tok])
            phase_gates(nc, c, a["A_log"], a["dt_bias"], [g[:, 0:NIT * NU] for g in gate_tok], g_dram)
            phase_delta(nc, c, a["w_qkv"], a["w_gate"], a["w_out"], None, a["norm_w"], xT_dram, g_dram, gate_tok, acc)
        phase_experts(nc, c, a, acc, out)


def phase_experts(nc, c, a, acc, out):
    with Phase(nc) as ctx:
        sb = lambda name, shape, dt=F32: ctx.enter_context(nc.sbuf_tensor(name, shape, dt))
        two = lambda name, shape, dt=F32: [sb(f"{name}{p}", shape, dt) for p in range(2)]
        bank = lambda name: ctx.enter_context(nc.psum_tensor(name, [P, 512], F32))
        pe, act, dve, pool, sp = nc.tensor, nc.scalar, nc.vector, nc.gpsimd, nc.sync
        s = Steps(nc, ctx)
        NR = E + E * PP
        wv = sb("e_wv", [P, KT, D])
        wr = sb("e_wr", [P, KT, NR])
        w1 = sb("e_w1", [P, KT, E * INNER])
        w2 = sb("e_w2", [P, KT, D])
        b2v = sb("e_b2v", [E + 1, D])
        bvc = sb("e_bvc", [P, KT])
        b1c = sb("e_b1c", [P, KT])
        b1h = sb("e_b1h", [P, KT])
        spread = sb("e_spread", [E, E * INNER])
        rows = sb("e_rows", [P, 5, E])
        alpha = sb("e_alpha", [P, 1])
        expert = sb("e_expert", [P, CH, E])
        x_in = two("e_x", [P, CH, D])
        x1 = two("e_x1_", [P, CH, D])
        xT = two("e_xT", [P, KT, T])
        xf = sb("e_xf", [P, CH, D])
        stats, mv, rstd = sb("e_stats", [P, CH, 6]), sb("e_mv", [P, CH, 2]), sb("e_rstd", [P, CH])
        o_stats, o_mv, o_rstd = sb("e_ostats", [P, CH, 6]), sb("e_omv", [P, CH, 2]), sb("e_orstd", [P, CH])
        vT = sb("e_vT", [P, KT, T])
        rc = sb("e_rc", [P, 2, CH, E])
        pv2 = sb("e_pv2", [P, CH, E, PP])
        c2 = sb("e_c2", [P, CH, E])
        mean, cen2 = sb("e_mean", [P, 2 * CH]), sb("e_cen2", [P, 2 * CH, E])
        var = sb("e_var", [P, 2 * CH])
        score = sb("e_score", [P, CH, E])
        top, idx = sb("e_top", [P, CH, 8]), sb("e_idx", [P, CH, 8], U32)
        idxf = sb("e_idxf", [P, CH, 8])
        gap, e2 = sb("e_gap", [P, CH]), sb("e_e2", [P, CH])
        share = sb("e_share", [P, CH, 2])
        hot = sb("e_hot", [P, 2, CH, E])
        we = sb("e_we", [P, CH, E + 1])
        weT = sb("e_weT", [E + 1, T])
        hz, hth, hw = sb("e_hz", [P, KT, T]), sb("e_hth", [P, KT, T]), sb("e_hw", [P, KT, T])
        yo = two("e_yo", [P, CH, D])
        turn = [bank(f"e_turn{k}") for k in range(KT)]
        vb = [bank(f"e_vb{k}") for k in range(KT)]
        rb, wb = bank("e_rb"), bank("e_wb")
        ob = [bank(f"e_ob{k}") for k in range(2)]

        s_w = ctx.semaphore("e_w_in")
        loads = [(wv[:], a["Wv"]), (wr[:], a["Wr"]), (w1[:], a["W1"]), (w2[:], a["W2"]), (b2v[:], a["b2v"]),
                 (bvc[:], a["bv"]), (b1c[:], a["b1"]), (rows[:], a["router_rows"].partition_broadcast(P)),
                 (alpha[:], a["alpha"].partition_broadcast(P))]
        for dst, src in loads:
            sp.dma_start(dst, src).then_inc(s_w, 16)
        s_k = ctx.semaphore("e_const")
        nk = [0]

        def build_step(ins):
            ins.then_inc(s_k, 1)
            nk[0] += 1
            pool.wait_ge(s_k, nk[0])

        build_step(pool.memset(spread[:], 0.5))
        build_step(pool.affine_select(out=spread[:], in_=spread[:], pattern=[[1, E * INNER]], compare_op=ALU.is_ge,
                                      fill=0.0, base=0, channel_multiplier=-INNER))
        build_step(pool.affine_select(out=spread[:], in_=spread[:], pattern=[[-1, E * INNER]], compare_op=ALU.is_ge,
                                      fill=0.0, base=INNER - 1, channel_multiplier=INNER))
        build_step(pool.iota(expert[:].bitcast(mybir.dt.int32), pattern=[[0, CH], [1, E]], base=0,
                             channel_multiplier=0))
        build_step(pool.tensor_copy(expert[:], expert[:].bitcast(mybir.dt.int32)))
        build_step(pool.memset(we[:, :, E:E + 1], 1.0))
        for eng in (pe, act, dve, pool):
            eng.wait_ge(s_w, 16 * len(loads))
            eng.wait_ge(s_k, nk[0])
        s_0 = ctx.semaphore("e_alpha_done")
        act.activation(alpha[:], alpha[:], ACT.Tanh, scale=0.5).then_inc(s_0, 1)
        act.mul(b1h[:], b1c[:], 0.5).then_inc(s_0, 1)
        act.wait_ge(s_0, 2)
        dve.wait_ge(s_0, 2)
        dve.tensor_scalar(alpha[:], alpha[:], 1.0, 0.5, ALU.add, ALU.mult).then_inc(s_0, 1)
        dve.wait_ge(s_0, 3)
        dve.tensor_scalar(rows[:, 2, :], rows[:, 2, :], alpha[:, 0:1], None, ALU.mult).then_inc(s_0, 1)
        dve.tensor_scalar(rows[:, 4, :], rows[:, 4, :], alpha[:, 0:1], None, ALU.mult).then_inc(s_0, 1)
        dve.wait_ge(s_0, 5)

        def chained(eng, i, name, ins):
            s.done(ins, name)
            s.need(eng, i, name)

        def norm_x(i, p):
            s.need(sp, i - 2, "x_x1")
            s.loaded(sp.dma_start(x_in[p][:], a["x"][bass.ds(i, 1)].rearrange("a p c d -> p (a c) d")),
                     f"x_in{p}")
            tiles = acc[:, bass.ds(i * CH, CH), :]
            for half in range(2):
                src = tiles if half == 0 else x1[p][:]
                for k in range(CH):
                    ins = dve.bn_stats(stats[:, k, :], src[:, k, :])
                chained(dve, i, f"x_bn{half}", ins)
                settle(dve, c["settle_dve"])
                for k in range(CH):
                    ins = dve.bn_aggr(mv[:, k, :], stats[:, k, :])
                chained(dve, i, f"x_mv{half}", ins)
                s.done(dve.tensor_scalar(rstd[:], mv[:, :, 1], LN_EPS, None, ALU.add), f"x_ve{half}")
                s.need(pool, i, f"x_ve{half}")
                s.done(pool.tensor_tensor(rstd[:], rstd[:], c["minus_half"][:, 0:CH], ALU.pow), f"x_rs{half}")
                s.need(dve, i, f"x_rs{half}")
                if half:
                    s.need(dve, i - 1, "x_turn")
                for k in range(CH):
                    ins = dve.tensor_scalar(xf[:, k, :] if half else tiles[:, k, :], src[:, k, :], mv[:, k, 0:1],
                                            rstd[:, k:k + 1], ALU.subtract, ALU.mult)
                if half == 0:
                    chained(dve, i, "x_y1", ins)
                    s.need_dma_of(dve, i, "x_in", p)
                    s.need(dve, i - 2, "o_sum")
                    chained(dve, i, "x_x1", dve.tensor_tensor(x1[p][:], tiles, x_in[p][:], ALU.add))
                else:
                    s.done(ins, "x_xf")
            s.need(pe, i, "x_xf")
            s.need(pe, i - 1, "x_xT")
            for k in range(KT):
                for m in range(CH):
                    ins = pe.transpose(turn[k][:, m * P:(m + 1) * P], xf[:, m, k * P:(k + 1) * P], c["ident"][:])
            s.done(ins, "x_turn")
            s.need(act, i, "x_turn")
            s.need(act, i - 2, "o_out1")
            for k in range(KT):
                ins = act.copy(xT[p][:, k, :], turn[k][:])
            s.done(ins, "x_xT")

        def experts(i, p):
            s.need(pe, i, "x_xT")
            s.need(pe, i - 1, "h_th1", "h_z1")
            for m in range(KT):
                for k in range(KT):
                    ins = pe.matmul(vb[m][:], wv[:, k, m * P:(m + 1) * P], xT[p][:, k, :], start=k == 0,
                                    stop=k == KT - 1)
            s.done(ins, "v_mm")
            s.need(act, i, "v_mm")
            s.need(act, i - 1, "h_mm1", "r_mm")
            for m in range(KT):
                ins = act.activation(vT[:, m, :], vb[m][:], ACT.Identity, bias=bvc[:, m:m + 1])
            s.done(ins, "v_T")
            s.need(pe, i, "v_T")
            s.need(pe, i - 1, "r_sq", "r_s")
            for m in range(CH):
                for k in range(KT):
                    ins = pe.matmul(rb[:, m * P:m * P + NR], vT[:, k, m * P:(m + 1) * P], wr[:, k, :], start=k == 0,
                                    stop=k == KT - 1)
            s.done(ins, "r_mm")
            for m in range(KT):
                for k in range(KT):
                    ins = pe.matmul(vb[m][:], w1[:, k, m * P:(m + 1) * P], vT[:, k, :], start=k == 0,
                                    stop=k == KT - 1)
                s.done(ins, f"h_mm{m}")
            r = rb[:].rearrange("p (c n) -> p c n", c=CH)
            s.need(act, i, "r_mm")
            s.need(act, i - 1, "r_c2")
            s.done(act.activation(pv2[:].rearrange("p c e n -> p c (e n)"), r[:, :, E:NR], ACT.Square), "r_sq")
            s.need(act, i - 1, "h_s1")
            for m in range(KT):
                s.need(act, i, f"h_mm{m}")
                s.done(act.activation(hth[:, m, :], vb[m][:], ACT.Tanh, bias=b1h[:, m:m + 1], scale=0.5), f"h_th{m}")
                s.done(act.activation(hz[:, m, :], vb[m][:], ACT.Identity, bias=b1c[:, m:m + 1]), f"h_z{m}")
            s.need(dve, i, "r_sq")
            s.need(dve, i - 1, "r_score")
            s.done(dve.tensor_tensor(rc[:, 0], r[:, :, 0:E], rows[:, 0, :].unsqueeze(1).broadcast_to([P, CH, E]),
                                     ALU.add), "r_s")
            s.need(dve, i - 1, "r_cn")
            s.done(dve.tensor_reduce(c2[:], pv2[:], AX.X, ALU.add), "r_c2")
            s.need(dve, i, "r_c2")
            s.done(dve.tensor_scalar(c2[:], c2[:], 1.0 / PP, None, ALU.mult), "r_c3")
            s.need(pool, i, "r_c3")
            s.need(pool, i - 1, "r_score")
            s.done(pool.tensor_tensor(rc[:, 1], c2[:], c["half"][:].unsqueeze(1)[:, :, 0:E].broadcast_to([P, CH, E]),
                                      ALU.pow), "r_cn")
            for m in range(KT):
                s.need(dve, i, f"h_z{m}", f"h_th{m}")
                s.need(dve, i - 1, "o_out1")
                s.done(dve.scalar_tensor_tensor(hw[:, m, :], hth[:, m, :], 1.0, hz[:, m, :], ALU.add, ALU.mult),
                       f"h_s{m}")
            flat = rc[:].rearrange("p n c e -> p (n c) e")
            along = lambda t: t[:].unsqueeze(2).broadcast_to([P, 2 * CH, E])
            per_kind = lambda k: rows[:, k:k + 2, :].unsqueeze(2).broadcast_to([P, 2, CH, E])
            s.need(dve, i, "r_cn", "r_s")
            chained(dve, i, "r_sum", dve.tensor_reduce(mean[:], flat, AX.X, ALU.add))
            chained(dve, i, "r_mean", dve.tensor_scalar(mean[:], mean[:], 1.0 / E, None, ALU.mult))
            chained(dve, i, "r_cen", dve.tensor_tensor(flat, flat, along(mean), ALU.subtract))
            chained(dve, i, "r_cen2", dve.tensor_tensor(cen2[:], flat, flat, ALU.mult))
            chained(dve, i, "r_var", dve.tensor_reduce(var[:], cen2[:], AX.X, ALU.add))
            s.done(dve.tensor_scalar(var[:], var[:], 1.0 / E, LN_EPS, ALU.mult, ALU.add), "r_vare")
            s.need(pool, i, "r_vare")
            s.done(pool.tensor_tensor(var[:], var[:], c["minus_half"][:, 0:2 * CH], ALU.pow), "r_rstd")
            s.need(dve, i, "r_rstd")
            chained(dve, i, "r_n0", dve.tensor_tensor(flat, flat, along(var), ALU.mult))
            chained(dve, i, "r_n1", dve.tensor_tensor(rc[:], rc[:], per_kind(1), ALU.mult))
            chained(dve, i, "r_n2", dve.tensor_tensor(rc[:], rc[:], per_kind(3), ALU.add))
            chained(dve, i, "r_score", dve.tensor_tensor(score[:], rc[:, 0], rc[:, 1], ALU.add))
            settle(dve, c["settle_dve"])
            for m in range(CH):
                ins = dve.max(top[:, m, :], score[:, m, :])
            chained(dve, i, "t_max", ins)
            settle(dve, c["settle_dve"])
            for m in range(CH):
                ins = dve.max_index(idx[:, m, :], top[:, m, :], score[:, m, :])
            chained(dve, i, "t_idx", ins)
            s.need(dve, i - 1, "t_e2")
            s.done(dve.tensor_tensor(gap[:], top[:, :, 1], top[:, :, 0], ALU.subtract), "t_gap")
            chained(dve, i, "t_idxf", dve.tensor_copy(idxf[:], idx[:]))
            s.need(act, i, "t_gap")
            s.need(act, i - 1, "t_sh1")
            s.done(act.activation(e2[:], gap[:], ACT.Exp), "t_e2")
            for k in range(2):
                ins = dve.tensor_tensor(hot[:, k], expert[:], idxf[:, :, k:k + 1].broadcast_to([P, CH, E]),
                                        ALU.is_equal)
            s.done(ins, "t_hot")
            s.need(dve, i, "t_e2")
            chained(dve, i, "t_den", dve.tensor_scalar(share[:, :, 0], e2[:], 1.0, None, ALU.add))
            chained(dve, i, "t_sh0", dve.reciprocal(share[:, :, 0], share[:, :, 0]))
            s.done(dve.tensor_tensor(share[:, :, 1], share[:, :, 0], e2[:], ALU.mult), "t_sh1")
            s.need(dve, i, "t_hot", "t_sh1")
            for k in range(2):
                ins = dve.tensor_tensor(hot[:, k], hot[:, k], share[:, :, k:k + 1].broadcast_to([P, CH, E]), ALU.mult)
            chained(dve, i, "t_w", ins)
            s.need(dve, i - 1, "w_turn")
            s.done(dve.tensor_tensor(we[:, :, 0:E], hot[:, 0], hot[:, 1], ALU.add), "t_we")
            s.need(pe, i, "t_we")
            s.need(pe, i - 1, "w_hw1")
            for m in range(CH):
                ins = pe.transpose(wb[0:E + 1, m * P:(m + 1) * P], we[:, m, :], c["ident"][:])
            s.done(ins, "w_turn")
            s.need(act, i, "w_turn")
            s.need(act, i - 1, "o_out1")
            s.done(act.copy(weT[:], wb[0:E + 1, :]), "w_T")
            for m in range(KT):
                s.need(pe, i, "w_T" if m == 0 else "w_hw0")
                s.done(pe.matmul(wb[:], spread[:, m * P:(m + 1) * P], weT[0:E, :], start=True, stop=True), f"w_mm{m}")
                s.need(dve, i, f"w_mm{m}", f"h_s{m}")
                s.done(dve.tensor_tensor(hw[:, m, :], hw[:, m, :], wb[:], ALU.mult), f"w_hw{m}")
            for half in range(2):
                s.need(pe, i, "w_hw1", "w_T")
                s.need(pe, i - 1, f"o_n{half}")
                for m in (2 * half, 2 * half + 1):
                    o = ob[half][:, (m % 2) * D:(m % 2 + 1) * D]
                    tok = slice(m * P, (m + 1) * P)
                    for k in range(KT):
                        pe.matmul(o, xT[p][:, k, tok], wv[:, k, :], start=k == 0, stop=False)
                    for k in range(KT):
                        pe.matmul(o, hw[:, k, tok], w2[:, k, :], start=False, stop=False)
                    ins = pe.matmul(o, weT[:, tok], b2v[:], start=False, stop=True)
                s.done(ins, f"o_out{half}")
            for half in range(2):
                s.need(dve, i, f"o_out{half}")
                for m in (2 * half, 2 * half + 1):
                    ins = dve.bn_stats(o_stats[:, m, :], ob[half][:, (m % 2) * D:(m % 2 + 1) * D])
            chained(dve, i, "o_bn", ins)
            settle(dve, c["settle_dve"])
            for m in range(CH):
                ins = dve.bn_aggr(o_mv[:, m, :], o_stats[:, m, :])
            chained(dve, i, "o_mv", ins)
            s.done(dve.tensor_scalar(o_rstd[:], o_mv[:, :, 1], LN_EPS, None, ALU.add), "o_ve")
            s.need(pool, i, "o_ve")
            s.done(pool.tensor_tensor(o_rstd[:], o_rstd[:], c["minus_half"][:, 0:CH], ALU.pow), "o_rs")
            s.need(dve, i, "o_rs")
            s.need_dma_of(dve, i - 2, "y_out", p)
            for half in range(2):
                for m in (2 * half, 2 * half + 1):
                    ins = dve.tensor_scalar(yo[p][:, m, :], ob[half][:, (m % 2) * D:(m % 2 + 1) * D],
                                            o_mv[:, m, 0:1], o_rstd[:, m:m + 1], ALU.subtract, ALU.mult)
                s.done(ins, f"o_n{half}")
            s.need(dve, i, "o_n1")
            s.done(dve.tensor_tensor(yo[p][:], yo[p][:], x1[p][:], ALU.add), "o_sum")
            s.need(sp, i, "o_sum")
            s.loaded(sp.dma_start(out[bass.ds(i, 1)].rearrange("a p c d -> p (a c) d"), yo[p][:]),
                     f"y_out{p}")

        def body(t, par):
            if active(t, NB):
                norm_x(t, par)
            if active(t - 1, NB):
                experts(t - 1, 1 - par)

        in_slots(nc, NB, 1, 3, EVERY, body)
        for p in range(2):
            sp.wait_ge(s.sem(f"y_out{p}"), 16 * NB // 2)


def kernel(**inputs):
    import numpy as np
    import concourse.bacc as bacc
    from concourse.bass_utils import run_bass_kernel_spmd

    v = {k: np.asarray(x) for k, x in inputs.items()}
    at = lambda name: v["L0_attn_" + name]
    ff = lambda name: v["L0_ffn_" + name]
    rows = lambda w: w.reshape(KT, P, -1).transpose(1, 0, 2)
    by_pair = lambda w, n: rows(w).reshape(P, KT, NP, n).transpose(2, 0, 1, 3)
    tap_of = lambda w, n: w.reshape(NP, n, P, TAPS).transpose(0, 2, 1, 3)
    wqkv = np.concatenate([by_pair(at("w_q"), P), by_pair(at("w_k"), P), by_pair(at("w_v"), 2 * P)], axis=3)
    taps = np.concatenate([tap_of(at("conv_q"), 1), tap_of(at("conv_k"), 1), tap_of(at("conv_v"), 2)], axis=2)
    arrays = {
        "x": at("x").reshape(NB, CH, P, D).transpose(0, 2, 1, 3),
        "w_ab": rows(np.concatenate([at("w_a"), at("w_b")], axis=1)),
        "A_log": at("A_log"),
        "dt_bias": at("dt_bias"),
        "w_qkv": np.concatenate([wqkv.reshape(NP, P, -1), taps.reshape(NP, P, -1)], axis=2),
        "w_gate": by_pair(at("w_g"), 2 * P),
        "w_out": at("w_out").reshape(NP, 2, P, D).transpose(0, 2, 1, 3),
        "norm_w": at("norm_w").reshape(P, 1),
        "Wv": rows(ff("Wv").T),
        "Wr": rows(np.concatenate([ff("Wg").T, ff("Wp").reshape(E * PP, D).T], axis=1)),
        "W1": rows(ff("W1").reshape(E * INNER, D).T),
        "W2": rows(ff("W2").transpose(0, 2, 1).reshape(E * INNER, D)),
        "b2v": np.concatenate([ff("b2"), ff("bv")[None]], axis=0),
        "bv": ff("bv").reshape(KT, P).T,
        "b1": ff("b1").reshape(KT, P).T,
        "router_rows": np.stack([ff("bg"), ff("g_r"), ff("g_c"), ff("b_r"), ff("b_c")]),
        "alpha": ff("alpha").reshape(1),
    }
    nc = bacc.Bacc("TRN2", target_bir_lowering=False, num_devices=1)
    arrays = {k: np.ascontiguousarray(x) for k, x in arrays.items()}
    aps = {k: nc.dram_tensor("in_" + k, x.shape, mybir.dt.from_np(x.dtype), kind="ExternalInput").ap()
           for k, x in arrays.items()}
    out = nc.dram_tensor("out_y", (NB, P, CH, D), F32, kind="ExternalOutput").ap()
    build(nc, aps, out)
    r = run_bass_kernel_spmd(nc, [{"in_" + k: x for k, x in arrays.items()}], core_ids=[0])
    y = r.results[0]["out_y"]
    return y.transpose(0, 2, 1, 3).reshape(NB, T, D)
```

```python
from contextlib import ExitStack

import concourse.bass as bass
from concourse import mybir

ALU = mybir.AluOpType
ACT = mybir.ActivationFunctionType
AX = mybir.AxisListType
F32 = mybir.dt.float32
F16 = mybir.dt.float16
U32 = mybir.dt.uint32

P = 128
D = 256
KT = D // P
NB, T = 16, 512
H, DK, DV = 16, 64, 128
NP = H // 2
NIT = NP * NB
CH = T // P
NU = 2 * CH
TAPS = 4
PAD = TAPS - 1
NLEV = 6
NTILE = NB * CH
E, INNER, PP = 8, 32, 8
COMPUTE = (mybir.EngineType.PE, mybir.EngineType.Activation, mybir.EngineType.DVE, mybir.EngineType.Pool)
EVERY = COMPUTE + (mybir.EngineType.SP,)
NEG = -1.0e30
LN_EPS = 1e-5
N_QKV = 2 * P + 2 * P


SLOT_ORDER = """
    a_proj0 b_kk00 a_evac0 b_kk01 b_ev00 c_Z0 b_ev01 b_diag0 b_t20 c_u0 b_bm00 b_g0 b_kk10 b_gam a_tap00 b_kk11
    c_SU0 b_tg0 c_O0 b_ev10 b_ev11 c_S0 b_Tq0 b_hi0 b_Tf0 a_tap01 a_proj1 b_diag1 b_t21 c_sq0 c_KS1 b_M00 b_Tq1
    b_sg0 c_y0 b_hi1 a_evac1 a_tap02 b_Me00 b_g1 b_Tf1 b_U00 b_bm01 b_M01 b_git c_R1 b_bm10 b_bm11 a_tap10
    a_tanh0 b_Ue00 a_tap11 c_Z1 b_Tp00 b_Me01 c_ss0 b_Te00 b_lo0 c_m0 b_U01 b_M10 a_silu0 b_bm20 a_proj2 b_bm21
    b_tg1 b_Me10 b_Ue01 b_Tp01 a_tap12 b_sel b_bm30 c_me0 b_sg1 b_U10 c_u1 b_Ue10 c_SU1 a_tanh1 c_O1 b_Te01
    b_M11 a_silu1 c_p0 b_Tp10 a_evac2 c_S1 b_bm31 c_sq1 b_Me11 b_Te10 a_tap20 b_bm40 b_lo1 c_out0 b_U11 b_Ue11
    b_vT0 c_acch0 b_E b_M20 a_proj3 b_Tp11 b_vtok0 b_Me20 b_Te11 c_KS2 b_U20 b_vT1 c_acc0 b_M21 c_y1 a_tap21
    c_R2 a_evac3 b_Ue20 c_Z2 a_tap22 b_Tp20 c_ss1 b_Me21 b_vtok1 b_U21 b_bm41 c_m1 b_Te20 c_u2 b_Ue21 b_M30
    b_kT b_Me30 b_Tp21 c_SU2 a_tap30 b_U30 c_me1 c_p1 b_bm50 b_Ue30 b_Te21 c_O2 a_tap31 b_M31 b_sq0 b_ktok
    b_Tp30 b_Me31 c_S2 b_Te30 c_out1 b_U31 b_M40 a_tanh2 c_KS3 b_Ue31 b_Tp31 c_acch1 b_bm51 c_R3 c_acc1 c_sq2
    b_qT b_Me40 b_U40 b_Te31 b_M41 c_Z3 b_Ue40 c_y2 b_Me41 b_Tp40 b_U41 b_Te40 b_Ue41 b_n0 c_ss2 b_M50 c_u3
    b_Tp41 b_Me50 c_m2 b_Te41 b_sq1 c_me2 c_p2 a_silu2 c_O3 b_U50 b_Ue50 c_sq3 b_M51 c_out2 b_n1 b_Tp50 b_gend
    b_Me51 c_acch2 c_y3 b_U51 c_ss3 b_Te50 b_P0 b_Ue51 b_R0 b_kqs c_m3 c_me3 b_Tp51 b_ss b_F0 c_acc2 b_Te51
    c_p3 b_P1 b_R1 b_w1 c_out3 b_T0 a_tap32 a_tanh3 b_F1 b_root c_acch3 b_T1 c_acc3 a_silu3 b_s2
""".split()


EXPERT_ORDER = """
    x_bn0 r_sum r_mean v_mm r_cen r_cen2 r_var r_vare r_rstd x_ve0 x_rs0 o_bn0 r_n0 r_n1 r_n2 r_score t_max
    x_y1 t_idx t_gap x_x1 t_e2 t_hot t_den t_sh0 t_sh1 v_T o_bn1 o_ve t_w x_bn1 t_we w_turn o_rs x_ve1 w_T
    x_rs1 q_mm w_mm0 o_n0 q_sq o_n1 w_hw0 q_s q_c2 o_sum h_mm w_mm1 h_th0 h_th1 x_xf q_cn w_hw1 o_store l_x
    x_turn h_s0 h_s1 w_out0 w_out1 x_xT
""".split()


class Phase(ExitStack):

    def __init__(self, nc):
        super().__init__()
        self.nc, self.sems = nc, []

    def semaphore(self, name):
        self.sems.append(self.nc.alloc_semaphore(name=name))
        return self.sems[-1]

    def finish(self):
        self.nc.all_engine_barrier()
        self.nc.clear_and_free_semaphores(self.sems)
        self.nc.all_engine_barrier()


class Steps:

    def __init__(self, nc, ctx):
        self.nc, self.ctx, self.at, self.last = nc, ctx, {}, {}

    def series(self, name, steps):
        sem = self.ctx.semaphore(name)
        self.last[name] = len(steps) - 1
        for k, step in enumerate(steps):
            self.at[step] = (sem, name, k, len(steps))

    def find(self, name):
        if name not in self.at:
            self.series(name, [name])
        return self.at[name]

    def sem(self, name):
        return self.find(name)[0]

    def done(self, instruction, name):
        sem, series, k, n = self.find(name)
        assert k == (self.last[series] + 1) % n, (name, self.last[series])
        self.last[series] = k
        instruction.then_inc(sem, 1)

    def loaded(self, dma, name):
        dma.then_inc(self.sem(name), 16)

    def need(self, eng, i, *names):
        if isinstance(i, int) and i < 0:
            return
        latest = {}
        for name in names:
            sem, series, k, n = self.find(name)
            if series not in latest or latest[series][1] < k:
                latest[series] = (sem, k, n)
        for sem, k, n in latest.values():
            eng.wait_ge(sem, i * n + (k + 1))

    def need_dma(self, eng, i, name):
        if isinstance(i, int) and i < 0:
            return
        eng.wait_ge(self.sem(name), (i + 1) * 16)

    def need_dma_of(self, eng, i, name, par):
        if isinstance(i, int) and i < 0:
            return
        eng.wait_ge(self.sem(f"{name}{par}"), (i // 2 + 1) * 16)


class Chain:

    def __init__(self, nc, ctx, name, per):
        self.sem, self.per, self.k = ctx.semaphore(name), per, 0

    def start(self, i):
        self.i, self.k = i, 0

    def inc(self, instruction):
        instruction.then_inc(self.sem, 1)
        self.k += 1
        return self.i * self.per + self.k

    def end(self):
        assert self.k == self.per, (self.k, self.per)

    def last_of(self, i):
        return (i + 1) * self.per


def in_slots(nc, n, lag, first, engines, body):
    for t in range(first):
        body(t, t % 2)
    end = first + (n - first) // 2 * 2
    with nc.Fori(first, end, 2, engines=engines) as t:
        body(t, first % 2)
        body(t + 1, (first + 1) % 2)
    for t in range(end, n + lag):
        body(t, t % 2)


def active(i, n):
    return not isinstance(i, int) or 0 <= i < n


def issue(order, threads):
    pending = {next(thread): thread for thread in threads}
    for name in order:
        if name in pending:
            thread = pending.pop(name)
            following = next(thread, None)
            if following:
                pending[following] = thread
    assert not pending, sorted(pending)


def settle(eng, scratch):
    eng.tensor_tensor(scratch[0:1, 0:1], scratch[0:1, 1:2], scratch[0:1, 1:2], ALU.add)


def make_constants(nc, ctx, sb):
    pool = nc.gpsimd
    s_const = ctx.enter_context(nc.semaphore("const_built"))
    n = [0]

    def step(ins):
        ins.then_inc(s_const, 1)
        n[0] += 1
        pool.wait_ge(s_const, n[0])

    c = {}
    c["ident"] = sb("ident", [P, P], F32)
    step(pool.memset(c["ident"][:], 1.0))
    step(pool.affine_select(out=c["ident"][:], in_=c["ident"][:], pattern=[[-1, P]], compare_op=ALU.is_equal,
                            fill=0.0, base=0, channel_multiplier=1))
    c["ident16"] = sb("ident16", [P, P], F16)
    step(pool.tensor_copy(c["ident16"][:], c["ident"][:]))
    c["upper"] = sb("upper", [P, P], F32)
    step(pool.memset(c["upper"][:], 1.0))
    step(pool.affine_select(out=c["upper"][:], in_=c["upper"][:], pattern=[[1, P]], compare_op=ALU.is_ge,
                            fill=0.0, base=0, channel_multiplier=-1))
    c["ones_col"] = sb("ones_col", [P, 1], F32)
    step(pool.memset(c["ones_col"][:], 1.0))
    for name in ("settle_dve", "settle_pool"):
        c[name] = sb(name, [P, 2], F32)
        step(pool.memset(c[name][:], 0.0))
    for name, value in (("half", 0.5), ("minus_half", -0.5)):
        c[name] = sb(name, [P, 16], F32)
        step(pool.memset(c[name][:], value))

    def block_mask(view_of, size, value):
        nblk = P // (2 * size)
        v = view_of.rearrange("p (b t r) -> p b t r", t=2, r=size)[:, :, 1, :]
        step(pool.memset(v, value))
        step(pool.affine_select(out=v, in_=v, pattern=[[-2 * size, nblk], [0, size]], compare_op=ALU.is_ge,
                                fill=0.0, base=0, channel_multiplier=1))
        step(pool.affine_select(out=v, in_=v, pattern=[[2 * size, nblk], [0, size]], compare_op=ALU.is_ge,
                                fill=0.0, base=size - 1, channel_multiplier=-1))

    c["mask"] = sb("mask", [P, NLEV, P], F16)
    step(pool.memset(c["mask"][:], 0.0))
    for lev in range(NLEV):
        block_mask(c["mask"][:, lev, :], 2 << lev, 1.0)
    c["first"] = sb("first", [P, P], F16)
    step(pool.memset(c["first"][:], 0.0))
    block_mask(c["first"][:], 1, -1.0)
    step(pool.tensor_tensor(c["first"][:], c["first"][:], c["ident16"][:], ALU.add))
    return c, s_const, n[0]


def phase_norm(nc, c, x, w_ab, xT_dram, gate_tok):
    with Phase(nc) as ctx:
        sb = lambda name, shape, dt=F32: ctx.enter_context(nc.sbuf_tensor(name, shape, dt))
        x_in = [sb(f"n_x{p}", [P, CH, D]) for p in range(2)]
        xn = [sb(f"n_xn{p}", [P, CH, D]) for p in range(2)]
        xT = [sb(f"n_xT{p}", [P, KT, T]) for p in range(2)]
        stats = sb("n_stats", [P, CH, 6])
        mv = sb("n_mv", [P, CH, 2])
        rstd = sb("n_rstd", [P, CH])
        wab = sb("n_wab", [P, KT, 2 * H])
        turn_ps = [ctx.enter_context(nc.psum_tensor(f"n_turn{k}", [P, T], F32)) for k in range(KT)]
        ab_ps = ctx.enter_context(nc.psum_tensor("n_ab", [P, CH, P], F32))
        s = Steps(nc, ctx)
        dve = Chain(nc, ctx, "n_dve", 3 * CH)

        nc.sync.dma_start(wab[:], w_ab).then_inc(s.sem("n_wab_in"), 16)

        def gates(j, q):
            s.need(nc.tensor, j, "n_xT")
            if isinstance(j, int) and j == 0:
                nc.tensor.wait_ge(s.sem("n_wab_in"), 16)
            s.need(nc.tensor, j - 1, "n_ab_out")
            for m in range(CH):
                for k in range(KT):
                    ins = nc.tensor.matmul(ab_ps[:, m, 0:2 * H], xT[q][:, k, m * P:(m + 1) * P], wab[:, k, :],
                                           start=k == 0, stop=k == KT - 1)
            s.done(ins, "n_ab")
            s.need(nc.vector, j, "n_ab")
            by_chunk = ab_ps[:, :, 0:2 * H].rearrange("p c (n q h) -> p n c q h", n=2, h=2)
            for n in range(2):
                for m in range(CH):
                    dst = gate_tok[n][:].rearrange("p (q x) -> p q x", q=NP)[:, :, bass.ds(j * NU + 2 * m, 2)]
                    ins = nc.vector.tensor_copy(dst, by_chunk[:, n, m])
            s.done(ins, "n_ab_out")

        def body(t, par):
            i, j, ab = t - 1, t - 2, t - 3
            if active(t, NB):
                s.need(nc.sync, t - 2, "n_xn")
                s.loaded(nc.sync.dma_start(x_in[par][:], x[bass.ds(t, 1)].rearrange("a p c d -> p (a c) d")),
                         f"n_x_in{par}")
            if active(j, NB):
                q = par
                s.need(nc.tensor, j, "n_xn")
                s.need(nc.tensor, j - 1, "n_xT")
                for k in range(KT):
                    for m in range(CH):
                        ins = nc.tensor.transpose(turn_ps[k][:, m * P:(m + 1) * P], xn[q][:, m, k * P:(k + 1) * P],
                                                  c["ident"][:])
                s.done(ins, "n_turn")
                s.need_dma_of(nc.scalar, j - 2, "n_xT_out", q)
                s.need(nc.scalar, j - 2, "n_ab")
                s.need(nc.scalar, j, "n_turn")
                for k in range(KT):
                    ins = nc.scalar.copy(xT[q][:, k, :], turn_ps[k][:])
                s.done(ins, "n_xT")
                s.need(nc.sync, j, "n_xT")
                s.loaded(nc.sync.dma_start(xT_dram[bass.ds(j, 1)].rearrange("a p k t -> p (a k) t"), xT[q][:]),
                         f"n_xT_out{q}")
            if active(i, NB):
                q = 1 - par
                s.need_dma_of(nc.vector, i, "n_x_in", q)
                dve.start(i)
                for k in range(CH):
                    v = dve.inc(nc.vector.bn_stats(stats[:, k, :], x_in[q][:, k, :]))
                nc.vector.wait_ge(dve.sem, v)
                settle(nc.vector, c["settle_dve"])
                for k in range(CH):
                    v = dve.inc(nc.vector.bn_aggr(mv[:, k, :], stats[:, k, :]))
                nc.vector.wait_ge(dve.sem, v)
                s.need(nc.vector, i - 1, "n_rstd")
                v = dve.inc(nc.vector.tensor_scalar(rstd[:], mv[:, :, 1], LN_EPS, None, ALU.add))
                nc.gpsimd.wait_ge(dve.sem, v)
                s.done(nc.gpsimd.tensor_tensor(rstd[:], rstd[:], c["minus_half"][:, 0:CH], ALU.pow), "n_rstd")
                s.need(nc.vector, i, "n_rstd")
                s.need(nc.vector, i - 2, "n_turn")
                for k in range(CH):
                    ins = nc.vector.tensor_scalar(xn[q][:, k, :], x_in[q][:, k, :], mv[:, k, 0:1],
                                                  rstd[:, k:k + 1], ALU.subtract, ALU.mult)
                    if k < CH - 1:
                        dve.inc(ins)
                s.done(ins, "n_xn")
            if active(ab, NB):
                gates(ab, 1 - par)

        in_slots(nc, NB, 3, 5, EVERY, body)
        for p in range(2):
            nc.sync.wait_ge(s.sem(f"n_xT_out{p}"), 16 * NB // 2)
        ctx.finish()


def phase_gates(nc, c, a_log, dt_bias, gate_tok, g_dram):
    with Phase(nc) as ctx:
        sb = lambda name, shape, dt=F32: ctx.enter_context(nc.sbuf_tensor(name, shape, dt))
        W = NIT * NU
        alog = sb("g_alog", [P, H])
        nega = sb("g_nega", [P, H])
        dtb = sb("g_dtb", [P, H])
        z, az, rows = sb("g_z", [P, W]), sb("g_az", [P, W]), sb("g_rows", [P, W // P, P])
        ps = [ctx.enter_context(nc.psum_tensor(f"g_ps{k}", [P, 512], F32)) for k in range(2)]
        s_in = ctx.semaphore("g_in")
        s_v = ctx.semaphore("g_dve")
        s_a = ctx.semaphore("g_act")
        s_p = ctx.semaphore("g_pe")
        s_out = ctx.semaphore("g_out")
        by_head = lambda t: t[:].rearrange("p (q x h) -> p q x h", q=NP, h=2)
        spread = lambda t: t[:].rearrange("p (q x h) -> p q x h", x=1, h=2).broadcast_to([P, NP, W // H, 2])

        nc.sync.dma_start(alog[:], a_log.partition_broadcast(P)).then_inc(s_in, 16)
        nc.sync.dma_start(dtb[:], dt_bias.partition_broadcast(P)).then_inc(s_in, 16)
        nc.vector.wait_ge(s_in, 32)
        nc.scalar.wait_ge(s_in, 32)
        nc.vector.tensor_tensor(by_head(z), by_head(gate_tok[0]), spread(dtb), ALU.add).then_inc(s_v, 1)
        nc.scalar.wait_ge(s_v, 1)
        nc.scalar.activation(az[:], z[:], ACT.Abs).then_inc(s_a, 1)
        nc.scalar.wait_ge(s_a, 1)
        nc.scalar.activation(az[:], az[:], ACT.Exp, scale=-1.0).then_inc(s_a, 1)
        nc.scalar.activation(nega[:], alog[:], ACT.Exp).then_inc(s_a, 1)
        nc.scalar.wait_ge(s_a, 2)
        nc.scalar.activation(az[:], az[:], ACT.Ln, bias=1.0).then_inc(s_a, 1)
        nc.vector.wait_ge(s_v, 1)
        nc.vector.wait_ge(s_a, 4)
        nc.vector.scalar_tensor_tensor(z[:], z[:], 0.0, az[:], ALU.max, ALU.add).then_inc(s_v, 1)
        nc.vector.tensor_scalar(nega[:], nega[:], -1.0, None, ALU.mult).then_inc(s_v, 1)
        nc.vector.wait_ge(s_v, 3)
        nc.vector.tensor_tensor(by_head(z), by_head(z), spread(nega), ALU.mult).then_inc(s_v, 1)
        nc.scalar.activation(gate_tok[1][:], gate_tok[1][:], ACT.Tanh, scale=0.5).then_inc(s_a, 1)
        nc.vector.wait_ge(s_a, 5)
        nc.vector.tensor_scalar(gate_tok[1][:], gate_tok[1][:], 1.0, None, ALU.add).then_inc(s_v, 1)
        nc.tensor.wait_ge(s_v, 4)
        for k in range(2):
            nc.tensor.matmul(ps[k][:], c["upper"][:], z[:, k * 512:(k + 1) * 512], start=True,
                             stop=True).then_inc(s_p, 1)
        for k in range(2):
            nc.vector.wait_ge(s_p, k + 1)
            nc.vector.tensor_copy(gate_tok[0][:, k * 512:(k + 1) * 512], ps[k][:]).then_inc(s_v, 1)
        for k in range(2):
            nc.tensor.wait_ge(s_v, 6 + k)
            for m in range(4):
                col = k * 512 + m * P
                ins = nc.tensor.transpose(ps[k][:, m * P:(m + 1) * P], gate_tok[0][:, col:col + P], c["ident"][:])
            ins.then_inc(s_p, 1)
        for k in range(2):
            nc.scalar.wait_ge(s_p, 3 + k)
            nc.scalar.copy(rows[:, 4 * k:4 * k + 4, :], ps[k][:].rearrange("p (a b) -> p a b", a=4)).then_inc(s_a, 1)
        nc.sync.wait_ge(s_a, 7)
        nc.sync.dma_start(g_dram[0:NIT * NU].rearrange("(a r) t -> r a t", r=P), rows[:]).then_inc(s_out, 16)
        nc.sync.wait_ge(s_out, 16)
        ctx.finish()


def phase_delta(nc, c, w_qkv, w_gate, w_out, norm_w, xT_dram, g_dram, gate_tok, acc):
    with Phase(nc) as ctx:
        sb = lambda name, shape, dt=F32: ctx.enter_context(nc.sbuf_tensor(name, shape, dt))
        two = lambda name, shape, dt=F32: [sb(f"{name}{p}", shape, dt) for p in range(2)]
        bank = lambda name: ctx.enter_context(nc.psum_tensor(name, [P, 512], F32))
        pe, act, dve, pool, sp = nc.tensor, nc.scalar, nc.vector, nc.gpsimd, nc.sync
        s = Steps(nc, ctx)

        wq = sb("wqkv", [P, KT * N_QKV + 4 * TAPS])
        wqkv = wq[:, 0:KT * N_QKV].rearrange("p (k n) -> p k n", k=KT)
        tap = wq[:, KT * N_QKV:].rearrange("p (j r) -> p j r", r=TAPS)
        wg = sb("wgate", [P, KT, 2 * P])
        wo = sb("wout", [P, 2, D])
        normw = sb("normw", [P, 1])
        xin = two("xin", [P, KT, T])
        kq = two("kq", [P, 2, T])
        vch = two("vch", [P, 2, T])
        pad = two("pad", [P, PAD + T])
        cv = two("cv", [P, T])
        th = sb("th", [P, T])
        grow = sb("grow", [P, NU, P])
        g_it = sb("g_it", [P, NU])
        dec = sb("dec", [P, NU, P])
        gam = sb("gam", [P, T])
        sq = sb("sq", [P, T])
        ss, rc, root = sb("ss", [P, 16]), sb("rc", [P, 16]), sb("root", [P, 16])
        bt = sb("bt", [P, NU, P])
        bm = sb("bm", [P, NLEV, NU, P], F16)
        tt = sb("tt", [P, 2, NU, P], F16)
        m1 = sb("m1", [P, NU, P], F16)
        bhi, blo = sb("bhi", [P, NU, P], F16), sb("blo", [P, NU, P], F16)
        r16 = sb("r16", [P, 4, P], F16)
        kqs = two("kqs", [P, 2, T])
        ktok = two("ktok", [P, NU, DK])
        vtok = two("vtok", [P, NU, DV])
        w1 = two("w1", [P, NU])
        s2 = two("s2", [P, NU])
        s2sq = two("s2sq", [P, NU])
        gend = two("gend", [P, CH])
        sg = two("sg", [P, 2, T])
        at = two("at", [P, NU, P])
        tinv = two("tinv", [P, NU, P])
        state = sb("state", [P, 2, DV])
        rr = sb("rr", [P, 2, DV])
        uu = sb("uu", [P, 2, DV])
        yy = sb("yy", [P, 2, P])
        sqo = sb("sqo", [P, 2, P])
        msq, rms = sb("msq", [P, 2]), sb("rms", [P, 2])

        ps_a, ps_b = bank("ps_a"), bank("ps_b")
        b0, b1, b2 = bank("b0"), bank("b1"), bank("b2")
        ck, cz, co = bank("ck"), bank("cz"), bank("co")
        halves = (b1, b2)

        def free(eng, users, name, i):
            k = users.index(name)
            if k:
                s.need(eng, i, users[k - 1])
            else:
                s.need(eng, i - 1, users[-1])

        A_USERS = [f"a_evac{j}" for j in range(4)]
        PB_USERS = ["b_ktok", "b_sq1", "b_sg0", "b_sg1", "b_vtok0", "b_vtok1"]
        levels = [(l, g) for l in range(NLEV) for g in range(2)]
        B0_USERS = [f"b_Me{l}{g}" for l, g in levels] + [f"b_R{g}" for g in range(2)]
        BH_USERS = [[f"b_ev0{k}", f"b_ev1{k}", f"b_Tf{k}"] + [f"{n}{l}{k}" for l in range(NLEV) for n in ("b_Ue", "b_Te")]
                    + [f"b_T{k}"] for k in range(2)]
        CK_USERS = ["c_S0"] + [n for m in range(1, CH) for n in ([f"c_R{m}", f"c_m{m - 1}"]
                                                                 + ([f"c_S{m}"] if m < CH - 1 else []))]
        CK_USERS += [f"c_m{CH - 1}"]
        CZ_USERS = ["c_u0"] + [n for m in range(1, CH) for n in (f"c_u{m}", f"c_acc{m - 1}")] + [f"c_acc{CH - 1}"]
        CO_USERS = [f"c_y{k}" for k in range(CH)]
        for name in ("a_proj", "a_pad", "a_evac", "a_tanh", "a_silu"):
            s.series(name, [f"{name}{j}" for j in range(4)])
        s.series("a_tap", [f"a_tap{j}{r}" for j in range(4) for r in range(PAD)])
        for name in ("b_M", "b_Me", "b_U", "b_Ue", "b_bm"):
            s.series(name, [f"{name}{l}{g}" for l, g in levels])
        s.series("b_Tp", ["b_Tq0", "b_Tq1"] + [f"b_Tp{l}{g}" for l, g in levels])
        s.series("b_Te", ["b_Tf0", "b_Tf1"] + [f"b_Te{l}{g}" for l, g in levels])
        s.series("b_turn", ["b_kT", "b_qT"])
        for name in ("b_sq", "b_n", "b_hi", "b_lo", "b_vT", "b_vtok", "b_g", "b_tg", "b_sg", "b_diag", "b_t2", "b_P",
                     "b_R", "b_F", "b_T"):
            s.series(name, [f"{name}{g}" for g in range(2)])
        for name in ("b_kk", "b_ev"):
            s.series(name, [f"{name}{g}{k}" for g in range(2) for k in range(2)])
        for name in ("c_KS", "c_R"):
            s.series(name, [f"{name}{m}" for m in range(1, CH)])
        for name in ("c_SU", "c_S"):
            s.series(name, [f"{name}{m}" for m in range(CH - 1)])
        for name in ("c_Z", "c_u", "c_O", "c_sq", "c_y", "c_ss", "c_out", "c_m", "c_me", "c_p", "c_r", "c_acch",
                     "c_acc"):
            s.series(name, [f"{name}{m}" for m in range(CH)])

        sp.dma_start(normw[:], norm_w).then_inc(s.sem("normw_in"), 16)

        def load_x(i, b, par):
            s.need(sp, i - 2, "b_g1")
            s.loaded(sp.dma_start(xin[par][:], xT_dram[bass.ds(b, 1)].rearrange("a p k t -> p (a k) t")),
                     f"xin_in{par}")

        def load_rows(i):
            s.need(sp, i - 1, "b_sel", "b_gam")
            s.loaded(sp.dma_start(grow[:], g_dram[bass.ds(i * NU, NU), :].partition_broadcast(P)), "grow_in")

        def load_pair(hp):
            i = hp * NB
            pair = w_qkv[bass.ds(hp, 1)].rearrange("a p n -> p (a n)")
            of_tile = lambda j: (wqkv[:, :, j * P:(j + 1) * P],
                                 pair[:, 0:KT * N_QKV].rearrange("p (k n) -> p k n", k=KT)[:, :, j * P:(j + 1) * P])
            load_x(i, 0, 0)
            load_rows(i)
            for j in range(4):
                s.need(sp, i - 1, f"a_proj{j}")
                s.loaded(sp.dma_start(*of_tile(j)), f"wqkv_in{j}")
            s.need(sp, i - 1, "a_tap32", "a_evac3")
            s.loaded(sp.dma_start(wq[:, KT * N_QKV:], pair[:, KT * N_QKV:]), "tap_in")
            s.need(sp, i - 1, "b_g1")
            s.loaded(sp.dma_start(wg[:], w_gate[bass.ds(hp, 1)].rearrange("a p k n -> p (a k) n")), "wg_in")
            load_x(i + 1, 1, 1)
            load_rows(i + 1)
            load_x(i + 2, 2, 0)
            load_rows(i + 2)
            s.need(sp, i - 1, f"c_out{CH - 1}")
            s.loaded(sp.dma_start(wo[:], w_out[bass.ds(hp, 1)].rearrange("a p h d -> p (a h) d")), "wo_in")
            load_x(i + 3, 3, 1)
            load_rows(i + 3)
            with sp.Fori(4, NB, 2) as b:
                for par in range(2):
                    load_x(i + b + par, b + par, par)
                    load_rows(i + b + par)

        def stage_a(i, p):
            dest = [kq[p][:, 1, :], kq[p][:, 0, :], vch[p][:, 0, :], vch[p][:, 1, :]]
            hp = i // NB

            def project(j):
                yield f"a_proj{j}"
                if j == 0:
                    s.need_dma_of(pe, i, "xin_in", p)
                s.need_dma(pe, hp, f"wqkv_in{j}")
                free(pe, A_USERS, f"a_evac{j}", i)
                for k in range(KT):
                    ins = pe.matmul(ps_a[:], wqkv[:, k, j * P:(j + 1) * P], xin[p][:, k, :], start=k == 0,
                                    stop=k == KT - 1)
                s.done(ins, f"a_proj{j}")
                yield f"a_evac{j}"
                if j == 0:
                    s.need_dma(act, hp, "tap_in")
                s.need(act, i if j > 1 else i - 1, f"a_silu{(j - 2) % 4}")
                s.need(act, i, f"a_proj{j}")
                s.done(act.copy(pad[j % 2][:, PAD:], ps_a[:]), f"a_pad{j}")
                s.done(act.activation(cv[j % 2][:], ps_a[:], ACT.Copy, scale=tap[:, j, TAPS - 1:TAPS]), f"a_evac{j}")
                for r in range(PAD):
                    yield f"a_tap{j}{r}"
                    if r == 0:
                        if j == 0:
                            s.need_dma(dve, hp, "tap_in")
                        s.need(dve, i, f"a_pad{j}", f"a_evac{j}")
                    else:
                        s.need(dve, i, f"a_tap{j}{r - 1}")
                    s.done(dve.scalar_tensor_tensor(cv[j % 2][:], pad[j % 2][:, r:r + T], tap[:, j, r:r + 1],
                                                    cv[j % 2][:], ALU.mult, ALU.add), f"a_tap{j}{r}")
                yield f"a_tanh{j}"
                s.need(act, i, f"a_tap{j}{PAD - 1}")
                s.need(act, i if j else i - 1, f"a_silu{(j - 1) % 4}")
                s.done(act.activation(th[:], cv[j % 2][:], ACT.Tanh, scale=0.5), f"a_tanh{j}")
                yield f"a_silu{j}"
                s.need(dve, i, f"a_tanh{j}")
                if j < 2:
                    s.need(dve, i - 2, "b_kqs", "b_kk11", "b_qT" if j == 0 else "b_kT")
                else:
                    s.need(dve, i - 2, f"b_vT{j - 2}")
                s.done(dve.scalar_tensor_tensor(dest[j], th[:], 1.0, cv[j % 2][:], ALU.add, ALU.mult),
                       f"a_silu{j}")

            return [project(j) for j in range(4)]

        def stage_b(i, p, early):
            tok = lambda k: gate_tok[k][:, bass.ds(i * NU, NU)]
            col = lambda t, u: t[:, u:u + 1]
            units = lambda g: slice(4 * g, 4 * g + 4)
            in_units = lambda t: t[:].rearrange("p (u t) -> p u t", t=P)

            def norms():
                for n in range(2):
                    yield f"b_sq{n}"
                    s.need(act, i, "b_kT" if n == 0 else "b_qT")
                    s.need(act, i if n else i - 1, f"b_n{1 - n}")
                    s.done(act.activation(sq[:], ps_b[:], ACT.Square), f"b_sq{n}")
                    yield f"b_n{n}"
                    s.need(dve, i, f"b_sq{n}")
                    s.need(dve, i - 1, "b_root")
                    s.done(dve.tensor_reduce(ss[:, n * NU:(n + 1) * NU], sq[:].rearrange("p (u e) -> p u e", e=DK),
                                             AX.X, ALU.add), f"b_n{n}")
                yield "b_ss"
                s.need(dve, i, "b_n1")
                s.done(dve.tensor_scalar(ss[:], ss[:], 4e-6, None, ALU.add), "b_ss")
                yield "b_w1"
                s.need(dve, i, "b_ss")
                s.done(dve.reciprocal(rc[:], ss[:]), "b_rc")
                s.need(dve, i, "b_rc")
                s.need(dve, i - 2, f"c_u{CH - 1}")
                s.done(dve.tensor_tensor(w1[p][:], rc[:, 0:NU], tok(1), ALU.mult), "b_w1")
                yield "b_root"
                s.need(pool, i, "b_ss")
                s.need(pool, i - 1, "b_s2", "b_vtok0", "b_vtok1")
                s.done(pool.tensor_tensor(root[:], ss[:], c["half"][:, 0:16], ALU.pow), "b_root")
                yield "b_s2"
                s.need(dve, i, "b_rc", "b_root")
                s.need(dve, i - 2, f"c_r{CH - 1}")
                s.done(dve.tensor_scalar(s2sq[p][:], rc[:, NU:], 1.0 / (256 * DV), None, ALU.mult), "b_s2sq")
                s.done(dve.scalar_tensor_tensor(s2[p][:], rc[:, NU:], 1.0 / 16, root[:, NU:], ALU.mult, ALU.mult),
                       "b_s2")

            def decays():
                yield "b_git"
                s.need(dve, i - 1, "b_E")
                s.done(dve.tensor_scalar(g_it[:], tok(0), -1.0, None, ALU.mult), "b_git")
                yield "b_sel"
                s.need_dma(pool, i, "grow_in")
                s.need(pool, i - 1, "b_ev11", "b_ktok")
                settle(pool, c["settle_pool"])
                s.done(pool.affine_select(out=dec[:], in_=grow[:], pattern=[[0, NU], [1, P]], compare_op=ALU.is_ge,
                                          fill=NEG, base=0, channel_multiplier=-1), "b_sel")
                yield "b_E"
                s.need(act, i, "b_git", "b_sel")
                for u in range(NU):
                    ins = act.activation(dec[:, u, :], dec[:, u, :], ACT.Exp, bias=col(g_it, u))
                s.done(ins, "b_E")

            def decayed_kq():
                yield "b_gam"
                s.need_dma(act, i, "grow_in")
                s.need(act, i - 1, "b_kqs", "b_gend")
                for h in range(2):
                    rows = slice(h * DK, (h + 1) * DK)
                    src = grow[rows].rearrange("p (c h) t -> p c h t", h=2)[:, :, h, :]
                    ins = act.activation(gam[rows, :].rearrange("p (c t) -> p c t", t=P), src, ACT.Exp)
                s.done(ins, "b_gam")
                yield "b_gend"
                s.need(dve, i, "b_gam")
                s.need(dve, i - 2, f"c_S{CH - 2}")
                s.done(dve.tensor_copy(gend[p][:], gam[:].rearrange("p (c t) -> p c t", t=P)[:, :, P - 1]), "b_gend")
                yield "b_kqs"
                s.need(pool, i, "b_gam", "a_silu0", "a_silu1")
                s.need(pool, i - 2, f"c_O{CH - 1}")
                s.done(pool.tensor_tensor(kqs[p][:], kq[p][:], gam[:].unsqueeze(1).broadcast_to([P, 2, T]), ALU.mult),
                       "b_kqs")

            def gate(h):
                yield f"b_g{h}"
                free(pe, PB_USERS, f"b_sg{h}", i)
                if h == 0:
                    s.need_dma(pe, i // NB, "wg_in")
                for k in range(KT):
                    ins = pe.matmul(ps_b[:], wg[:, k, h * P:(h + 1) * P], xin[p][:, k, :], start=k == 0,
                                    stop=k == KT - 1)
                s.done(ins, f"b_g{h}")
                yield f"b_tg{h}"
                s.need(act, i, f"b_g{h}")
                s.need(act, i - 2, f"c_y{CH - 1}")
                s.done(act.activation(sg[p][:, h, :], ps_b[:], ACT.Tanh, scale=0.5), f"b_tg{h}")
                yield f"b_sg{h}"
                s.need(dve, i, f"b_tg{h}")
                s.done(dve.scalar_tensor_tensor(sg[p][:, h, :], sg[p][:, h, :], 1.0, ps_b[:], ALU.add, ALU.mult),
                       f"b_sg{h}")

            def turn_kq():
                yield "b_kT"
                s.need(pe, i, "a_silu1")
                free(pe, PB_USERS, "b_ktok", i)
                for m in range(CH):
                    ins = pe.transpose(ps_b[:, m * P:(m + 1) * P], kq[p][:, 0, m * P:(m + 1) * P], c["ident"][:])
                s.done(ins, "b_kT")
                yield "b_ktok"
                s.need(dve, i, "b_sq0", "b_E")
                s.need(dve, i - 2, f"c_SU{CH - 2}")
                s.done(dve.tensor_tensor(ktok[p][:], ps_b[:].rearrange("p (u e) -> p u e", e=DK),
                                         dec[:, :, P - 1:P].broadcast_to([P, NU, DK]), ALU.mult), "b_ktok")
                yield "b_qT"
                s.need(pe, i, "a_silu0")
                free(pe, PB_USERS, "b_sq1", i)
                for m in range(CH):
                    ins = pe.transpose(ps_b[:, m * P:(m + 1) * P], kq[p][:, 1, m * P:(m + 1) * P], c["ident"][:])
                s.done(ins, "b_qT")

            def turn_v(h):
                yield f"b_vT{h}"
                s.need(pe, i, f"a_silu{2 + h}")
                free(pe, PB_USERS, f"b_vtok{h}", i)
                for m in range(CH):
                    ins = pe.transpose(ps_b[:, m * P:(m + 1) * P], vch[p][:, h, m * P:(m + 1) * P], c["ident"][:])
                s.done(ins, f"b_vT{h}")
                yield f"b_vtok{h}"
                s.need(dve, i, f"b_vT{h}", "b_root")
                s.need(dve, i - 2, f"c_Z{CH - 1}")
                scale = root[:, 0:NU].rearrange("p (c h) -> p c h", h=2)[:, :, h:h + 1].broadcast_to([P, CH, DV])
                s.done(dve.tensor_tensor(vtok[p][:].rearrange("p (c h) e -> p c h e", h=2)[:, :, h, :],
                                         ps_b[:].rearrange("p (c e) -> p c e", e=DV), scale, ALU.mult), f"b_vtok{h}")

            def products(g, k):
                users, ps, rows = BH_USERS[k], halves[k], slice(k * DK, (k + 1) * DK)
                yield f"b_kk{g}{k}"
                s.need(pe, i, "a_silu0", "a_silu1")
                free(pe, users, f"b_ev{g}{k}", i)
                for n in range(2):
                    t = slice((2 * g + n) * P, (2 * g + n + 1) * P)
                    ins = pe.matmul(ps[:, n * 2 * P:(n + 1) * 2 * P], kq[p][rows, 0, t], kq[p][rows, :, t],
                                    start=True, stop=True)
                s.done(ins, f"b_kk{g}{k}")
                yield f"b_ev{g}{k}"
                s.need(dve, i, f"b_kk{g}{k}", "b_E", "b_w1")
                s.need(dve, i - 1, f"b_bm{NLEV - 1}{g}", f"b_lo{g}")
                for n in range(2):
                    u = 4 * g + 2 * n + k
                    dve.scalar_tensor_tensor(bt[:, u, :], ps[:, n * 2 * P:n * 2 * P + P], col(w1[p], u), dec[:, u, :],
                                             ALU.mult, ALU.mult)
                of_head = lambda t: t[:, 4 * g:4 * g + 4, :].rearrange("p (n h) t -> p n h t", h=2)[:, :, k, :]
                s.need(dve, i - 2, f"c_O{CH - 1}")
                s.done(dve.tensor_tensor(of_head(at[p]), ps[:].rearrange("p (n q t) -> p n q t", n=2, q=2)[:, :, 1, :],
                                         of_head(dec), ALU.mult), f"b_ev{g}{k}")

            def masks(g):
                yield f"b_diag{g}"
                s.need(pool, i, f"b_ev{g}0", f"b_ev{g}1")
                settle(pool, c["settle_pool"])
                s.done(pool.affine_select(out=bt[:, units(g), :], in_=bt[:, units(g), :], pattern=[[0, 4], [1, P]],
                                          compare_op=ALU.not_equal, fill=1.0, base=0, channel_multiplier=-1),
                       f"b_diag{g}")
                yield f"b_t2{g}"
                s.need(pool, i, f"b_diag{g}")
                s.need(pool, i - 1, f"b_T{g}")
                s.done(pool.tensor_tensor(tt[:, 1, units(g), :], bt[:, units(g), :],
                                          c["first"][:].unsqueeze(1).broadcast_to([P, 4, P]), ALU.mult), f"b_t2{g}")
                for l in range(NLEV):
                    yield f"b_bm{l}{g}"
                    s.need(pool, i - 1, f"b_M{l}{g}")
                    s.done(pool.tensor_tensor(half_of(bm[:, l, units(g), :], l, 1), half_of(bt[:, units(g), :], l, 1),
                                              half_of(c["mask"][:, l, :].unsqueeze(1).broadcast_to([P, 4, P]), l, 1),
                                              ALU.mult), f"b_bm{l}{g}")

            def parts(g):
                yield f"b_hi{g}"
                s.need(act, i, f"b_diag{g}")
                s.need(act, i - 1, f"b_P{g}")
                s.done(act.copy(bhi[:, units(g), :], bt[:, units(g), :]), f"b_hi{g}")
                yield f"b_lo{g}"
                s.need(pool, i, f"b_hi{g}")
                s.done(pool.tensor_tensor(blo[:, units(g), :], bt[:, units(g), :], bhi[:, units(g), :],
                                          ALU.subtract), f"b_lo{g}")

            def half_of(t, l, k):
                return t.rearrange("p u (b k r) -> p u b k r", k=2, r=2 << l)[:, :, :, k, :]

            def half_bank(bank, l):
                return bank[:, 0:2 * P].rearrange("p (u b r) -> p u b r", u=4, r=2 << l)

            def invert(g):
                bank = halves[g]
                yield f"b_Tq{g}"
                s.need(pe, i, f"b_t2{g}", f"b_ev1{g}")
                for k in range(4):
                    ins = pe.transpose(bank[:].bitcast(F16)[:, k * P:(k + 1) * P], tt[:, 1, 4 * g + k, :],
                                       c["ident16"][:])
                s.done(ins, f"b_Tq{g}")
                yield f"b_Tf{g}"
                s.need(act, i, f"b_Tq{g}")
                s.done(act.copy(tt[:, 0, units(g), :],
                                bank[:].bitcast(F16)[:, 0:4 * P].rearrange("p (u t) -> p u t", t=P)), f"b_Tf{g}")
                for l in range(NLEV):
                    yield f"b_M{l}{g}"
                    s.need(pe, i, f"b_bm{l}{g}", f"b_Te{l - 1}{g}" if l else f"b_Tf{g}")
                    free(pe, B0_USERS, f"b_Me{l}{g}", i)
                    for k in range(4):
                        ins = pe.matmul(b0[:, k * P:(k + 1) * P], bm[:, l, 4 * g + k, :], tt[:, 0, 4 * g + k, :],
                                        start=True, stop=True)
                    s.done(ins, f"b_M{l}{g}")
                    yield f"b_Me{l}{g}"
                    s.need(act, i, f"b_M{l}{g}")
                    s.done(act.mul(m1[:, units(g), :], in_units(b0), -1.0), f"b_Me{l}{g}")
                    yield f"b_U{l}{g}"
                    s.need(pe, i, f"b_Me{l}{g}")
                    for k in range(4):
                        u = 4 * g + k
                        ins = pe.matmul(half_bank(bank, l)[:, k], m1[:, u, :], half_of(tt[:, 1], l, 1)[:, u],
                                        start=True, stop=True)
                    s.done(ins, f"b_U{l}{g}")
                    yield f"b_Ue{l}{g}"
                    s.need(dve, i, f"b_U{l}{g}")
                    new = half_of(tt[:, 1, units(g), :], l, 1)
                    s.done(dve.tensor_tensor(new, new, half_bank(bank, l), ALU.add), f"b_Ue{l}{g}")
                    yield f"b_Tp{l}{g}"
                    s.need(pe, i, f"b_Ue{l}{g}")
                    for k in range(4):
                        ins = pe.matmul(half_bank(bank, l)[:, k], tt[:, 1, 4 * g + k, :],
                                        half_of(c["ident16"][:].unsqueeze(1), l, 0)[:, 0], start=True, stop=True)
                    s.done(ins, f"b_Tp{l}{g}")
                    yield f"b_Te{l}{g}"
                    s.need(act, i, f"b_Tp{l}{g}")
                    s.done(act.copy(half_of(tt[:, 0, units(g), :], l, 0), half_bank(bank, l)), f"b_Te{l}{g}")
                yield f"b_P{g}"
                s.need(pe, i, f"b_Te{NLEV - 1}{g}", f"b_lo{g}")
                free(pe, B0_USERS, f"b_R{g}", i)
                for k in range(4):
                    u = 4 * g + k
                    pe.matmul(b0[:, k * P:(k + 1) * P], bhi[:, u, :], tt[:, 0, u, :], start=True, stop=False)
                    ins = pe.matmul(b0[:, k * P:(k + 1) * P], blo[:, u, :], tt[:, 0, u, :], start=False, stop=True)
                s.done(ins, f"b_P{g}")
                yield f"b_R{g}"
                s.need(dve, i, f"b_P{g}")
                s.need(dve, i if g else i - 1, f"b_F{1 - g}")
                s.done(dve.tensor_tensor(r16[:], c["ident"][:].unsqueeze(1).broadcast_to([P, 4, P]), in_units(b0),
                                         ALU.subtract), f"b_R{g}")
                yield f"b_F{g}"
                s.need(pe, i, f"b_R{g}")
                for k in range(4):
                    ins = pe.matmul(bank[:, k * P:(k + 1) * P], r16[:, k, :], tt[:, 1, 4 * g + k, :], start=True,
                                    stop=True)
                s.done(ins, f"b_F{g}")
                yield f"b_T{g}"
                s.need(dve, i, f"b_F{g}")
                s.need(dve, i - 2, f"c_Z{CH - 1}")
                s.done(dve.tensor_tensor(tinv[p][:, units(g), :], tt[:, 1, units(g), :], in_units(bank), ALU.add),
                       f"b_T{g}")

            if early:
                return [norms(), decays(), decayed_kq(), turn_kq()]
            threads = []
            for g in range(2):
                threads += [gate(g), turn_v(g), products(g, 0), products(g, 1), masks(g), parts(g), invert(g)]
            return threads

        def stage_c(i, p):
            def recur():
                for m in range(CH):
                    if m:
                        yield f"c_KS{m}"
                        s.need(pe, i, f"c_S{m - 1}", "b_kqs")
                        free(pe, CK_USERS, f"c_R{m}", i)
                        ins = pe.matmul(ck[:, 0:2 * DV], kqs[p][:, 0, m * P:(m + 1) * P],
                                        state[:].rearrange("p h e -> p (h e)"), start=True, stop=True)
                        s.done(ins, f"c_KS{m}")
                        yield f"c_R{m}"
                        s.need(dve, i, f"c_KS{m}", "b_vtok0", "b_vtok1")
                        s.done(dve.tensor_tensor(rr[:], vtok[p][:, 2 * m:2 * m + 2, :],
                                                 ck[:, 0:2 * DV].rearrange("p (h e) -> p h e", h=2), ALU.subtract),
                               f"c_R{m}")
                    yield f"c_Z{m}"
                    if m == 0:
                        s.need(pe, i, "b_T0", "b_vtok0", "b_vtok1")
                    else:
                        s.need(pe, i, f"c_R{m}", f"b_T{m // 2}")
                    free(pe, CZ_USERS, f"c_u{m}", i)
                    for h in range(2):
                        rhs = rr[:, h, :] if m else vtok[p][:, h, :]
                        ins = pe.matmul(cz[:, h * DV:(h + 1) * DV], tinv[p][:, 2 * m + h, :], rhs, start=True,
                                        stop=True)
                    s.done(ins, f"c_Z{m}")
                    yield f"c_u{m}"
                    s.need(act, i, f"c_Z{m}", "b_w1")
                    if m:
                        s.need(act, i, f"c_O{m - 1}")
                    else:
                        s.need(act, i - 1, f"c_O{CH - 1}")
                    for h in range(2):
                        ins = act.activation(uu[:, h, :], cz[:, h * DV:(h + 1) * DV], ACT.Copy,
                                             scale=w1[p][:, 2 * m + h:2 * m + h + 1])
                    s.done(ins, f"c_u{m}")
                    if m < CH - 1:
                        yield f"c_SU{m}"
                        s.need(pe, i, f"c_u{m}", "b_ktok")
                        free(pe, CK_USERS, f"c_S{m}", i)
                        for h in range(2):
                            ins = pe.matmul(ck[h * DK:(h + 1) * DK, 2 * DV:3 * DV], ktok[p][:, 2 * m + h, :],
                                            uu[:, h, :], start=True, stop=True)
                        s.done(ins, f"c_SU{m}")
                    yield f"c_O{m}"
                    s.need(pe, i, f"c_u{m}", "b_ktok", "b_kqs", f"b_ev{m // 2}1")
                    free(pe, CO_USERS, f"c_y{m}", i)
                    for h in range(2):
                        if m:
                            pe.matmul(co[:, h * P:(h + 1) * P], state[:, h, :], kqs[p][:, 1, m * P:(m + 1) * P],
                                      start=True, stop=False)
                        ins = pe.matmul(co[:, h * P:(h + 1) * P], uu[:, h, :], at[p][:, 2 * m + h, :], start=m == 0,
                                        stop=True)
                    s.done(ins, f"c_O{m}")
                    if m < CH - 1:
                        yield f"c_S{m}"
                        s.need(dve, i, f"c_SU{m}", f"c_O{m}", "b_gend")
                        for h in range(2):
                            rows = slice(h * DK, (h + 1) * DK)
                            if m == 0:
                                ins = dve.tensor_copy(state[rows, h, :], ck[rows, 2 * DV:3 * DV])
                            else:
                                ins = dve.scalar_tensor_tensor(state[rows, h, :], state[rows, h, :],
                                                               gend[p][rows, m:m + 1], ck[rows, 2 * DV:3 * DV],
                                                               ALU.mult, ALU.add)
                        s.done(ins, f"c_S{m}")

            def emit(m):
                yield f"c_sq{m}"
                s.need(act, i, f"c_O{m}")
                if m:
                    s.need(act, i, f"c_ss{m - 1}")
                else:
                    s.need(act, i - 1, f"c_ss{CH - 1}")
                s.done(act.activation(sqo[:], co[:, 0:2 * P].rearrange("p (h t) -> p h t", h=2), ACT.Square),
                       f"c_sq{m}")
                yield f"c_y{m}"
                s.need(dve, i, f"c_sq{m}", "b_sg0", "b_sg1")
                if m:
                    s.need(dve, i, f"c_out{m - 1}")
                else:
                    s.need(dve, i - 1, f"c_out{CH - 1}")
                s.done(dve.scalar_tensor_tensor(yy[:], co[:, 0:2 * P].rearrange("p (h t) -> p h t", h=2),
                                                normw[:, 0:1], sg[p][:, :, m * P:(m + 1) * P], ALU.mult, ALU.mult),
                       f"c_y{m}")
                yield f"c_ss{m}"
                s.need(pe, i, f"c_sq{m}")
                free(pe, CK_USERS, f"c_m{m}", i)
                for h in range(2):
                    ins = pe.matmul(ck[:, 3 * DV + h:3 * DV + h + 1], sqo[:, h, :], c["ones_col"][:], start=True,
                                    stop=True)
                s.done(ins, f"c_ss{m}")
                yield f"c_m{m}"
                s.need(dve, i, f"c_ss{m}", "b_s2sq", "b_s2")
                if m:
                    s.need(dve, i, f"c_r{m - 1}")
                else:
                    s.need(dve, i - 1, f"c_r{CH - 1}")
                s.done(dve.tensor_tensor(msq[:], ck[:, 3 * DV:3 * DV + 2], s2sq[p][:, 2 * m:2 * m + 2], ALU.mult),
                       f"c_m{m}")
                yield f"c_me{m}"
                s.need(dve, i, f"c_m{m}")
                s.done(dve.tensor_scalar(msq[:], msq[:], LN_EPS, None, ALU.add), f"c_me{m}")
                yield f"c_p{m}"
                s.need(pool, i, f"c_me{m}")
                if m:
                    s.need(pool, i, f"c_acc{m - 1}")
                else:
                    s.need(pool, i - 1, f"c_acc{CH - 1}")
                s.done(pool.tensor_tensor(rms[:], msq[:], c["minus_half"][:, 0:2], ALU.pow), f"c_p{m}")
                s.need(pool, i, f"c_p{m}")
                s.done(pool.tensor_tensor(rms[:], rms[:], s2[p][:, 2 * m:2 * m + 2], ALU.mult), f"c_r{m}")
                yield f"c_out{m}"
                s.need(pe, i, f"c_y{m}")
                if m == 0:
                    s.need_dma(pe, i // NB, "wo_in")
                free(pe, CZ_USERS, f"c_acc{m}", i)
                for h in range(2):
                    ins = pe.matmul(cz[:, h * D:(h + 1) * D], yy[:, h, :], wo[:, h, :], start=True, stop=True)
                s.done(ins, f"c_out{m}")
                yield f"c_acch{m}"
                s.need(dve, i, f"c_out{m}", f"c_r{m}")
                a = acc[:, bass.ds((i % NB) * CH + m, 1), :].rearrange("p a d -> p (a d)")
                s.done(dve.scalar_tensor_tensor(a, cz[:, 0:D], rms[:, 0:1], a, ALU.mult, ALU.add), f"c_acch{m}")
                yield f"c_acc{m}"
                s.need(dve, i, f"c_acch{m}")
                s.done(dve.scalar_tensor_tensor(a, cz[:, D:2 * D], rms[:, 1:2], a, ALU.mult, ALU.add), f"c_acc{m}")

            return [recur()] + [emit(m) for m in range(CH)]

        def body(t, par):
            threads = []
            if active(t, NIT):
                threads += stage_a(t, par) + stage_b(t, par, early=True)
            if active(t - 1, NIT):
                threads += stage_b(t - 1, 1 - par, early=False)
            if active(t - 2, NIT):
                threads += stage_c(t - 2, par)
            issue(SLOT_ORDER, threads)

        for p in range(2):
            ins = pool.memset(pad[p][:, 0:PAD], 0.0)
        ins.then_inc(s.sem("pad_zero"), 1)
        dve.wait_ge(s.sem("pad_zero"), 1)
        pool.memset(bm[:], 0.0).then_inc(s.sem("bm_zero"), 1)
        pool.wait_ge(s.sem("bm_zero"), 1)
        dve.memset(state[:], 0.0).then_inc(s.sem("state_zero"), 1)
        pe.wait_ge(s.sem("state_zero"), 1)
        dve.wait_ge(s.sem("normw_in"), 16)
        dve.tensor_scalar(normw[:], normw[:], 0.5, None, ALU.mult).then_inc(s.sem("normw_half"), 1)
        dve.wait_ge(s.sem("normw_half"), 1)
        load_pair(0)
        with sp.Fori(1, NP) as hp:
            load_pair(hp)
        in_slots(nc, NIT, 2, 4, COMPUTE, body)
        ctx.finish()


def build(nc, a, out):
    with ExitStack() as ctx:
        sb = lambda name, shape, dt=F32: ctx.enter_context(nc.sbuf_tensor(name, shape, dt))
        xT_dram = nc.dram_tensor("xT_scratch", [NB + 1, P, KT, T], F32).ap()
        g_dram = nc.dram_tensor("g_scratch", [(NIT + 1) * NU, P], F32).ap()
        acc = sb("acc", [P, NTILE, D])
        c, s_const, n_const = make_constants(nc, ctx, sb)
        for eng in (nc.tensor, nc.vector, nc.scalar):
            eng.wait_ge(s_const, n_const)
        with ExitStack() as gates:
            gate_tok = [gates.enter_context(nc.sbuf_tensor(f"gate_tok{k}", [P, NIT * NU + NU], F32)) for k in range(2)]
            phase_norm(nc, c, a["x"], a["w_ab"], xT_dram, [g[:, 0:NIT * NU] for g in gate_tok])
            s_zero = ctx.enter_context(nc.semaphore("acc_zero"))
            nc.gpsimd.memset(acc[:], 0.0).then_inc(s_zero, 1)
            phase_gates(nc, c, a["A_log"], a["dt_bias"], [g[:, 0:NIT * NU] for g in gate_tok], g_dram)
            nc.vector.wait_ge(s_zero, 1)
            phase_delta(nc, c, a["w_qkv"], a["w_gate"], a["w_out"], a["norm_w"], xT_dram, g_dram, gate_tok, acc)
        phase_experts(nc, c, a, acc, out)


def phase_experts(nc, c, a, acc, out):
    with Phase(nc) as ctx:
        sb = lambda name, shape, dt=F32: ctx.enter_context(nc.sbuf_tensor(name, shape, dt))
        two = lambda name, shape, dt=F32: [sb(f"{name}{p}", shape, dt) for p in range(2)]
        bank = lambda name: ctx.enter_context(nc.psum_tensor(name, [P, 512], F32))
        pe, act, dve, pool, sp = nc.tensor, nc.scalar, nc.vector, nc.gpsimd, nc.sync
        s = Steps(nc, ctx)
        NR = E + E * PP
        wv = sb("e_wv", [P, KT, D])
        wr = sb("e_wr", [P, KT, NR])
        w1 = sb("e_w1", [P, KT, E * INNER])
        w2 = sb("e_w2", [P, KT, D])
        b2v = sb("e_b2v", [E + 1, D])
        bvc = sb("e_bvc", [P, KT])
        b1c = sb("e_b1c", [P, KT])
        b1h = sb("e_b1h", [P, KT])
        spread = sb("e_spread", [E, E * INNER])
        rows = sb("e_rows", [P, 5, E])
        alpha = sb("e_alpha", [P, 1])
        expert = sb("e_expert", [P, CH, E])
        x_in = two("e_x", [P, CH, D])
        xT = two("e_xT", [P, KT, T])
        xf = sb("e_xf", [P, CH, D])
        stats, mv, rstd = sb("e_stats", [P, CH, 6]), sb("e_mv", [P, CH, 2]), sb("e_rstd", [P, CH])
        o_stats, o_mv, o_rstd = sb("e_ostats", [P, CH, 6]), sb("e_omv", [P, CH, 2]), sb("e_orstd", [P, CH])
        vT = sb("e_vT", [P, KT, T])
        rc = two("e_rc", [P, 2, CH, E])
        pv2 = sb("e_pv2", [P, CH, E, PP])
        c2 = sb("e_c2", [P, CH, E])
        mean, cen2 = sb("e_mean", [P, 2 * CH]), sb("e_cen2", [P, 2 * CH, E])
        var = sb("e_var", [P, 2 * CH])
        score = sb("e_score", [P, CH, E])
        top, idx = sb("e_top", [P, CH, 8]), sb("e_idx", [P, CH, 8], U32)
        idxf = sb("e_idxf", [P, CH, 8])
        gap, e2 = sb("e_gap", [P, CH]), sb("e_e2", [P, CH])
        share = sb("e_share", [P, CH, 2])
        hot = sb("e_hot", [P, 2, CH, E])
        we = sb("e_we", [P, CH, E + 1])
        weT = sb("e_weT", [E + 1, T])
        hz, hth, hw = sb("e_hz", [P, KT, T]), sb("e_hth", [P, KT, T]), two("e_hw", [P, KT, T])
        yo = two("e_yo", [P, CH, D])
        turn = [bank(f"e_turn{k}") for k in range(KT)]
        vb = [bank(f"e_vb{k}") for k in range(KT)]
        rb, wb = bank("e_rb"), bank("e_wb")
        ob = [bank(f"e_ob{k}") for k in range(2)]

        s_w = ctx.semaphore("e_w_in")
        loads = [(wv[:], a["Wv"]), (wr[:], a["Wr"]), (w1[:], a["W1"]), (w2[:], a["W2"]), (b2v[:], a["b2v"]),
                 (bvc[:], a["bv"]), (b1c[:], a["b1"]), (rows[:], a["router_rows"].partition_broadcast(P)),
                 (alpha[:], a["alpha"].partition_broadcast(P))]
        for dst, src in loads:
            sp.dma_start(dst, src).then_inc(s_w, 16)
        s_k = ctx.semaphore("e_const")
        nk = [0]

        def build_step(ins):
            ins.then_inc(s_k, 1)
            nk[0] += 1
            pool.wait_ge(s_k, nk[0])

        build_step(pool.memset(spread[:], 0.5))
        build_step(pool.affine_select(out=spread[:], in_=spread[:], pattern=[[1, E * INNER]], compare_op=ALU.is_ge,
                                      fill=0.0, base=0, channel_multiplier=-INNER))
        build_step(pool.affine_select(out=spread[:], in_=spread[:], pattern=[[-1, E * INNER]], compare_op=ALU.is_ge,
                                      fill=0.0, base=INNER - 1, channel_multiplier=INNER))
        build_step(pool.iota(expert[:].bitcast(mybir.dt.int32), pattern=[[0, CH], [1, E]], base=0,
                             channel_multiplier=0))
        build_step(pool.tensor_copy(expert[:], expert[:].bitcast(mybir.dt.int32)))
        build_step(pool.memset(we[:, :, E:E + 1], 1.0))
        for eng in (pe, act, dve, pool):
            eng.wait_ge(s_w, 16 * len(loads))
            eng.wait_ge(s_k, nk[0])
        s_0 = ctx.semaphore("e_alpha_done")
        act.activation(alpha[:], alpha[:], ACT.Tanh, scale=0.5).then_inc(s_0, 1)
        act.mul(b1h[:], b1c[:], 0.5).then_inc(s_0, 1)
        act.wait_ge(s_0, 2)
        dve.wait_ge(s_0, 2)
        dve.tensor_scalar(alpha[:], alpha[:], 1.0, 0.5, ALU.add, ALU.mult).then_inc(s_0, 1)
        dve.wait_ge(s_0, 3)
        dve.tensor_scalar(rows[:, 2, :], rows[:, 2, :], alpha[:, 0:1], None, ALU.mult).then_inc(s_0, 1)
        dve.tensor_scalar(rows[:, 4, :], rows[:, 4, :], alpha[:, 0:1], None, ALU.mult).then_inc(s_0, 1)
        dve.wait_ge(s_0, 5)

        def chained(eng, i, name, ins):
            s.done(ins, name)
            s.need(eng, i, name)

        def load(i, p):
            yield "l_x"
            s.need(sp, i - 2, "x_x1")
            s.loaded(sp.dma_start(x_in[p][:], a["x"][bass.ds(i, 1)].rearrange("a p c d -> p (a c) d")), f"x_in{p}")

        def norm_x(i, p):
            tiles = acc[:, bass.ds(i * CH, CH), :]
            for half in range(2):
                yield f"x_bn{half}"
                for k in range(CH):
                    ins = dve.bn_stats(stats[:, k, :], tiles[:, k, :])
                s.done(ins, f"x_bn{half}")
                yield f"x_ve{half}"
                s.need(dve, i, f"x_bn{half}")
                settle(dve, c["settle_dve"])
                for k in range(CH):
                    ins = dve.bn_aggr(mv[:, k, :], stats[:, k, :])
                chained(dve, i, f"x_mv{half}", ins)
                s.done(dve.tensor_scalar(rstd[:], mv[:, :, 1], LN_EPS, None, ALU.add), f"x_ve{half}")
                yield f"x_rs{half}"
                s.need(pool, i, f"x_ve{half}")
                s.done(pool.tensor_tensor(rstd[:], rstd[:], c["minus_half"][:, 0:CH], ALU.pow), f"x_rs{half}")
                yield "x_xf" if half else "x_y1"
                s.need(dve, i, f"x_rs{half}")
                if half:
                    s.need(dve, i - 1, "x_turn")
                for k in range(CH):
                    ins = dve.tensor_scalar(xf[:, k, :] if half else tiles[:, k, :], tiles[:, k, :], mv[:, k, 0:1],
                                            rstd[:, k:k + 1], ALU.subtract, ALU.mult)
                s.done(ins, "x_xf" if half else "x_y1")
                if half == 0:
                    yield "x_x1"
                    s.need(dve, i, "x_y1")
                    s.need_dma_of(dve, i, "x_in", p)
                    chained(dve, i, "x_x1", dve.tensor_tensor(tiles, tiles, x_in[p][:], ALU.add))
            yield "x_turn"
            s.need(pe, i, "x_xf")
            s.need(pe, i - 1, "x_xT")
            for k in range(KT):
                for m in range(CH):
                    ins = pe.transpose(turn[k][:, m * P:(m + 1) * P], xf[:, m, k * P:(k + 1) * P], c["ident"][:])
            s.done(ins, "x_turn")
            yield "x_xT"
            s.need(act, i, "x_turn")
            s.need(act, i - 2, "w_out1")
            for k in range(KT):
                ins = act.copy(xT[p][:, k, :], turn[k][:])
            s.done(ins, "x_xT")

        def values(i, p):
            r = rb[:].rearrange("p (c n) -> p c n", c=CH)

            def products():
                yield "v_mm"
                s.need(pe, i, "x_xT")
                s.need(pe, i - 1, "h_th1", "h_z1")
                for m in range(KT):
                    for k in range(KT):
                        ins = pe.matmul(vb[m][:], wv[:, k, m * P:(m + 1) * P], xT[p][:, k, :], start=k == 0,
                                        stop=k == KT - 1)
                s.done(ins, "v_mm")
                yield "v_T"
                s.need(act, i, "v_mm")
                s.need(act, i - 1, "h_mm1", "q_mm")
                for m in range(KT):
                    ins = act.activation(vT[:, m, :], vb[m][:], ACT.Identity, bias=bvc[:, m:m + 1])
                s.done(ins, "v_T")
                yield "q_mm"
                s.need(pe, i, "v_T")
                s.need(pe, i - 1, "q_sq", "q_s")
                for m in range(CH):
                    for k in range(KT):
                        ins = pe.matmul(rb[:, m * P:m * P + NR], vT[:, k, m * P:(m + 1) * P], wr[:, k, :],
                                        start=k == 0, stop=k == KT - 1)
                s.done(ins, "q_mm")
                yield "h_mm"
                for m in range(KT):
                    for k in range(KT):
                        ins = pe.matmul(vb[m][:], w1[:, k, m * P:(m + 1) * P], vT[:, k, :], start=k == 0,
                                        stop=k == KT - 1)
                    s.done(ins, f"h_mm{m}")
                for m in range(KT):
                    yield f"h_th{m}"
                    s.need(act, i, f"h_mm{m}")
                    s.need(act, i - 1, f"h_s{m}")
                    s.done(act.activation(hth[:, m, :], vb[m][:], ACT.Tanh, bias=b1h[:, m:m + 1], scale=0.5),
                           f"h_th{m}")
                    s.done(act.activation(hz[:, m, :], vb[m][:], ACT.Identity, bias=b1c[:, m:m + 1]), f"h_z{m}")
                for m in range(KT):
                    yield f"h_s{m}"
                    s.need(dve, i, f"h_z{m}", f"h_th{m}")
                    s.need(dve, i - 2, "w_out1")
                    s.done(dve.scalar_tensor_tensor(hw[p][:, m, :], hth[:, m, :], 1.0, hz[:, m, :], ALU.add,
                                                    ALU.mult), f"h_s{m}")

            def norms():
                yield "q_sq"
                s.need(act, i, "q_mm")
                s.need(act, i - 1, "q_c2")
                s.done(act.activation(pv2[:].rearrange("p c e n -> p c (e n)"), r[:, :, E:NR], ACT.Square), "q_sq")
                yield "q_s"
                s.need(dve, i, "q_sq")
                s.need(dve, i - 2, "r_score")
                s.done(dve.tensor_tensor(rc[p][:, 0], r[:, :, 0:E], rows[:, 0, :].unsqueeze(1).broadcast_to([P, CH, E]),
                                         ALU.add), "q_s")
                yield "q_c2"
                s.need(dve, i - 1, "q_cn")
                s.done(dve.tensor_reduce(c2[:], pv2[:], AX.X, ALU.add), "q_c2")
                s.need(dve, i, "q_c2")
                s.done(dve.tensor_scalar(c2[:], c2[:], 1.0 / PP, None, ALU.mult), "q_c3")
                yield "q_cn"
                s.need(pool, i, "q_c3")
                s.need(pool, i - 2, "r_score")
                s.done(pool.tensor_tensor(rc[p][:, 1], c2[:],
                                          c["half"][:].unsqueeze(1)[:, :, 0:E].broadcast_to([P, CH, E]), ALU.pow),
                       "q_cn")

            return [products(), norms()]

        def route(i, p):
            flat = rc[p][:].rearrange("p n c e -> p (n c) e")
            along = lambda t: t[:].unsqueeze(2).broadcast_to([P, 2 * CH, E])
            per_kind = lambda k: rows[:, k:k + 2, :].unsqueeze(2).broadcast_to([P, 2, CH, E])
            yield "r_sum"
            s.need(dve, i, "q_cn", "q_s")
            s.done(dve.tensor_reduce(mean[:], flat, AX.X, ALU.add), "r_sum")
            yield "r_mean"
            s.need(dve, i, "r_sum")
            s.done(dve.tensor_scalar(mean[:], mean[:], 1.0 / E, None, ALU.mult), "r_mean")
            yield "r_cen"
            s.need(dve, i, "r_mean")
            s.done(dve.tensor_tensor(flat, flat, along(mean), ALU.subtract), "r_cen")
            yield "r_cen2"
            s.need(dve, i, "r_cen")
            s.done(dve.tensor_tensor(cen2[:], flat, flat, ALU.mult), "r_cen2")
            yield "r_var"
            s.need(dve, i, "r_cen2")
            s.done(dve.tensor_reduce(var[:], cen2[:], AX.X, ALU.add), "r_var")
            yield "r_vare"
            s.need(dve, i, "r_var")
            s.done(dve.tensor_scalar(var[:], var[:], 1.0 / E, LN_EPS, ALU.mult, ALU.add), "r_vare")
            yield "r_rstd"
            s.need(pool, i, "r_vare")
            s.done(pool.tensor_tensor(var[:], var[:], c["minus_half"][:, 0:2 * CH], ALU.pow), "r_rstd")
            yield "r_n0"
            s.need(dve, i, "r_rstd")
            s.done(dve.tensor_tensor(flat, flat, along(var), ALU.mult), "r_n0")
            yield "r_n1"
            s.need(dve, i, "r_n0")
            s.done(dve.tensor_tensor(rc[p][:], rc[p][:], per_kind(1), ALU.mult), "r_n1")
            yield "r_n2"
            s.need(dve, i, "r_n1")
            s.done(dve.tensor_tensor(rc[p][:], rc[p][:], per_kind(3), ALU.add), "r_n2")
            yield "r_score"
            s.need(dve, i, "r_n2")
            s.done(dve.tensor_tensor(score[:], rc[p][:, 0], rc[p][:, 1], ALU.add), "r_score")
            yield "t_max"
            s.need(dve, i, "r_score")
            settle(dve, c["settle_dve"])
            for m in range(CH):
                ins = dve.max(top[:, m, :], score[:, m, :])
            s.done(ins, "t_max")
            yield "t_idx"
            s.need(dve, i, "t_max")
            settle(dve, c["settle_dve"])
            for m in range(CH):
                ins = dve.max_index(idx[:, m, :], top[:, m, :], score[:, m, :])
            s.done(ins, "t_idx")
            yield "t_gap"
            s.need(dve, i, "t_idx")
            s.need(dve, i - 1, "t_e2")
            s.done(dve.tensor_tensor(gap[:], top[:, :, 1], top[:, :, 0], ALU.subtract), "t_gap")
            s.done(dve.tensor_copy(idxf[:], idx[:]), "t_idxf")
            yield "t_e2"
            s.need(act, i, "t_gap")
            s.need(act, i - 1, "t_sh1")
            s.done(act.activation(e2[:], gap[:], ACT.Exp), "t_e2")
            yield "t_hot"
            s.need(dve, i, "t_idxf")
            for k in range(2):
                ins = dve.tensor_tensor(hot[:, k], expert[:], idxf[:, :, k:k + 1].broadcast_to([P, CH, E]),
                                        ALU.is_equal)
            s.done(ins, "t_hot")
            yield "t_den"
            s.need(dve, i, "t_e2")
            s.done(dve.tensor_scalar(share[:, :, 0], e2[:], 1.0, None, ALU.add), "t_den")
            yield "t_sh0"
            s.need(dve, i, "t_den")
            s.done(dve.reciprocal(share[:, :, 0], share[:, :, 0]), "t_sh0")
            yield "t_sh1"
            s.need(dve, i, "t_sh0")
            s.done(dve.tensor_tensor(share[:, :, 1], share[:, :, 0], e2[:], ALU.mult), "t_sh1")
            yield "t_w"
            s.need(dve, i, "t_hot", "t_sh1")
            for k in range(2):
                ins = dve.tensor_tensor(hot[:, k], hot[:, k], share[:, :, k:k + 1].broadcast_to([P, CH, E]), ALU.mult)
            s.done(ins, "t_w")
            yield "t_we"
            s.need(dve, i, "t_w")
            s.need(dve, i - 1, "w_turn")
            s.done(dve.tensor_tensor(we[:, :, 0:E], hot[:, 0], hot[:, 1], ALU.add), "t_we")
            yield "w_turn"
            s.need(pe, i, "t_we")
            s.need(pe, i - 1, "w_hw1")
            for m in range(CH):
                ins = pe.transpose(wb[0:E + 1, m * P:(m + 1) * P], we[:, m, :], c["ident"][:])
            s.done(ins, "w_turn")
            yield "w_T"
            s.need(act, i, "w_turn")
            s.need(act, i - 1, "w_out1")
            s.done(act.copy(weT[:], wb[0:E + 1, :]), "w_T")
            for m in range(KT):
                yield f"w_mm{m}"
                s.need(pe, i, "w_T" if m == 0 else "w_hw0")
                s.done(pe.matmul(wb[:], spread[:, m * P:(m + 1) * P], weT[0:E, :], start=True, stop=True), f"w_mm{m}")
                yield f"w_hw{m}"
                s.need(dve, i, f"w_mm{m}", f"h_s{m}")
                s.done(dve.tensor_tensor(hw[p][:, m, :], hw[p][:, m, :], wb[:], ALU.mult), f"w_hw{m}")
            for half in range(2):
                yield f"w_out{half}"
                s.need(pe, i, "w_hw1", "w_T")
                s.need(pe, i - 1, f"o_n{half}")
                for m in (2 * half, 2 * half + 1):
                    o = ob[half][:, (m % 2) * D:(m % 2 + 1) * D]
                    tok = slice(m * P, (m + 1) * P)
                    for k in range(KT):
                        pe.matmul(o, xT[p][:, k, tok], wv[:, k, :], start=k == 0, stop=False)
                    for k in range(KT):
                        pe.matmul(o, hw[p][:, k, tok], w2[:, k, :], start=False, stop=False)
                    ins = pe.matmul(o, weT[:, tok], b2v[:], start=False, stop=True)
                s.done(ins, f"w_out{half}")

        def finish(i, p):
            for half in range(2):
                yield f"o_bn{half}"
                s.need(dve, i, f"w_out{half}")
                for m in (2 * half, 2 * half + 1):
                    ins = dve.bn_stats(o_stats[:, m, :], ob[half][:, (m % 2) * D:(m % 2 + 1) * D])
                s.done(ins, f"o_bn{half}")
            yield "o_ve"
            s.need(dve, i, "o_bn1")
            settle(dve, c["settle_dve"])
            for m in range(CH):
                ins = dve.bn_aggr(o_mv[:, m, :], o_stats[:, m, :])
            chained(dve, i, "o_mv", ins)
            s.done(dve.tensor_scalar(o_rstd[:], o_mv[:, :, 1], LN_EPS, None, ALU.add), "o_ve")
            yield "o_rs"
            s.need(pool, i, "o_ve")
            s.done(pool.tensor_tensor(o_rstd[:], o_rstd[:], c["minus_half"][:, 0:CH], ALU.pow), "o_rs")
            for half in range(2):
                yield f"o_n{half}"
                if half == 0:
                    s.need(dve, i, "o_rs")
                    s.need_dma_of(dve, i - 2, "y_out", p)
                for m in (2 * half, 2 * half + 1):
                    ins = dve.tensor_scalar(yo[p][:, m, :], ob[half][:, (m % 2) * D:(m % 2 + 1) * D],
                                            o_mv[:, m, 0:1], o_rstd[:, m:m + 1], ALU.subtract, ALU.mult)
                s.done(ins, f"o_n{half}")
            yield "o_sum"
            s.need(dve, i, "o_n1")
            s.done(dve.tensor_tensor(yo[p][:], yo[p][:], acc[:, bass.ds(i * CH, CH), :], ALU.add), "o_sum")
            yield "o_store"
            s.need(sp, i, "o_sum")
            s.loaded(sp.dma_start(out[bass.ds(i, 1)].rearrange("a p c d -> p (a c) d"), yo[p][:]), f"y_out{p}")

        def body(t, par):
            threads = []
            if active(t - 1, NB):
                threads.append(load(t - 1, 1 - par))
            if active(t - 2, NB):
                threads.append(norm_x(t - 2, par))
            if active(t - 3, NB):
                threads += values(t - 3, 1 - par)
            if active(t - 4, NB):
                threads.append(route(t - 4, par))
            if active(t - 5, NB):
                threads.append(finish(t - 5, 1 - par))
            issue(EXPERT_ORDER, threads)

        for name in (["x_bn", "x_mv", "x_ve", "x_rs"] + ["o_n", "o_bn", "h_mm", "h_s", "h_z", "h_th", "w_mm", "w_hw",
                                                         "w_out"]):
            s.series(name, [f"{name}{k}" for k in range(2)])
        s.series("r_dve", ["r_sum", "r_mean", "r_cen", "r_cen2", "r_var", "r_vare", "r_n0", "r_n1", "r_n2", "r_score"])
        s.series("t_dve", ["t_max", "t_idx", "t_gap", "t_idxf", "t_hot", "t_den", "t_sh0", "t_sh1", "t_w", "t_we"])
        in_slots(nc, NB, 5, 7, EVERY, body)
        for p in range(2):
            sp.wait_ge(s.sem(f"y_out{p}"), 16 * NB // 2)


def kernel(**inputs):
    import numpy as np
    import concourse.bacc as bacc
    from concourse.bass_utils import run_bass_kernel_spmd

    v = {k: np.asarray(x) for k, x in inputs.items()}
    at = lambda name: v["L0_attn_" + name]
    ff = lambda name: v["L0_ffn_" + name]
    rows = lambda w: w.reshape(KT, P, -1).transpose(1, 0, 2)
    by_pair = lambda w, n: rows(w).reshape(P, KT, NP, n).transpose(2, 0, 1, 3)
    tap_of = lambda w, n: w.reshape(NP, n, P, TAPS).transpose(0, 2, 1, 3)
    wqkv = np.concatenate([by_pair(at("w_q"), P), by_pair(at("w_k"), P), by_pair(at("w_v"), 2 * P)], axis=3)
    taps = np.concatenate([tap_of(at("conv_q"), 1), tap_of(at("conv_k"), 1), tap_of(at("conv_v"), 2)], axis=2)
    arrays = {
        "x": at("x").reshape(NB, CH, P, D).transpose(0, 2, 1, 3),
        "w_ab": rows(np.concatenate([at("w_a"), at("w_b")], axis=1)),
        "A_log": at("A_log"),
        "dt_bias": at("dt_bias"),
        "w_qkv": np.concatenate([wqkv.reshape(NP, P, -1), taps.reshape(NP, P, -1)], axis=2),
        "w_gate": by_pair(at("w_g"), 2 * P),
        "w_out": at("w_out").reshape(NP, 2, P, D).transpose(0, 2, 1, 3),
        "norm_w": at("norm_w").reshape(P, 1),
        "Wv": rows(ff("Wv").T),
        "Wr": rows(np.concatenate([ff("Wg").T, ff("Wp").reshape(E * PP, D).T], axis=1)),
        "W1": rows(ff("W1").reshape(E * INNER, D).T),
        "W2": rows(ff("W2").transpose(0, 2, 1).reshape(E * INNER, D)),
        "b2v": np.concatenate([ff("b2"), ff("bv")[None]], axis=0),
        "bv": ff("bv").reshape(KT, P).T,
        "b1": ff("b1").reshape(KT, P).T,
        "router_rows": np.stack([ff("bg"), ff("g_r"), ff("g_c"), ff("b_r"), ff("b_c")]),
        "alpha": ff("alpha").reshape(1),
    }
    nc = bacc.Bacc("TRN2", target_bir_lowering=False, num_devices=1)
    arrays = {k: np.ascontiguousarray(x) for k, x in arrays.items()}
    aps = {k: nc.dram_tensor("in_" + k, x.shape, mybir.dt.from_np(x.dtype), kind="ExternalInput").ap()
           for k, x in arrays.items()}
    out = nc.dram_tensor("out_y", (NB, P, CH, D), F32, kind="ExternalOutput").ap()
    build(nc, aps, out)
    r = run_bass_kernel_spmd(nc, [{"in_" + k: x for k, x in arrays.items()}], core_ids=[0])
    y = r.results[0]["out_y"]
    return y.transpose(0, 2, 1, 3).reshape(NB, T, D)
```
